# Optimizing a Trainium2 kernel written in Bass

```python
import numpy as np
import jax
import jax.numpy as jnp

def _softmax(x, axis=-1):
    return jax.nn.softmax(x, axis=axis)

def _gelu(x):
    return jax.nn.gelu(x, approximate=True)

def _silu(x):
    return jax.nn.silu(x)

def _sigmoid(x):
    return jax.nn.sigmoid(x)

def _layernorm(x, axis=-1, eps=1e-05):
    m = jnp.mean(x, axis=axis, keepdims=True)
    v = jnp.var(x, axis=axis, keepdims=True)
    return (x - m) / jnp.sqrt(v + eps)

def _scatter_add(tgt, idx, src, axis=0):
    return tgt.at[idx].add(src)

def _segment_sum(src, seg, n):
    return jax.ops.segment_sum(src, seg, n)
kernel_name = 'mk_gnn_ffn_d1_gnn_r8_1b421a'

def setup_inputs(seed: int=0):
    np.random.seed(seed)
    _w = jnp.asarray

    def _rec_inputs():
        import jax
        import jax.numpy as jnp
        _gk = jax.random.key(seed)
        x = -0.0002117 + 1 * jax.random.normal(jax.random.fold_in(_gk, 1), (6250, 256), jnp.float32)
        src = jax.random.randint(jax.random.fold_in(_gk, 2), (100000,), 0, 6250, jnp.int32)
        dst = jnp.minimum((6250 * jax.random.uniform(jax.random.fold_in(_gk, 3), (100000,)) ** 2.0).astype(jnp.int32), 49999)
        _o = jnp.argsort(dst, stable=True)
        src = src[_o]
        dst = dst[_o]
        edge_weight = jax.random.uniform(jax.random.fold_in(_gk, 12), (100000,), jnp.float32, 0.0, 0.999998)
        edge_weight_n2 = jax.random.uniform(jax.random.fold_in(_gk, 13), (100000,), jnp.float32, 0.0, 0.999998)
        return (x, src, dst, edge_weight, edge_weight_n2)
    x, src, dst, edge_weight, edge_weight_n2 = _rec_inputs()

    def _L0_gnn_setup():
        import jax, jax.numpy as jnp
        import numpy as np
        N_NODES = 12500
        N_EDGES = 100000
        DIM = 256
        EPS = 1e-05
        key = jax.random.key(seed)
        ks = jax.random.split(key, 12)
        H = DIM
        s = 1.0 / np.sqrt(H)
        s2 = 1.0 / np.sqrt(2 * H)
        return {'feat': jax.random.normal(ks[0], (N_NODES, DIM), dtype=jnp.float32), 'src': jax.random.randint(ks[1], (N_EDGES,), 0, N_NODES, dtype=jnp.int32), 'dst': jax.random.randint(ks[2], (N_EDGES,), 0, N_NODES, dtype=jnp.int32), 'iw': jax.random.uniform(ks[3], (N_EDGES,), dtype=jnp.float32), 'ow': jax.random.uniform(ks[4], (N_EDGES,), dtype=jnp.float32), 'gamma': jnp.ones((DIM,), jnp.float32), 'beta': jnp.zeros((DIM,), jnp.float32), 'W_in': jax.random.uniform(ks[5], (H, H), jnp.float32, -s, s), 'b_in': jax.random.uniform(ks[6], (H,), jnp.float32, -s, s), 'W_out': jax.random.uniform(ks[7], (H, H), jnp.float32, -s, s), 'b_out': jax.random.uniform(ks[8], (H,), jnp.float32, -s, s), 'W_x2i': jax.random.uniform(ks[9], (2 * H, 2 * H), jnp.float32, -s2, s2), 'b_x2i': jax.random.uniform(ks[10], (2 * H,), jnp.float32, -s2, s2), 'W_h2h': jax.random.uniform(ks[11], (H, 2 * H), jnp.float32, -s, s)}
    _L0_gnn_all = _L0_gnn_setup()
    _L0_gnn_in = {k: v for k, v in _L0_gnn_all.items() if k in ('gamma', 'beta', 'W_in', 'b_in', 'W_out', 'b_out', 'W_x2i', 'b_x2i', 'W_h2h')}
    del _L0_gnn_all

    def _L0_ffn_setup():
        import jax, jax.numpy as jnp
        import numpy as np
        E, D, H, TOP_K = (6, 256, 256, 2)
        ROUTER_H = D // 2
        key = jax.random.key(seed)
        ks = jax.random.split(key, 12)
        s = 1.0 / np.sqrt(D)
        sh = 1.0 / np.sqrt(H)
        sr = 1.0 / np.sqrt(ROUTER_H)
        return {'features': jax.random.normal(ks[0], (8, 512, D), dtype=jnp.float32), 'router_w1': jax.random.uniform(ks[1], (D, ROUTER_H), jnp.float32, -s, s), 'router_b1': jnp.zeros((ROUTER_H,), jnp.float32), 'router_w2': jax.random.uniform(ks[2], (ROUTER_H, E), jnp.float32, -sr, sr), 'router_b2': jnp.zeros((E,), jnp.float32), 'expert_w1': jax.random.uniform(ks[3], (E, D, H), jnp.float32, -s, s), 'expert_b1': jnp.zeros((E, H), jnp.float32), 'expert_w2': jax.random.uniform(ks[4], (E, H, H), jnp.float32, -sh, sh), 'expert_b2': jnp.zeros((E, H), jnp.float32), 'expert_w3': jax.random.uniform(ks[5], (E, H, D), jnp.float32, -sh, sh), 'expert_b3': jnp.zeros((E, D), jnp.float32)}
    _L0_ffn_all = _L0_ffn_setup()
    _L0_ffn_in = {k: v for k, v in _L0_ffn_all.items() if k in ('router_w1', 'router_b1', 'router_w2', 'router_b2', 'expert_w1', 'expert_b1', 'expert_w2', 'expert_b2', 'expert_w3', 'expert_b3')}
    del _L0_ffn_all
    return {'x': x, 'src': src, 'dst': dst, 'edge_weight': edge_weight, 'edge_weight_n2': edge_weight_n2, 'L0_gnn_gamma': _L0_gnn_in['gamma'], 'L0_gnn_beta': _L0_gnn_in['beta'], 'L0_gnn_W_in': _L0_gnn_in['W_in'], 'L0_gnn_b_in': _L0_gnn_in['b_in'], 'L0_gnn_W_out': _L0_gnn_in['W_out'], 'L0_gnn_b_out': _L0_gnn_in['b_out'], 'L0_gnn_W_x2i': _L0_gnn_in['W_x2i'], 'L0_gnn_b_x2i': _L0_gnn_in['b_x2i'], 'L0_gnn_W_h2h': _L0_gnn_in['W_h2h'], 'L0_ffn_router_w1': _L0_ffn_in['router_w1'], 'L0_ffn_router_b1': _L0_ffn_in['router_b1'], 'L0_ffn_router_w2': _L0_ffn_in['router_w2'], 'L0_ffn_router_b2': _L0_ffn_in['router_b2'], 'L0_ffn_expert_w1': _L0_ffn_in['expert_w1'], 'L0_ffn_expert_b1': _L0_ffn_in['expert_b1'], 'L0_ffn_expert_w2': _L0_ffn_in['expert_w2'], 'L0_ffn_expert_b2': _L0_ffn_in['expert_b2'], 'L0_ffn_expert_w3': _L0_ffn_in['expert_w3'], 'L0_ffn_expert_b3': _L0_ffn_in['expert_b3']}

def reference(x, src, dst, edge_weight, edge_weight_n2, L0_gnn_gamma, L0_gnn_beta, L0_gnn_W_in, L0_gnn_b_in, L0_gnn_W_out, L0_gnn_b_out, L0_gnn_W_x2i, L0_gnn_b_x2i, L0_gnn_W_h2h, L0_ffn_router_w1, L0_ffn_router_b1, L0_ffn_router_w2, L0_ffn_router_b2, L0_ffn_expert_w1, L0_ffn_expert_b1, L0_ffn_expert_w2, L0_ffn_expert_b2, L0_ffn_expert_w3, L0_ffn_expert_b3):
    import jax
    import jax.numpy as jnp

    def _L0_gnn_ref(feat, src, dst, iw, ow, gamma, beta, W_in, b_in, W_out, b_out, W_x2i, b_x2i, W_h2h):
        import jax, jax.numpy as jnp
        import numpy as np
        N_NODES = 12500
        N_EDGES = 100000
        DIM = 256
        EPS = 1e-05
        N = feat.shape[0]
        num_steps = 1
        mean = jnp.mean(feat, axis=0)
        var = jnp.var(feat, axis=0)
        h = (feat - mean) * jax.lax.rsqrt(var + EPS) * gamma + beta
        for _ in range(num_steps):
            feat_in = h @ W_in + b_in
            feat_out = h @ W_out + b_out
            a_in = jax.ops.segment_sum(feat_in[src] * iw[:, None], dst, num_segments=N)
            a_out = jax.ops.segment_sum(feat_out[dst] * ow[:, None], src, num_segments=N)
            a = jnp.concatenate((a_in, a_out), axis=1)
            xi = a @ W_x2i + b_x2i
            hh = h @ W_h2h
            i_i, i_n = jnp.split(xi, 2, axis=1)
            h_i, h_n = jnp.split(hh, 2, axis=1)
            input_gate = jax.nn.sigmoid(i_i + h_i)
            new_gate = jnp.tanh(i_n + h_n)
            h = new_gate + input_gate * (h - new_gate)
        return h

    def _L0_ffn_ref(features, router_w1, router_b1, router_w2, router_b2, expert_w1, expert_b1, expert_w2, expert_b2, expert_w3, expert_b3):
        import jax, jax.numpy as jnp
        import numpy as np
        E, D, H, TOP_K = (6, 256, 256, 2)
        ROUTER_H = D // 2
        rh = jax.nn.relu(features @ router_w1 + router_b1)
        expert_logits = jax.nn.softmax(rh @ router_w2 + router_b2, axis=-1)
        top_w, top_i = jax.lax.top_k(expert_logits, TOP_K)
        routing_weights = jax.nn.softmax(top_w, axis=-1)
        h1 = jax.nn.relu(jnp.einsum('bsd,edh->bseh', features, expert_w1) + expert_b1)
        h2 = jax.nn.relu(jnp.einsum('bseh,ehf->bsef', h1, expert_w2) + expert_b2)
        expert_out = jnp.einsum('bsef,efo->bseo', h2, expert_w3) + expert_b3
        sel = jnp.take_along_axis(expert_out, top_i[:, :, :, None], axis=2)
        combined = jnp.sum(sel * routing_weights[..., None], axis=2)
        return combined
    x = x + _L0_gnn_ref(_layernorm(x, axis=-1), src, dst, edge_weight, edge_weight_n2, L0_gnn_gamma, L0_gnn_beta, L0_gnn_W_in, L0_gnn_b_in, L0_gnn_W_out, L0_gnn_b_out, L0_gnn_W_x2i, L0_gnn_b_x2i, L0_gnn_W_h2h)
    x = x + _L0_ffn_ref(_layernorm(x, axis=-1)[None], L0_ffn_router_w1, L0_ffn_router_b1, L0_ffn_router_w2, L0_ffn_router_b2, L0_ffn_expert_w1, L0_ffn_expert_b1, L0_ffn_expert_w2, L0_ffn_expert_b2, L0_ffn_expert_w3, L0_ffn_expert_b3)[0]
    return x

_drawn_inputs = setup_inputs


def setup_inputs(seed=0):
    import zlib

    import numpy as np

    out = dict(_drawn_inputs(seed))
    spreads = {'L0_gnn_gamma': (1.0, 0.2),
     'L0_gnn_beta': (0.0, 0.1),
     'L0_ffn_router_b1': (0.0, 0.318),
     'L0_ffn_router_b2': (0.0, 0.1),
     'L0_ffn_expert_b1': (0.0, 0.8),
     'L0_ffn_expert_b2': (0.0, 0.445),
     'L0_ffn_expert_b3': (0.0, 0.1)}
    factors = {'L0_gnn_b_x2i': 6.032}
    for name, (base, spread) in spreads.items():
        noise = np.random.default_rng([zlib.crc32(name.encode()), seed]).standard_normal(out[name].shape)
        drawn = base * np.exp(spread * noise) if base else spread * noise
        out[name] = jnp.asarray(drawn.astype(out[name].dtype))
    for name, factor in factors.items():
        out[name] = (out[name] * factor).astype(out[name].dtype)
    return out
```

```python
from contextlib import ExitStack

import concourse.bass as bass
from concourse import mybir

P = 128
N = 6250
E = 100000
D = 256
H = D // P
EPS = 1e-5
NT = -(-N // P)
NP = NT * P
TAIL = N - (NT - 1) * P
BLK = 7
NB = NT // BLK
ET = -(-E // P)
ETAIL = E - (ET - 1) * P
EC = -(-ET // P)
QUAD = 4
BODY = 2 * QUAD
TILES = -(-ET // BODY) * BODY
TURNS = TILES // BODY
ROWS = 6400
SPARE = ROWS - P
ACCW = ROWS
GN = 448
ST = 4
SP_ = GN // ST
GROUPS = -(-N // GN)
NE = 6
RH = 128

F32 = mybir.dt.float32
I32 = mybir.dt.int32
ALU = mybir.AluOpType
ACT = mybir.ActivationFunctionType
AX = mybir.AxisListType


def reached(eng, sem, value):
    if not isinstance(value, int) or value > 0:
        eng.wait_ge(sem, value)


def turns(eng, n, body, peel_last=False):
    body(0, True, False)
    with eng.Fori(1, n - peel_last) as i:
        body(i, False, False)
    if peel_last:
        body(n - 1, False, True)


def tile_at(x, i):
    return x[:, i, :] if isinstance(i, int) else x[:, bass.ds(i, 1), :].rearrange("p a d -> p (a d)")


def persistent(nc, ctx):
    def sb(name, shape, dt=F32):
        return ctx.enter_context(nc.sbuf_tensor(name, shape, dt))

    return {
        "ident": sb("ident", [P, P]),
        "eps": sb("eps", [P, 1]),
        "wx": sb("wx", [P, 2 * H, 2 * D]),
        "wh": sb("wh", [P, H, 2 * D]),
        "wr1": sb("wr1", [P, H, RH]),
        "wr2": sb("wr2", [P, NE]),
        "bx": sb("bx", [P, 2 * H]),
        "br1": sb("br1", [P, 1]),
        "gamma": sb("gamma", [P, H]),
        "beta": sb("beta", [P, H]),
        "be1": sb("be1", [P, NE, H]),
        "be2": sb("be2", [P, NE, H]),
        "be3": sb("be3", [NE, D]),
        "br2": sb("br2", [P, NE]),
        "scale": sb("scale", [P, H]),
        "shift": sb("shift", [P, H]),
        "xlT": sb("xlT", [P, H, NP]),
        "accT": sb("accT", [P, H, ACCW]),
        "we": sb("we", [P, 3, NE, H, D]),
        "far": sb("far", [1, 1], I32),
        "prior": sb("prior", [P, NE, NE]),
    }


def for_edges(nc, ctx):
    def sb(name, shape, dt=F32):
        return ctx.enter_context(nc.sbuf_tensor(name, shape, dt))

    return {
        "below": sb("below", [P, P]),
        "iota": sb("iota", [P, P]),
        "spare": sb("spare", [P, QUAD]),
        "wio": sb("wio", [P, H, 2 * D]),
        "col": sb("col", [P, EC * P, 4]),
        "base": sb("base", [1, EC * P], I32),
    }


def normalise_nodes(nc, c, bank, a, dram):
    with ExitStack() as ctx:
        def sb(name, shape, dt=F32):
            return ctx.enter_context(nc.sbuf_tensor(name, shape, dt))

        def sem(name):
            return ctx.enter_context(nc.semaphore(name))

        X = c["accT"][:].rearrange("p h n -> p (h n)")[:, 0:NT * D].rearrange("p (t d) -> p t d", d=D)
        XN = sb("XN", [P, BLK, D])
        rows = sb("rows", [P, 2, EC, P], I32)
        wrow = sb("wrow", [P, 2, EC, P])
        stats = sb("stats", [P, BLK, 6])
        mv = sb("mv", [P, BLK, 2])
        sd = sb("sd", [P, BLK])
        rstd = sb("rstd", [P, BLK])
        fstat = sb("fstat", [P, H, NP // 512 + 1, 6])
        fmv = sb("fmv", [P, H, 2])
        fsd = sb("fsd", [P, H])
        frs = sb("frs", [P, H])
        fms = sb("fms", [P, H])
        spot = c["we"][:].rearrange("p l e h d -> p (l e h d)")
        EW = EC * P

        def view(n):
            return spot[:, n * EW:(n + 1) * EW].rearrange("p (c j) -> p c j", c=EC)

        srcf, dstf, rel, near, iwn, own, iwf, owf = (view(n) for n in range(8))
        least = sb("least", [P, EC])
        most = sb("most", [P, 1])
        mostr = sb("mostr", [1, 1])

        x_in = [sem(f"x_in{b}") for b in range(NB)]
        tail_in = sem("tail_in")
        tail_z = sem("tail_z")
        e_in = sem("e_in")
        w_in = sem("w_in")
        filled = sem("filled")
        consts = sem("consts")
        idx_f = sem("idx_f")
        lst = sem("lst")
        rel_s = sem("rel_s")
        near_s = sem("near_s")
        wn_s = sem("wn_s")
        wf_s = sem("wf_s")
        most_s = sem("most_s")
        edge_T = sem("edge_T")
        edge_c = sem("edge_c")
        base_T = sem("base_T")
        base_c = sem("base_c")
        most_T = sem("most_T")
        most_r = sem("most_r")
        far_s = sem("far_s")
        st_s = sem("st_s")
        held = sem("held1")
        mv_s = sem("mv_s")
        sd_s = sem("sd_s")
        rs_s = sem("rs_s")
        xn_s = sem("xn_s")
        xT_s = sem("xT_s")
        xTc_s = sem("xTc_s")
        fst = sem("fst")
        fmv_s = sem("fmv_s")
        fsd_s = sem("fsd_s")
        frs_s = sem("frs_s")
        fsc = sem("fsc")
        fms_s = sem("fms_s")
        slow_out = sem("slow_out")

        block = ctx.enter_context(nc.Block())
        full = (ET - 1) // P * P
        rest = ET - 1 - full

        @block.sync
        def _(sp):
            sp.wait_ge(filled, 4)
            for n, e in enumerate((a["src"], a["dst"], a["edge_weight"], a["edge_weight_n2"])):
                to = rows[:, n] if n < 2 else wrow[:, n - 2]
                sp.dma_start(to[:, 0:EC - 1, :], e[0:full * P].rearrange("(c p j) -> p c j", p=P, j=P)).then_inc(e_in, 16)
                sp.dma_start(to[0:rest, EC - 1, :],
                             e[full * P:(full + rest) * P].rearrange("(p j) -> p j", j=P)).then_inc(e_in, 16)
                sp.dma_start(to[rest:rest + 1, EC - 1, 0:ETAIL],
                             e[(full + rest) * P:E].rearrange("(p j) -> p j", p=1)).then_inc(e_in, 16)
            for b in range(NB):
                t0, t1 = b * BLK, min((b + 1) * BLK, NT - 1)
                sp.dma_start(X[:, t0:t1, :], a["x"][t0 * P:t1 * P].rearrange("(t p) d -> p t d", p=P)).then_inc(x_in[b], 16)
            sp.wait_ge(tail_z, 1)
            sp.dma_start(X[0:TAIL, NT - 1, :], a["x"][(NT - 1) * P:N]).then_inc(tail_in, 16)
            sp.wait_ge(wf_s, 2)
            for k, v in enumerate((srcf, dstf, iwf, owf)):
                sp.dma_start(dram["slow"][k].rearrange("(c p j) -> p c j", p=P, j=P), v).then_inc(slow_out, 16)
            sp.wait_ge(slow_out, 64)

        @block.gpsimd
        def _(pool):
            nc.gpsimd.memset(rows[:, 0, EC - 1, :], 0).then_inc(filled, 1)
            nc.gpsimd.memset(rows[:, 1, EC - 1, :], N - 1).then_inc(filled, 1)
            nc.gpsimd.memset(wrow[:, :, EC - 1, :], 0.0).then_inc(filled, 1)
            nc.gpsimd.memset(c["ident"][:], 0.0).then_inc(filled, 1)
            nc.gpsimd.memset(c["below"][:], 1.0).then_inc(consts, 1)
            pool.wait_ge(filled, 4)
            nc.gpsimd.affine_select(out=c["ident"][:], in_=c["ident"][:], compare_op=ALU.not_equal, fill=1.0, base=0,
                                    pattern=[[-1, P]], channel_multiplier=1).then_inc(consts, 1)
            pool.wait_ge(consts, 2)
            nc.gpsimd.affine_select(out=c["below"][:], in_=c["below"][:], compare_op=ALU.is_gt, fill=0.0, base=0,
                                    pattern=[[-1, P]], channel_multiplier=1).then_inc(consts, 1)
            nc.gpsimd.iota(c["iota"][:], pattern=[[1, P]], base=0, channel_multiplier=0,
                           allow_small_or_imprecise_dtypes=True).then_inc(consts, 1)
            nc.gpsimd.iota(c["spare"][:], pattern=[[0, QUAD]], base=SPARE, channel_multiplier=1,
                           allow_small_or_imprecise_dtypes=True).then_inc(consts, 1)
            nc.gpsimd.memset(c["eps"][:], EPS).then_inc(consts, 1)
            nc.gpsimd.memset(c["prior"][:], 1.0).then_inc(consts, 1)
            pool.wait_ge(consts, 7)
            nc.gpsimd.affine_select(out=c["prior"][:], in_=c["prior"][:], compare_op=ALU.is_gt, fill=0.0, base=0,
                                    pattern=[[1, NE], [-1, NE]], channel_multiplier=0).then_inc(consts, 1)

        @block.scalar
        def _(act):
            for name, src in (
                ("wx", a["L0_gnn_W_x2i"].rearrange("(k p) n -> p k n", p=P)),
                ("wh", a["L0_gnn_W_h2h"].rearrange("(k p) n -> p k n", p=P)),
                ("wr1", a["L0_ffn_router_w1"].rearrange("(k p) n -> p k n", p=P)),
                ("wr2", a["L0_ffn_router_w2"]),
                ("bx", a["L0_gnn_b_x2i"].rearrange("(k p) -> p k", p=P)),
                ("br1", a["L0_ffn_router_b1"].rearrange("(p a) -> p a", a=1)),
                ("gamma", a["L0_gnn_gamma"].rearrange("(k p) -> p k", p=P)),
                ("beta", a["L0_gnn_beta"].rearrange("(k p) -> p k", p=P)),
                ("be3", a["L0_ffn_expert_b3"]),
                ("br2", a["L0_ffn_router_b2"].rearrange("(a e) -> a e", a=1).partition_broadcast(P)),
            ):
                act.dma_start(c[name][:], src).then_inc(w_in, 16)
            act.dma_start(c["be1"][:], a["L0_ffn_expert_b1"].rearrange("e (k p) -> p e k", p=P)).then_inc(w_in, 16)
            act.dma_start(c["be2"][:], a["L0_ffn_expert_b2"].rearrange("e (k p) -> p e k", p=P)).then_inc(w_in, 16)
            for k, name in enumerate(("L0_gnn_W_in", "L0_gnn_W_out")):
                act.dma_start(c["wio"][:, :, k * D:(k + 1) * D], a[name].rearrange("(k p) n -> p k n", p=P)).then_inc(w_in, 16)
            for ch in range(EC):
                act.wait_ge(edge_T, ch + 1)
                nc.scalar.copy(c["col"][:, ch * P:(ch + 1) * P, :].rearrange("p t k -> p k t"),
                               bank[ch % 2][:].rearrange("p (k t) -> p k t", k=4)).then_inc(edge_c, 1)
            act.wait_ge(base_T, 1)
            nc.scalar.copy(c["base"][:, 0:4 * P], bank[2][0:1, :]).then_inc(base_c, 1)
            nc.scalar.copy(c["base"][:, 4 * P:EC * P], bank[3][0:1, 0:(EC - 4) * P]).then_inc(base_c, 1)
            act.wait_ge(consts, 6)

            def block_turn(i, first, last):
                act.wait_ge(mv_s, i + 1)
                if not first:
                    act.wait_ge(rs_s, i)
                nc.scalar.activation(sd[:], mv[:, :, 1], ACT.Sqrt, bias=c["eps"][:]).then_inc(sd_s, 1)
                for j in range(BLK):
                    act.wait_ge(xT_s, BLK * i + j + 1)
                    nc.scalar.copy(c["xlT"][:, :, bass.ds((BLK * i + j) * P, P)],
                                   bank[4 + j % 4][:, 0:D].rearrange("p (h n) -> p h n", h=H)).then_inc(xTc_s, 1)

            turns(act, NB, block_turn)
            act.wait_ge(fmv_s, H)
            nc.scalar.activation(fsd[:], fmv[:, :, 1], ACT.Sqrt, bias=c["eps"][:]).then_inc(fsd_s, 1)
            act.wait_ge(w_in, 14 * 16)

        @block.tensor
        def _(pe):
            pe.wait_ge(consts, 2)
            pe.wait_ge(wn_s, 2)
            for ch in range(EC):
                if ch >= 2:
                    pe.wait_ge(edge_c, ch - 1)
                for k, v in enumerate((srcf, rel, iwn, own)):
                    last = nc.tensor.transpose(bank[ch % 2][:, k * P:(k + 1) * P], v[:, ch, :], c["ident"][:])
                last.then_inc(edge_T, 1)
            for ch in range(EC):
                last = nc.tensor.transpose(bank[2 + ch // 4][0:1, (ch % 4) * P:(ch % 4 + 1) * P], least[:, ch:ch + 1], c["ident"][:])
            last.then_inc(base_T, 1)
            pe.wait_ge(most_s, 1)
            pe.wait_ge(base_c, 2)
            nc.tensor.transpose(bank[2][0:1, 0:P], most[:], c["ident"][:]).then_inc(most_T, 1)

            def block_turn(i, first, last):
                for j in range(BLK):
                    pe.wait_ge(xn_s, BLK * i + j + 1)
                    reached(pe, xTc_s, BLK * i + j - 3)
                    for h in range(H):
                        mm = nc.tensor.transpose(bank[4 + j % 4][:, h * P:(h + 1) * P], XN[:, j, h * P:(h + 1) * P], c["ident"][:])
                    mm.then_inc(xT_s, 1)

            turns(pe, NB, block_turn)

        @block.vector
        def _(dve):
            nc.vector.memset(X[:, NT - 1, :], 0.0).then_inc(tail_z, 1)
            dve.wait_ge(e_in, 12 * 16)
            nc.vector.tensor_copy(srcf, rows[:, 0]).then_inc(idx_f, 1)
            nc.vector.tensor_copy(dstf, rows[:, 1]).then_inc(idx_f, 1)
            dve.wait_ge(idx_f, 2)
            nc.vector.tensor_reduce(least[:], dstf, AX.X, ALU.min).then_inc(lst, 1)
            dve.wait_ge(lst, 1)
            nc.vector.tensor_tensor(rel, dstf, least[:].unsqueeze(2).to_broadcast([P, EC, P]), ALU.subtract).then_inc(rel_s, 1)
            dve.wait_ge(rel_s, 1)
            nc.vector.tensor_scalar(near, rel, float(P), None, ALU.is_lt).then_inc(near_s, 1)
            nc.vector.tensor_reduce(most[:], rel, AX.XY, ALU.max).then_inc(most_s, 1)
            dve.wait_ge(near_s, 1)
            nc.vector.tensor_tensor(iwn, wrow[:, 0], near, ALU.mult).then_inc(wn_s, 1)
            nc.vector.tensor_tensor(own, wrow[:, 1], near, ALU.mult).then_inc(wn_s, 1)
            dve.wait_ge(wn_s, 2)
            nc.vector.tensor_tensor(iwf, wrow[:, 0], iwn, ALU.subtract).then_inc(wf_s, 1)
            nc.vector.tensor_tensor(owf, wrow[:, 1], own, ALU.subtract).then_inc(wf_s, 1)
            dve.wait_ge(most_T, 1)
            nc.vector.tensor_reduce(mostr[:], bank[2][0:1, 0:P], AX.X, ALU.max).then_inc(most_r, 1)
            dve.wait_ge(most_r, 1)
            nc.vector.tensor_scalar(c["far"][:], mostr[:], float(P), None, ALU.is_ge).then_inc(far_s, 1)

            def block_turn(i, first, last):
                if not first:
                    dve.wait_ge(xn_s, BLK * i)
                for j in range(BLK):
                    nc.vector.bn_stats(stats[:, j, :], tile_at(X, BLK * i + j)).then_inc(st_s, 1)
                dve.wait_ge(st_s, BLK * i + BLK)
                dve.sem_inc(held, 1)
                for j in range(BLK):
                    mm = nc.vector.bn_aggr(mv[:, j, :], stats[:, j, :])
                mm.then_inc(mv_s, 1)
                dve.wait_ge(sd_s, i + 1)
                nc.vector.reciprocal(rstd[:], sd[:]).then_inc(rs_s, 1)
                dve.wait_ge(rs_s, i + 1)
                for j in range(BLK):
                    if not first:
                        dve.wait_ge(xT_s, BLK * i + j - BLK + 1)
                    nc.vector.tensor_scalar(XN[:, j, :], tile_at(X, BLK * i + j),
                                            mv[:, j, 0:1], rstd[:, j:j + 1], ALU.subtract, ALU.mult).then_inc(xn_s, 1)

            for b in range(NB):
                dve.wait_ge(x_in[b], 16)
            dve.wait_ge(tail_in, 16)
            turns(dve, NB, block_turn)
            dve.wait_ge(xTc_s, NT)
            pieces = [(n, min(n + 512, N)) for n in range(0, N, 512)]
            for h in range(H):
                for k, (n0, n1) in enumerate(pieces):
                    nc.vector.bn_stats(fstat[:, h, k, :], c["xlT"][:, h, n0:n1]).then_inc(fst, 1)
            dve.wait_ge(fst, H * len(pieces))
            for h in range(H):
                nc.vector.bn_aggr(fmv[:, h, :], fstat[:, h, 0:len(pieces), :].rearrange("p k s -> p (k s)")).then_inc(fmv_s, 1)
            dve.wait_ge(fsd_s, 1)
            nc.vector.reciprocal(frs[:], fsd[:]).then_inc(frs_s, 1)
            dve.wait_ge(frs_s, 1)
            dve.wait_ge(w_in, 14 * 16)
            nc.vector.tensor_tensor(c["scale"][:], frs[:], c["gamma"][:], ALU.mult).then_inc(fsc, 1)
            dve.wait_ge(fsc, 1)
            nc.vector.tensor_tensor(fms[:], fmv[:, :, 0], c["scale"][:], ALU.mult).then_inc(fms_s, 1)
            dve.wait_ge(fms_s, 1)
            nc.vector.tensor_tensor(c["shift"][:], c["beta"][:], fms[:], ALU.subtract).then_inc(fsc, 1)


def transform_nodes(nc, c, bank, a, dram):
    with ExitStack() as ctx:
        def sb(name, shape, dt=F32):
            return ctx.enter_context(nc.sbuf_tensor(name, shape, dt))

        def sem(name):
            return ctx.enter_context(nc.semaphore(name))

        hT = sb("hT", [P, BLK, H, P])
        F = sb("F", [P, BLK, 2 * D])
        bio = sb("bio", [P, 2 * D])
        b_in = sem("b_in")
        h_s = sem("h_s")
        mm_s = sem("mm_s")
        f_s = sem("f_s")
        out_in = [sem(f"out_in{j}") for j in range(BLK)]
        out_out = [sem(f"out_out{j}") for j in range(BLK)]
        acc_z = sem("acc_z")
        z_out = sem("z_out")
        we_in = sem("we_in")
        block = ctx.enter_context(nc.Block())

        @block.gpsimd
        def _(pool):
            for n in range(3):
                pool.dma_start(c["we"][:, n], a[f"L0_ffn_expert_w{n + 1}"].rearrange("e (k p) n -> p e k n", p=P)).then_inc(we_in, 16)
            acc = c["accT"][:].rearrange("p h n -> p (h n)")
            nc.gpsimd.memset(acc, 0.0).then_inc(acc_z, 1)
            pool.wait_ge(acc_z, 1)
            for n in ("T0", "T1", "TA"):
                pool.dma_start(dram[n].rearrange("(p r) d -> p (r d)", p=P), acc).then_inc(z_out, 16)
            pool.dma_start(dram["Fin"][NP:ROWS], acc[:, 0:D]).then_inc(z_out, 16)
            pool.dma_start(dram["Fout"][NP:ROWS], acc[:, 0:D]).then_inc(z_out, 16)
            pool.wait_ge(z_out, 80)
            pool.wait_ge(we_in, 48)

        def node_turns(eng, step):
            def body(i, first, last):
                for j in range(BLK):
                    step(i, j, BLK * i + j, first)
            turns(eng, NB, body)

        @block.scalar
        def _(act):
            def step(i, j, t, first):
                reached(act, mm_s, t - BLK + 1)
                for h in range(H):
                    mm = nc.scalar.activation(hT[:, j, h, :], c["xlT"][:, h, bass.ds(t * P, P)], ACT.Identity,
                                              bias=c["shift"][:, h:h + 1], scale=c["scale"][:, h:h + 1])
                mm.then_inc(h_s, 1)
            node_turns(act, step)

        @block.tensor
        def _(pe):
            def step(i, j, t, first):
                pe.wait_ge(h_s, t + 1)
                reached(pe, f_s, t - BLK + 1)
                for h in range(H):
                    mm = nc.tensor.matmul(bank[j][:], hT[:, j, h, :], c["wio"][:, h, :], start=(h == 0), stop=(h == H - 1))
                mm.then_inc(mm_s, 1)
            node_turns(pe, step)

        @block.vector
        def _(dve):
            dve.wait_ge(b_in, 32)

            def step(i, j, t, first):
                dve.wait_ge(mm_s, t + 1)
                if not first:
                    dve.wait_ge(out_in[j], 16 * i)
                    dve.wait_ge(out_out[j], 16 * i)
                nc.vector.tensor_tensor(F[:, j, :], bank[j][:], bio[:], ALU.add).then_inc(f_s, 1)
            node_turns(dve, step)

        @block.sync
        def _(sp):
            for k, name in enumerate(("L0_gnn_b_in", "L0_gnn_b_out")):
                sp.dma_start(bio[:, k * D:(k + 1) * D], a[name].rearrange("(a d) -> a d", a=1).partition_broadcast(P)).then_inc(b_in, 16)

            def step(i, j, t, first):
                sp.wait_ge(f_s, t + 1)
                sp.dma_start(dram["Fin"][bass.ds(t * P, P), :], F[:, j, 0:D]).then_inc(out_in[j], 16)
                sp.dma_start(dram["Fout"][bass.ds(t * P, P), :], F[:, j, D:2 * D]).then_inc(out_out[j], 16)
            node_turns(sp, step)
            for j in range(BLK):
                sp.wait_ge(out_in[j], 16 * NB)
                sp.wait_ge(out_out[j], 16 * NB)


def sum_over_edges(nc, c, bank, a, dram):
    with ExitStack() as ctx:
        def sb(name, shape, dt=F32):
            return ctx.enter_context(nc.sbuf_tensor(name, shape, dt))

        def sem(name):
            return ctx.enter_context(nc.semaphore(name))

        stage = sb("stage", [P, 2, QUAD, 4])
        gsrc = sb("gsrc", [P, 2, QUAD], I32)
        sdst = sb("sdst", [P, 2, QUAD], I32)
        seen = sb("seen", [P, 2, QUAD])
        moved = sb("moved", [P, 2, QUAD])
        G = sb("G", [P, BODY, D])
        W = sb("W", [P, QUAD, D])
        place_w = sb("place_w", [P, 2, P])
        place = sb("place", [P, 2, P])
        same = sb("same", [P, 2, P])
        cnt_junk = sb("cnt_junk", [P, 2, P])
        Ps = sb("Ps", [P, 2, P])
        O = sb("O", [P, BODY, D])

        stage_s = sem("stage_s")
        bc_s = sem("bc_s")
        place_s = sem("place_s")
        same_s = sem("same_s")
        a_s = sem("a_s")
        add_s = sem("add_s")
        p_s = sem("p_s")
        ps_s = sem("ps_s")
        o_s = sem("o_s")
        os_s = sem("os_s")
        held = sem("held3")
        cl_s = sem("cl_s")
        sd_s = sem("sd_s")
        g_in = [sem(f"g_in{j}") for j in range(BODY)]
        w_in = [sem(f"w_in{j}") for j in range(QUAD)]
        t_out = [sem(f"t_out{j}") for j in range(2)]
        block = ctx.enter_context(nc.Block())

        def edge_turns(eng, quad_step, tile_step):
            def body(i, first, last):
                for q in range(2):
                    quad_step(i, q, 2 * i + q, first and q == 0, last and q == 1)
                    for u in range(QUAD):
                        tile_step(i, q, u, BODY * i + QUAD * q + u, first, last)
            turns(eng, TURNS, body, peel_last=True)

        @block.sync
        def _(sp):
            def tile_step(i, q, u, t, first, last):
                reached(sp, o_s, t - QUAD + 1)
                base = sp.value_load(c["base"][0:1, bass.ds(t, 1)], min_val=0, max_val=N - 1)
                sp.dma_start(W[:, u, :], dram["Fout"][bass.ds(base, P), :]).then_inc(w_in[u], 16)
            edge_turns(sp, lambda *x: None, tile_step)

        @block.gpsimd
        def _(pool):
            def gather(j):
                pool.indirect_dma_start(G[:, j, :], None, dram["Fin"],
                                        bass.IndirectOffsetOnAxis(ap=gsrc[:, j // QUAD, j % QUAD:j % QUAD + 1], axis=0)
                                        ).then_inc(g_in[j], 16)

            def scatter(j, t):
                pool.wait_ge(os_s, t + 1)
                reached(pool, t_out[j % 2], 8 * (t - j % 2))
                pool.sem_inc(held, 1)
                pool.indirect_dma_start(dram[f"T{j % 2}"],
                                        bass.IndirectOffsetOnAxis(ap=sdst[:, j // QUAD, j % QUAD:j % QUAD + 1], axis=0),
                                        O[:, j, :], None, compute_op=ALU.add).then_inc(t_out[j % 2], 16)

            def quad_step(i, q, Q, first, last):
                if not last:
                    pool.wait_ge(stage_s, Q + 2)
                if not first:
                    pool.wait_ge(sd_s, Q)

            def tile_step(i, q, u, t, first, last):
                if not (last and q == 1):
                    reached(pool, a_s, t - QUAD + 1)
                    pool.sem_inc(held, 1)
                    gather(QUAD * (1 - q) + u)
                if not (first and q == 0):
                    scatter(QUAD * (1 - q) + u, t - QUAD)

            pool.wait_ge(stage_s, 1)
            for u in range(QUAD):
                gather(u)
            edge_turns(pool, quad_step, tile_step)
            pool.wait_ge(sd_s, TILES // QUAD)
            for u in range(QUAD):
                scatter(QUAD + u, TILES - QUAD + u)
            for j in range(2):
                pool.wait_ge(t_out[j], 16 * (TILES // 2))

        @block.scalar
        def _(act):
            def stage_quad(Q, q):
                nc.scalar.copy(stage[:, q], c["col"][:, bass.ds(QUAD * Q, QUAD), :])
                nc.scalar.copy(gsrc[:, q], c["col"][:, bass.ds(QUAD * Q, QUAD), 0:1].rearrange("p t a -> p (t a)")).then_inc(stage_s, 1)

            def quad_step(i, q, Q, first, last):
                if last:
                    return
                if not first:
                    act.wait_ge(same_s, QUAD * Q)
                    act.wait_ge(bc_s, QUAD * Q)
                    act.wait_ge(sd_s, Q)
                    for u in range(QUAD):
                        reached(act, g_in[QUAD * (1 - q) + u], 8 * (Q + q))
                stage_quad(Q + 1, 1 - q)

            def rows_out(j, t):
                act.wait_ge(o_s, t + 1)
                reached(act, t_out[j % 2], 8 * (t - 6 - j % 2))
                nc.scalar.copy(O[:, j, :], bank[6 + j % 2][:, 0:D]).then_inc(os_s, 1)

            def tile_step(i, q, u, t, first, last):
                act.wait_ge(p_s, t + 1)
                reached(act, o_s, t - 1)
                nc.scalar.copy(Ps[:, u % 2, :], bank[4 + u % 2][:, 0:P]).then_inc(ps_s, 1)
                if not (first and q == 0 and u == 0):
                    rows_out((QUAD * q + u - 1) % BODY, t - 1)

            stage_quad(0, 0)
            edge_turns(act, quad_step, tile_step)
            rows_out(BODY - 1, TILES - 1)

        @block.tensor
        def _(pe):
            def spread(q, Q):
                pe.wait_ge(stage_s, Q + 1)
                reached(pe, same_s, QUAD * (Q - 1))
                for u in range(QUAD):
                    nc.tensor.transpose(bank[q][:, u * P:(u + 1) * P], stage[:, q, u, 0:1].to_broadcast([P, P]),
                                        c["ident"][:]).then_inc(bc_s, 1)

            def quad_step(i, q, Q, first, last):
                if not last:
                    spread(1 - q, Q + 1)

            def out_rows(j, t):
                pe.wait_ge(ps_s, t + 1)
                pe.wait_ge(w_in[j % QUAD], 4 * (t - j % QUAD) + 16)
                reached(pe, os_s, t - 1)
                nc.tensor.matmul(bank[6 + j % 2][:, 0:D], Ps[:, j % 2, :], W[:, j % QUAD, :], start=True, stop=True).then_inc(o_s, 1)

            def tile_step(i, q, u, t, first, last):
                j = QUAD * q + u
                pe.wait_ge(place_s, t + 1)
                pe.wait_ge(g_in[j], 2 * (t - j) + 16)
                reached(pe, add_s, t - 1)
                for h in range(H):
                    mm = nc.tensor.matmul(bank[2 + j % 2][:, h * P:(h + 1) * P], G[:, j, h * P:(h + 1) * P],
                                          place_w[:, j % 2, :], start=True, stop=True)
                mm.then_inc(a_s, 1)
                pe.wait_ge(same_s, t + 1)
                reached(pe, ps_s, t - 1)
                nc.tensor.matmul(bank[4 + j % 2][:, 0:P], place[:, j % 2, :], same[:, j % 2, :], start=True, stop=True).then_inc(p_s, 1)
                if not (first and j == 0):
                    out_rows((j - 1) % BODY, t - 1)

            spread(0, 0)
            edge_turns(pe, quad_step, tile_step)
            out_rows(BODY - 1, TILES - 1)

        @block.vector
        def _(dve):
            def quad_step(i, q, Q, first, last):
                dve.wait_ge(stage_s, Q + 1)

            def add_sums(j, t):
                dve.wait_ge(a_s, t + 1)
                reached(dve, add_s, t)
                base = dve.value_load(c["base"][0:1, bass.ds(t, 1)], min_val=0, max_val=N - 1)
                at = c["accT"][:, :, bass.ds(base, P)]
                nc.vector.tensor_tensor(at, bank[2 + j % 2][:, 0:D].rearrange("p (h n) -> p h n", h=H), at, ALU.add).then_inc(add_s, 1)

            def tile_step(i, q, u, t, first, last):
                j = QUAD * q + u
                s = stage[:, q, u]
                reached(dve, p_s, t - 1)
                nc.vector.tensor_scalar(place_w[:, j % 2, :], c["iota"][:], s[:, 1:2], s[:, 2:3], ALU.is_equal, ALU.mult)
                nc.vector.tensor_scalar(place[:, j % 2, :], c["iota"][:], s[:, 1:2], None, ALU.is_equal).then_inc(place_s, 1)
                if u == 0:
                    dve.wait_ge(bc_s, QUAD * (2 * i + q + 1))
                srcs = bank[q][:, u * P:(u + 1) * P]
                nc.vector.tensor_scalar(same[:, j % 2, :], srcs, s[:, 0:1], s[:, 3:4], ALU.is_equal, ALU.mult)
                nc.vector.scalar_tensor_tensor(out=cnt_junk[:, j % 2, :], in0=srcs, scalar=s[:, 0:1], in1=c["below"][:],
                                               op0=ALU.is_equal, op1=ALU.mult, accum_out=seen[:, q, u:u + 1]).then_inc(same_s, 1)
                if not (first and j == 0):
                    add_sums((j - 1) % BODY, t - 1)
                if u == QUAD - 1:
                    Q = 2 * i + q
                    dve.wait_ge(same_s, t + 1)
                    for k in range(2):
                        reached(dve, t_out[k], 16 * 2 * (Q - 1))
                    nc.vector.scalar_tensor_tensor(out=moved[:, q], in0=seen[:, q], scalar=1.0, in1=c["spare"][:],
                                                   op0=ALU.min, op1=ALU.mult).then_inc(cl_s, 1)
                    dve.wait_ge(cl_s, Q + 1)
                    nc.vector.tensor_tensor(sdst[:, q], moved[:, q], stage[:, q, :, 0:1].rearrange("p t a -> p (t a)"),
                                            ALU.max).then_inc(sd_s, 1)

            edge_turns(dve, quad_step, tile_step)
            add_sums(BODY - 1, TILES - 1)


def sum_far_edges(nc, c, bank, dram):
    with ExitStack() as ctx:
        def sb(name, shape, dt=F32):
            return ctx.enter_context(nc.sbuf_tensor(name, shape, dt))

        def sem(name):
            return ctx.enter_context(nc.semaphore(name))

        edge = sb("far_edge", [P, 4])
        gidx = sb("far_gidx", [P, 2], I32)
        sidx = sb("far_sidx", [P, 2], I32)
        G = sb("far_G", [P, 2, D])
        O = sb("far_O", [P, 2, D])
        same = sb("far_same", [P, 2, P])
        seen = sb("far_seen", [P, 2])
        junk = sb("far_junk", [P, P])
        moved = sb("far_moved", [P, 2])
        e_in = sem("far_e_in")
        gidx_s = sem("far_gidx_s")
        g_in = [sem(f"far_g_in{k}") for k in range(2)]
        bc_s = sem("far_bc_s")
        same_s = sem("far_same_s")
        mm_s = sem("far_mm_s")
        o_s = sem("far_o_s")
        moved_s = sem("far_moved_s")
        sidx_s = sem("far_sidx_s")
        t_out = [sem(f"far_t_out{k}") for k in range(2)]
        held = sem("far_held")
        block = ctx.enter_context(nc.Block())

        def if_far(eng, body):
            far = eng.value_load(c["far"][0:1, 0:1], min_val=0, max_val=1)
            with eng.If(far):
                body(0, True)
                with eng.Fori(1, ET) as t:
                    body(t, False)
            with eng.Else():
                eng.nop()

        @block.sync
        def _(sp):
            def tile_step(t, first):
                reached(sp, t_out[0], 16 * t)
                reached(sp, t_out[1], 16 * t)
                sp.dma_start(edge[:].unsqueeze(2), dram["slow"][:, bass.ds(t * P, P)].rearrange("k (p a) -> p k a", a=1)).then_inc(e_in, 16)
            if_far(sp, tile_step)

        @block.vector
        def _(dve):
            def tile_step(t, first):
                dve.wait_ge(e_in, 16 * t + 16)
                nc.vector.tensor_copy(gidx[:], edge[:, 0:2]).then_inc(gidx_s, 1)
                dve.wait_ge(bc_s, 2 * t + 2)
                for k in range(2):
                    row = bank[k][:, 0:P]
                    nc.vector.tensor_scalar(same[:, k, :], row, edge[:, 1 - k:2 - k], edge[:, 2 + k:3 + k], ALU.is_equal, ALU.mult)
                    nc.vector.scalar_tensor_tensor(out=junk[:], in0=row, scalar=edge[:, 1 - k:2 - k], in1=c["below"][:],
                                                   op0=ALU.is_equal, op1=ALU.mult, accum_out=seen[:, k:k + 1]).then_inc(same_s, 1)
                    dve.wait_ge(same_s, 2 * t + 1 + k)
                nc.vector.scalar_tensor_tensor(out=moved[:], in0=seen[:], scalar=1.0, in1=c["spare"][:, 0:2],
                                               op0=ALU.min, op1=ALU.mult).then_inc(moved_s, 1)
                dve.wait_ge(moved_s, t + 1)
                for k in range(2):
                    nc.vector.tensor_tensor(sidx[:, k:k + 1], moved[:, k:k + 1], edge[:, 1 - k:2 - k], ALU.max).then_inc(sidx_s, 1)
            if_far(dve, tile_step)

        @block.gpsimd
        def _(pool):
            def tile_step(t, first):
                pool.wait_ge(gidx_s, t + 1)
                pool.sem_inc(held, 1)
                for k, table in enumerate(("Fin", "Fout")):
                    pool.indirect_dma_start(G[:, k, :], None, dram[table],
                                            bass.IndirectOffsetOnAxis(ap=gidx[:, k:k + 1], axis=0)).then_inc(g_in[k], 16)
                pool.wait_ge(sidx_s, 2 * t + 2)
                pool.wait_ge(o_s, 2 * t + 2)
                pool.sem_inc(held, 1)
                for k, table in enumerate(("TA", "T0")):
                    pool.indirect_dma_start(dram[table], bass.IndirectOffsetOnAxis(ap=sidx[:, k:k + 1], axis=0),
                                            O[:, k, :], None, compute_op=ALU.add).then_inc(t_out[k], 16)
                for k in range(2):
                    pool.wait_ge(t_out[k], 16 * t + 16)
            if_far(pool, tile_step)

        @block.tensor
        def _(pe):
            def tile_step(t, first):
                pe.wait_ge(e_in, 16 * t + 16)
                for k in range(2):
                    nc.tensor.transpose(bank[k][:, 0:P], edge[:, 1 - k:2 - k].to_broadcast([P, P]), c["ident"][:]).then_inc(bc_s, 1)
                pe.wait_ge(same_s, 2 * t + 2)
                for k in range(2):
                    pe.wait_ge(g_in[k], 16 * t + 16)
                    nc.tensor.matmul(bank[2 + k][:, 0:D], same[:, k, :], G[:, k, :], start=True, stop=True).then_inc(mm_s, 1)
            if_far(pe, tile_step)

        @block.scalar
        def _(act):
            def tile_step(t, first):
                for k in range(2):
                    act.wait_ge(mm_s, 2 * t + 1 + k)
                    nc.scalar.copy(O[:, k, :], bank[2 + k][:, 0:D]).then_inc(o_s, 1)
            if_far(act, tile_step)


def update_nodes(nc, c, bank, a, dram, out):
    with ExitStack() as ctx:
        def sb(name, shape, dt=F32):
            return ctx.enter_context(nc.sbuf_tensor(name, shape, dt))

        def sem(name):
            return ctx.enter_context(nc.semaphore(name))

        xg = sb("xg", [SP_, ST, D])
        tg = sb("tg", [SP_, 3, ST, D])
        y = sb("y", [SP_, ST, D])
        aT = sb("aT", [P, 2 * H, GN])
        hT = sb("hTg", [P, H, GN])
        gate = sb("gate", [P, H, GN])
        new = sb("new", [P, H, GN])
        yT = sb("yT", [P, H, GN])
        rhT = sb("rhT", [P, GN])
        h1 = sb("h1", [P, H, GN])
        h2 = sb("h2", [P, H, GN])
        cfT = sb("cfT", [NE, GN])
        stats = sb("lstats", [SP_, ST, 6])
        mv = sb("lmv", [SP_, ST, 2])
        sd = sb("lsd", [SP_, ST])
        rstd = sb("lrstd", [SP_, ST])
        lg = sb("lg", [SP_, ST, NE])
        lg2 = sb("lg2", [SP_, ST, NE])
        pe_ = sb("pexp", [SP_, ST, NE])
        pr = sb("pr", [SP_, ST, NE])
        m1 = sb("m1", [SP_, ST])
        s1 = sb("s1", [SP_, ST])
        r1 = sb("r1", [SP_, ST])
        m2 = sb("m2", [SP_, ST])
        s2 = sb("s2", [SP_, ST])
        r2 = sb("r2", [SP_, ST])
        pd = sb("pd", [SP_, ST, NE])
        pex = sb("pex", [SP_, ST, NE])
        pse = sb("pse", [SP_, ST, NE])
        cf = sb("cf", [SP_, ST, NE])
        gt = sb("gt", [SP_, ST, NE, NE])
        eq = sb("eq", [SP_, ST, NE, NE])
        rank = sb("rank", [SP_, ST, NE])

        held = sem("held4")
        x_in = sem("gx_in")
        t_in = sem("gt_in")
        ts_s = sem("ts_s")
        tT_s = sem("tT_s")
        ao_s = sem("ao_s")
        ai_s = sem("ai_s")
        h_s = sem("gh_s")
        g_s = sem("g_s")
        act_s = sem("act_s")
        v = sem("v")
        gnn_s = sem("gnn_s")
        gT_s = sem("gT_s")
        x1_s = sem("x1_s")
        mv_s = sem("lmv_s")
        sd_s = sem("lsd_s")
        y_s = sem("y_s")
        yT_s = sem("yT_s")
        yTc_s = sem("yTc_s")
        r_s = sem("r_s")
        rh_s = sem("rh_s")
        lg_s = sem("lg_s")
        l2_s = sem("l2_s")
        e1_s = sem("e1_s")
        pd_s = sem("pd_s")
        e2_s = sem("e2_s")
        cf_s = sem("cf_s")
        cT_s = sem("cT_s")
        cTc_s = sem("cTc_s")
        b3_s = sem("b3_s")
        acc0_s = sem("acc0_s")
        l1_s = sem("l1_s")
        h1_s = sem("h1_s")
        l2m_s = sem("l2m_s")
        h2_s = sem("h2_s")
        l3_s = sem("l3_s")
        acc_s = sem("acc_s")
        o_out = sem("o_out")
        block = ctx.enter_context(nc.Block())

        def group_turns(eng, step):
            def body(i, first, last):
                step(i, N - GN if last else GN * i, last)
            turns(eng, GROUPS, body, peel_last=True)

        def rows_of(t, s):
            return t[bass.ds(s, GN), :].rearrange("(j p) d -> p j d", p=SP_)

        def three(row):
            return row.unsqueeze(2).to_broadcast([SP_, ST, NE])

        @block.sync
        def _(sp):
            def step(g, s, last):
                reached(sp, tT_s, 4 * g)
                for n, t in enumerate(("T0", "T1", "TA")):
                    sp.dma_start(tg[:, n], rows_of(dram[t], s)).then_inc(t_in, 16)
                reached(sp, o_out, 16 * g)
                sp.dma_start(xg[:], rows_of(a["x"], s)).then_inc(x_in, 16)
                sp.wait_ge(acc_s, NE * ST * (g + 1))
                sp.dma_start(rows_of(out, s), xg[:]).then_inc(o_out, 16)
            group_turns(sp, step)
            sp.wait_ge(o_out, 16 * GROUPS)

        @block.gpsimd
        def _(pool):
            def step(g, s, last):
                pool.wait_ge(t_in, 48 * (g + 1))
                nc.gpsimd.tensor_tensor(tg[:, 0], tg[:, 0], tg[:, 1], ALU.add).then_inc(ts_s, 1)
            group_turns(pool, step)

        @block.scalar
        def _(act):
            def step(g, s, last):
                reached(act, g_s, 4 * g)
                for h in range(H):
                    if h == 0:
                        reached(act, gnn_s, g)
                    nc.scalar.activation(hT[:, h, :], c["xlT"][:, h, bass.ds(s, GN)], ACT.Identity,
                                         bias=c["shift"][:, h:h + 1], scale=c["scale"][:, h:h + 1]).then_inc(h_s, 1)
                for h in range(H):
                    act.wait_ge(tT_s, 4 * g + 1 + h)
                    nc.scalar.copy(aT[:, H + h, :], bank[h][:, 0:GN]).then_inc(ao_s, 1)
                for m in range(2 * H):
                    act.wait_ge(g_s, 4 * g + m + 1)
                    nc.scalar.activation((gate if m < H else new)[:, m % H, :], bank[4 + m][:, 0:GN],
                                         ACT.Sigmoid if m < H else ACT.Tanh, bias=c["bx"][:, m:m + 1]).then_inc(act_s, 1)
                act.wait_ge(mv_s, g + 1)
                nc.scalar.activation(sd[:], mv[:, :, 1], ACT.Sqrt, bias=c["eps"][0:SP_]).then_inc(sd_s, 1)
                for h in range(H):
                    act.wait_ge(yT_s, H * g + h + 1)
                    nc.scalar.copy(yT[:, h, :], bank[2 + h][:, 0:GN]).then_inc(yTc_s, 1)
                act.wait_ge(r_s, g + 1)
                nc.scalar.activation(rhT[:], bank[4][:, 0:GN], ACT.Relu, bias=c["br1"][:]).then_inc(rh_s, 1)
                act.wait_ge(l2_s, g + 1)
                nc.scalar.activation(pe_[:], lg2[:], ACT.Exp).then_inc(e1_s, 1)
                act.wait_ge(pd_s, g + 1)
                nc.scalar.activation(pex[:], pd[:], ACT.Exp).then_inc(e2_s, 1)
                act.wait_ge(cT_s, g + 1)
                nc.scalar.copy(cfT[:], bank[6][0:NE, 0:GN]).then_inc(cTc_s, 1)

                def relus(e, to, b0, mm, bias, sem_out):
                    for m in range(H):
                        act.wait_ge(mm, H * (NE * g + e) + m + 1)
                        nc.scalar.activation(to[:, m, :], bank[b0 + m][:, 0:GN], ACT.Relu,
                                             bias=c[bias][:, e, m:m + 1]).then_inc(sem_out, 1)

                relus(0, h1, 0, l1_s, "be1", h1_s)
                for e in range(NE):
                    reached(act, l3_s, ST * (NE * g + e))
                    relus(e, h2, 2, l2m_s, "be2", h2_s)
                    if e + 1 < NE:
                        act.wait_ge(l2m_s, H * (NE * g + e + 1))
                        relus(e + 1, h1, 0, l1_s, "be1", h1_s)
            group_turns(act, step)

        @block.tensor
        def _(pe):
            def step(g, s, last):
                pe.wait_ge(ts_s, g + 1)
                for n, k in ((0, 0), (2, 2)):
                    for h in range(H):
                        for j in range(ST):
                            mm = nc.tensor.transpose(bank[k + h][:, j * SP_:(j + 1) * SP_], tg[:, n, j, h * P:(h + 1) * P],
                                                     c["ident"][0:SP_, 0:SP_])
                        mm.then_inc(tT_s, 1)
                pe.wait_ge(ao_s, H * (g + 1))
                pe.wait_ge(ai_s, H * (g + 1))
                pe.wait_ge(h_s, H * (g + 1))
                reached(pe, acc_s, NE * ST * g)
                for m in range(2 * H):
                    o = bank[4 + m][:, 0:GN]
                    for k in range(2 * H):
                        nc.tensor.matmul(o, c["wx"][:, k, m * P:(m + 1) * P], aT[:, k, :], start=(k == 0), stop=False)
                    for k in range(H):
                        mm = nc.tensor.matmul(o, c["wh"][:, k, m * P:(m + 1) * P], hT[:, k, :], start=False, stop=(k == H - 1))
                    mm.then_inc(g_s, 1)
                pe.wait_ge(gnn_s, g + 1)
                for j in range(ST):
                    for h in range(H):
                        mm = nc.tensor.transpose(bank[j // 2][0:SP_, (j % 2) * D + h * P:(j % 2) * D + (h + 1) * P],
                                                 new[:, h, j * SP_:(j + 1) * SP_], c["ident"][:])
                    mm.then_inc(gT_s, 1)
                for h in range(H):
                    for j in range(ST):
                        if h == 0:
                            pe.wait_ge(y_s, ST * g + j + 1)
                        mm = nc.tensor.transpose(bank[2 + h][:, j * SP_:(j + 1) * SP_], y[:, j, h * P:(h + 1) * P], c["ident"][0:SP_, 0:SP_])
                    mm.then_inc(yT_s, 1)
                pe.wait_ge(yTc_s, H * (g + 1))
                for k in range(H):
                    mm = nc.tensor.matmul(bank[4][:, 0:GN], c["wr1"][:, k, :], yT[:, k, :], start=(k == 0), stop=(k == H - 1))
                mm.then_inc(r_s, 1)
                pe.wait_ge(rh_s, g + 1)
                for j in range(ST):
                    mm = nc.tensor.matmul(bank[5][0:SP_, j * NE:(j + 1) * NE], rhT[:, j * SP_:(j + 1) * SP_], c["wr2"][:], start=True, stop=True)
                mm.then_inc(lg_s, 1)

                def layer(e, n, b0, src, sem_out):
                    for m in range(H):
                        for k in range(H):
                            mm = nc.tensor.matmul(bank[b0 + m][:, 0:GN], c["we"][:, n, e, k, m * P:(m + 1) * P], src[:, k, :],
                                                  start=(k == 0), stop=(k == H - 1))
                        mm.then_inc(sem_out, 1)

                pe.wait_ge(x1_s, 2 * (g + 1))
                layer(0, 0, 0, yT, l1_s)
                pe.wait_ge(cf_s, g + 1)
                for j in range(ST):
                    mm = nc.tensor.transpose(bank[6][0:NE, j * SP_:(j + 1) * SP_], cf[:, j, :], c["ident"][0:SP_, 0:SP_])
                mm.then_inc(cT_s, 1)
                pe.wait_ge(cTc_s, g + 1)
                for j in range(ST):
                    mm = nc.tensor.matmul(bank[4 + j // 2][0:SP_, (j % 2) * D:(j % 2 + 1) * D], cfT[:, j * SP_:(j + 1) * SP_], c["be3"][:], start=True, stop=True)
                mm.then_inc(b3_s, 1)
                for e in range(NE):
                    n = NE * g + e
                    pe.wait_ge(h1_s, H * (n + 1))
                    reached(pe, h2_s, H * n)
                    layer(e, 1, 2, h1, l2m_s)
                    if e + 1 < NE:
                        layer(e + 1, 0, 0, yT, l1_s)
                    pe.wait_ge(h2_s, H * (n + 1))
                    if e % 2 == 1:
                        pe.wait_ge(acc0_s, g + 1)
                    for j in range(ST):
                        if e >= 2:
                            pe.wait_ge(acc_s, ST * (n - 2) + 2 * (j // 2 + 1))
                        b = 4 + 2 * ((e + 1) % 2) + j // 2
                        for k in range(H):
                            mm = nc.tensor.matmul(bank[b][0:SP_, (j % 2) * D:(j % 2 + 1) * D], h2[:, k, j * SP_:(j + 1) * SP_],
                                                  c["we"][:, 2, e, k, :], start=(k == 0), stop=(k == H - 1))
                        mm.then_inc(l3_s, 1)
            group_turns(pe, step)

        @block.vector
        def _(dve):
            OWN = 17

            def step(g, s, last):
                count = [0]

                def link(ins):
                    count[0] += 1
                    ins.then_inc(v, 1)
                    dve.wait_ge(v, OWN * g + count[0])

                reached(dve, g_s, 4 * g)
                for h in range(H):
                    dve.wait_ge(tT_s, 4 * g + 3 + h)
                    nc.vector.tensor_tensor(aT[:, h, :], bank[2 + h][:, 0:GN], c["accT"][:, h, bass.ds(s, GN)], ALU.add).then_inc(ai_s, 1)
                dve.wait_ge(act_s, 4 * (g + 1))
                link(nc.vector.tensor_tensor(hT[:], hT[:], new[:], ALU.subtract))
                link(nc.vector.tensor_tensor(hT[:], hT[:], gate[:], ALU.mult))
                nc.vector.tensor_tensor(new[:], new[:], hT[:], ALU.add).then_inc(gnn_s, 1)
                dve.wait_ge(x_in, 16 * (g + 1))
                for j in range(0, ST, 2):
                    dve.wait_ge(gT_s, ST * g + j + 2)
                    nc.vector.tensor_tensor(xg[:, j:j + 2, :], xg[:, j:j + 2, :], bank[j // 2][0:SP_, :].rearrange("p (j d) -> p j d", j=2), ALU.add).then_inc(x1_s, 1)
                dve.wait_ge(x1_s, 2 * (g + 1))
                for j in range(ST):
                    mm = nc.vector.bn_stats(stats[:, j, :], xg[:, j, :])
                mm.then_inc(v, 1)
                count[0] += 1
                dve.wait_ge(v, OWN * g + count[0])
                dve.sem_inc(held, 1)
                for j in range(ST):
                    mm = nc.vector.bn_aggr(mv[:, j, :], stats[:, j, :])
                mm.then_inc(mv_s, 1)
                dve.wait_ge(sd_s, g + 1)
                link(nc.vector.reciprocal(rstd[:], sd[:]))
                for j in range(ST):
                    nc.vector.tensor_scalar(y[:, j, :], xg[:, j, :], mv[:, j, 0:1], rstd[:, j:j + 1], ALU.subtract, ALU.mult).then_inc(y_s, 1)
                dve.wait_ge(lg_s, g + 1)
                link(nc.vector.tensor_tensor(lg[:], bank[5][0:SP_, 0:ST * NE].rearrange("p (j e) -> p j e", e=NE),
                                             c["br2"][0:SP_, :].unsqueeze(1).to_broadcast([SP_, ST, NE]), ALU.add))
                link(nc.vector.tensor_reduce(m1[:], lg[:], AX.X, ALU.max))
                nc.vector.tensor_tensor(lg2[:], lg[:], three(m1[:]), ALU.subtract).then_inc(l2_s, 1)
                dve.wait_ge(e1_s, g + 1)
                link(nc.vector.tensor_reduce(s1[:], pe_[:], AX.X, ALU.add))
                link(nc.vector.reciprocal(r1[:], s1[:]))
                link(nc.vector.tensor_tensor(pr[:], pe_[:], three(r1[:]), ALU.mult))
                link(nc.vector.tensor_reduce(m2[:], pr[:], AX.X, ALU.max))
                nc.vector.tensor_tensor(pd[:], pr[:], three(m2[:]), ALU.subtract).then_inc(pd_s, 1)
                other = pr[:].unsqueeze(2).to_broadcast([SP_, ST, NE, NE])
                own = pr[:].unsqueeze(3).to_broadcast([SP_, ST, NE, NE])
                nc.vector.tensor_tensor(gt[:], other, own, ALU.is_gt)
                link(nc.vector.tensor_tensor(eq[:], other, own, ALU.is_equal))
                link(nc.vector.tensor_tensor(eq[:], eq[:], c["prior"][0:SP_].unsqueeze(1).to_broadcast([SP_, ST, NE, NE]), ALU.mult))
                link(nc.vector.tensor_tensor(gt[:], gt[:], eq[:], ALU.add))
                link(nc.vector.tensor_reduce(rank[:], gt[:], AX.X, ALU.add))
                dve.wait_ge(e2_s, g + 1)
                link(nc.vector.scalar_tensor_tensor(out=pse[:], in0=rank[:], scalar=2.0, in1=pex[:], op0=ALU.is_lt, op1=ALU.mult))
                link(nc.vector.tensor_reduce(s2[:], pse[:], AX.X, ALU.add))
                link(nc.vector.reciprocal(r2[:], s2[:]))
                assert count[0] == OWN, count
                nc.vector.tensor_tensor(cf[:], pse[:], three(r2[:]), ALU.mult).then_inc(cf_s, 1)
                dve.wait_ge(b3_s, g + 1)
                for j in range(0, ST, 2):
                    mm = nc.vector.tensor_tensor(xg[:, j:j + 2, :], xg[:, j:j + 2, :], bank[4 + j // 2][0:SP_, :].rearrange("p (j d) -> p j d", j=2), ALU.add)
                mm.then_inc(acc0_s, 1)
                dve.wait_ge(acc0_s, g + 1)
                dve.wait_ge(cf_s, g + 1)
                for e in range(NE):
                    n = NE * g + e
                    for j in range(ST):
                        dve.wait_ge(l3_s, ST * n + 2 * (j // 2 + 1))
                        reached(dve, acc_s, ST * (n - 1) + j + 1)
                        b = 4 + 2 * ((e + 1) % 2) + j // 2
                        nc.vector.scalar_tensor_tensor(out=xg[:, j, :], in0=bank[b][0:SP_, (j % 2) * D:(j % 2 + 1) * D],
                                                       scalar=cf[:, j, e:e + 1], in1=xg[:, j, :],
                                                       op0=ALU.mult, op1=ALU.add).then_inc(acc_s, 1)
            group_turns(dve, step)


def graph_layer(nc, a, out):
    dram = {n: nc.dram_tensor(n, [ROWS, D], F32).ap() for n in ("Fin", "Fout", "T0", "T1", "TA")}
    dram["slow"] = nc.dram_tensor("slow", [4, EC * P * P], F32).ap()
    with ExitStack() as ctx:
        ctx.enter_context(nc.allow_non_contiguous_dma(reason="bias columns, and single edges on the rare path"))
        bank = [ctx.enter_context(nc.psum_tensor(f"bank{n}", [P, 512], F32)) for n in range(8)]
        c = persistent(nc, ctx)
        with ExitStack() as edges:
            c.update(for_edges(nc, edges))
            normalise_nodes(nc, c, bank, a, dram)
            transform_nodes(nc, c, bank, a, dram)
            sum_over_edges(nc, c, bank, a, dram)
            sum_far_edges(nc, c, bank, dram)
        update_nodes(nc, c, bank, a, dram, out)


_INS = ['x', 'src', 'dst', 'edge_weight', 'edge_weight_n2', 'L0_gnn_gamma', 'L0_gnn_beta', 'L0_gnn_W_in', 'L0_gnn_b_in',
        'L0_gnn_W_out', 'L0_gnn_b_out', 'L0_gnn_W_x2i', 'L0_gnn_b_x2i', 'L0_gnn_W_h2h', 'L0_ffn_router_w1',
        'L0_ffn_router_b1', 'L0_ffn_router_w2', 'L0_ffn_router_b2', 'L0_ffn_expert_w1', 'L0_ffn_expert_b1',
        'L0_ffn_expert_w2', 'L0_ffn_expert_b2', 'L0_ffn_expert_w3', 'L0_ffn_expert_b3']


def kernel(**inputs):
    import numpy as _np
    import concourse.bacc as _bacc
    from concourse import mybir as _mybir
    from concourse.bass_utils import run_bass_kernel_spmd as _run

    nc = _bacc.Bacc("TRN2", target_bir_lowering=False, num_devices=1)
    arrays, args = {}, {}
    for name in _INS:
        arr = _np.ascontiguousarray(inputs[name])
        arrays[f"in_{name}_dram"] = arr
        args[name] = nc.dram_tensor(f"in_{name}_dram", arr.shape, _mybir.dt.from_np(arr.dtype), kind="ExternalInput").ap()
    out = nc.dram_tensor("out_0_dram", (N, D), F32, kind="ExternalOutput").ap()
    graph_layer(nc, args, out)
    r = _run(nc, [arrays], core_ids=[0])
    return r.results[0]["out_0_dram"]
```

```python
from contextlib import ExitStack

import concourse.bass as bass
from concourse import mybir

P = 128
N = 6250
E = 100000
D = 256
H = D // P
EPS = 1e-5
NT = -(-N // P)
NP = NT * P
TAIL = N - (NT - 1) * P
BLK = 7
NB = NT // BLK
ET = -(-E // P)
ETAIL = E - (ET - 1) * P
EC = -(-ET // P)
QUAD = 4
BODY = 2 * QUAD
TILES = -(-ET // BODY) * BODY
TURNS = TILES // BODY
ROWS = 6400
SPARE = ROWS - P
ACCW = ROWS
GN = 448
ST = 4
GP = GN // ST
GROUPS = -(-N // GN)
NE = 6
ROWX = D + 2
REG = 6400
STEPS = 2 * GROUPS * GN // P + NE
RH = 128

F32 = mybir.dt.float32
I32 = mybir.dt.int32
BF16 = mybir.dt.bfloat16
ALU = mybir.AluOpType
ACT = mybir.ActivationFunctionType
AX = mybir.AxisListType


def reached(eng, sem, value):
    if not isinstance(value, int) or value > 0:
        eng.wait_ge(sem, value)


def turns(eng, n, body, peel_last=False):
    body(0, True, False)
    with eng.Fori(1, n - peel_last) as i:
        body(i, False, False)
    if peel_last:
        body(n - 1, False, True)


def tile_at(x, i):
    return x[:, i, :] if isinstance(i, int) else x[:, bass.ds(i, 1), :].rearrange("p a d -> p (a d)")


def persistent(nc, ctx):
    def sb(name, shape, dt=F32):
        return ctx.enter_context(nc.sbuf_tensor(name, shape, dt))

    return {
        "ident": sb("ident", [P, P]),
        "eps": sb("eps", [P, 1]),
        "wx": sb("wx", [P, 2 * H, 2 * D]),
        "wh": sb("wh", [P, H, 2 * D]),
        "wr1": sb("wr1", [P, H, RH]),
        "wr2": sb("wr2", [P, NE]),
        "bx": sb("bx", [P, 2 * H]),
        "br1": sb("br1", [P, 1]),
        "gamma": sb("gamma", [P, H]),
        "beta": sb("beta", [P, H]),
        "be1": sb("be1", [P, NE, H]),
        "be2": sb("be2", [P, NE, H]),
        "count": sb("count", [P, NE]),
        "region": sb("region", [P, ST * NE]),
        "br2": sb("br2", [P, NE]),
        "scale": sb("scale", [P, H]),
        "shift": sb("shift", [P, H]),
        "xlT": sb("xlT", [P, H, NP]),
        "accT": sb("accT", [P, H, ACCW]),
        "we": sb("we", [P, 3, NE, H, D]),
        "far": sb("far", [1, 1], I32),
        "prior": sb("prior", [P, NE, NE]),
    }


def for_edges(nc, ctx):
    def sb(name, shape, dt=F32):
        return ctx.enter_context(nc.sbuf_tensor(name, shape, dt))

    return {
        "below": sb("below", [P, P]),
        "iota": sb("iota", [P, P]),
        "spare": sb("spare", [P, QUAD]),
        "wio": sb("wio", [P, H, 2 * D]),
        "col": sb("col", [P, EC * P, 4]),
        "base": sb("base", [1, EC * P], I32),
    }


def normalise_nodes(nc, c, bank, a, dram):
    with ExitStack() as ctx:
        def sb(name, shape, dt=F32):
            return ctx.enter_context(nc.sbuf_tensor(name, shape, dt))

        def sem(name):
            return nc.alloc_semaphore("n_" + name)

        X = c["accT"][:].rearrange("p h n -> p (h n)")[:, 0:NT * D].rearrange("p (t d) -> p t d", d=D)
        XN = sb("XN", [P, BLK, D])
        rows = sb("rows", [P, 2, EC, P], I32)
        wrow = sb("wrow", [P, 2, EC, P])
        stats = sb("stats", [P, BLK, 6])
        mv = sb("mv", [P, BLK, 2])
        sd = sb("sd", [P, BLK])
        rstd = sb("rstd", [P, BLK])
        fstat = sb("fstat", [P, H, NP // 512 + 1, 6])
        fmv = sb("fmv", [P, H, 2])
        fsd = sb("fsd", [P, H])
        frs = sb("frs", [P, H])
        fms = sb("fms", [P, H])
        spot = c["we"][:].rearrange("p l e h d -> p (l e h d)")
        EW = EC * P

        def view(n):
            return spot[:, n * EW:(n + 1) * EW].rearrange("p (c j) -> p c j", c=EC)

        srcf, dstf, rel, near, iwn, own, iwf, owf = (view(n) for n in range(8))
        least = sb("least", [P, EC])
        most = sb("most", [P, 1])
        mostr = sb("mostr", [1, 1])

        x_in = [sem(f"x_in{b}") for b in range(NB)]
        tail_in = sem("tail_in")
        tail_z = sem("tail_z")
        e_in = sem("e_in")
        w_in = sem("w_in")
        filled = sem("filled")
        consts = sem("consts")
        idx_f = sem("idx_f")
        lst = sem("lst")
        rel_s = sem("rel_s")
        near_s = sem("near_s")
        wn_s = sem("wn_s")
        wf_s = sem("wf_s")
        most_s = sem("most_s")
        edge_T = sem("edge_T")
        edge_c = sem("edge_c")
        base_T = sem("base_T")
        base_c = sem("base_c")
        most_T = sem("most_T")
        most_r = sem("most_r")
        far_s = sem("far_s")
        st_s = sem("st_s")
        held = sem("held1")
        mv_s = sem("mv_s")
        sd_s = sem("sd_s")
        rs_s = sem("rs_s")
        xn_s = sem("xn_s")
        xT_s = sem("xT_s")
        xTc_s = sem("xTc_s")
        fst = sem("fst")
        fmv_s = sem("fmv_s")
        fsd_s = sem("fsd_s")
        frs_s = sem("frs_s")
        fsc = sem("fsc")
        fms_s = sem("fms_s")
        slow_out = sem("slow_out")

        block = ctx.enter_context(nc.Block())
        full = (ET - 1) // P * P
        rest = ET - 1 - full

        @block.sync
        def _(sp):
            sp.wait_ge(filled, 4)
            for n, e in enumerate((a["src"], a["dst"], a["edge_weight"], a["edge_weight_n2"])):
                to = rows[:, n] if n < 2 else wrow[:, n - 2]
                sp.dma_start(to[:, 0:EC - 1, :], e[0:full * P].rearrange("(c p j) -> p c j", p=P, j=P)).then_inc(e_in, 16)
                sp.dma_start(to[0:rest, EC - 1, :],
                             e[full * P:(full + rest) * P].rearrange("(p j) -> p j", j=P)).then_inc(e_in, 16)
                sp.dma_start(to[rest:rest + 1, EC - 1, 0:ETAIL],
                             e[(full + rest) * P:E].rearrange("(p j) -> p j", p=1)).then_inc(e_in, 16)
            for b in range(NB):
                t0, t1 = b * BLK, min((b + 1) * BLK, NT - 1)
                sp.dma_start(X[:, t0:t1, :], a["x"][t0 * P:t1 * P].rearrange("(t p) d -> p t d", p=P)).then_inc(x_in[b], 16)
            sp.wait_ge(tail_z, 1)
            sp.dma_start(X[0:TAIL, NT - 1, :], a["x"][(NT - 1) * P:N]).then_inc(tail_in, 16)
            sp.wait_ge(wf_s, 2)
            for k, v in enumerate((srcf, dstf, iwf, owf)):
                sp.dma_start(dram["slow"][k].rearrange("(c p j) -> p c j", p=P, j=P), v).then_inc(slow_out, 16)
            sp.wait_ge(slow_out, 64)

        @block.gpsimd
        def _(pool):
            nc.gpsimd.memset(rows[:, 0, EC - 1, :], 0).then_inc(filled, 1)
            nc.gpsimd.memset(rows[:, 1, EC - 1, :], N - 1).then_inc(filled, 1)
            nc.gpsimd.memset(wrow[:, :, EC - 1, :], 0.0).then_inc(filled, 1)
            nc.gpsimd.memset(c["ident"][:], 0.0).then_inc(filled, 1)
            nc.gpsimd.memset(c["below"][:], 1.0).then_inc(consts, 1)
            pool.wait_ge(filled, 4)
            nc.gpsimd.affine_select(out=c["ident"][:], in_=c["ident"][:], compare_op=ALU.not_equal, fill=1.0, base=0,
                                    pattern=[[-1, P]], channel_multiplier=1).then_inc(consts, 1)
            pool.wait_ge(consts, 2)
            nc.gpsimd.affine_select(out=c["below"][:], in_=c["below"][:], compare_op=ALU.is_gt, fill=0.0, base=0,
                                    pattern=[[-1, P]], channel_multiplier=1).then_inc(consts, 1)
            nc.gpsimd.iota(c["iota"][:], pattern=[[1, P]], base=0, channel_multiplier=0,
                           allow_small_or_imprecise_dtypes=True).then_inc(consts, 1)
            nc.gpsimd.iota(c["spare"][:], pattern=[[0, QUAD]], base=SPARE, channel_multiplier=1,
                           allow_small_or_imprecise_dtypes=True).then_inc(consts, 1)
            nc.gpsimd.memset(c["eps"][:], EPS).then_inc(consts, 1)
            nc.gpsimd.memset(c["prior"][:], 1.0).then_inc(consts, 1)
            pool.wait_ge(consts, 7)
            nc.gpsimd.affine_select(out=c["prior"][:], in_=c["prior"][:], compare_op=ALU.is_gt, fill=0.0, base=0,
                                    pattern=[[1, NE], [-1, NE]], channel_multiplier=0).then_inc(consts, 1)

        @block.scalar
        def _(act):
            for name, src in (
                ("wx", a["L0_gnn_W_x2i"].rearrange("(k p) n -> p k n", p=P)),
                ("wh", a["L0_gnn_W_h2h"].rearrange("(k p) n -> p k n", p=P)),
                ("wr1", a["L0_ffn_router_w1"].rearrange("(k p) n -> p k n", p=P)),
                ("wr2", a["L0_ffn_router_w2"]),
                ("bx", a["L0_gnn_b_x2i"].rearrange("(k p) -> p k", p=P)),
                ("br1", a["L0_ffn_router_b1"].rearrange("(p a) -> p a", a=1)),
                ("gamma", a["L0_gnn_gamma"].rearrange("(k p) -> p k", p=P)),
                ("beta", a["L0_gnn_beta"].rearrange("(k p) -> p k", p=P)),
                ("br2", a["L0_ffn_router_b2"].rearrange("(a e) -> a e", a=1).partition_broadcast(P)),
            ):
                act.dma_start(c[name][:], src).then_inc(w_in, 16)
            act.dma_start(c["be1"][:], a["L0_ffn_expert_b1"].rearrange("e (k p) -> p e k", p=P)).then_inc(w_in, 16)
            act.dma_start(c["be2"][:], a["L0_ffn_expert_b2"].rearrange("e (k p) -> p e k", p=P)).then_inc(w_in, 16)
            for k, name in enumerate(("L0_gnn_W_in", "L0_gnn_W_out")):
                act.dma_start(c["wio"][:, :, k * D:(k + 1) * D], a[name].rearrange("(k p) n -> p k n", p=P)).then_inc(w_in, 16)
            for ch in range(EC):
                act.wait_ge(edge_T, ch + 1)
                nc.scalar.copy(c["col"][:, ch * P:(ch + 1) * P, :].rearrange("p t k -> p k t"),
                               bank[ch % 2][:].rearrange("p (k t) -> p k t", k=4)).then_inc(edge_c, 1)
            act.wait_ge(base_T, 1)
            nc.scalar.copy(c["base"][:, 0:4 * P], bank[2][0:1, :]).then_inc(base_c, 1)
            nc.scalar.copy(c["base"][:, 4 * P:EC * P], bank[3][0:1, 0:(EC - 4) * P]).then_inc(base_c, 1)
            act.wait_ge(consts, 6)

            def block_turn(i, first, last):
                act.wait_ge(mv_s, i + 1)
                if not first:
                    act.wait_ge(rs_s, i)
                nc.scalar.activation(sd[:], mv[:, :, 1], ACT.Sqrt, bias=c["eps"][:]).then_inc(sd_s, 1)
                for j in range(BLK):
                    act.wait_ge(xT_s, BLK * i + j + 1)
                    nc.scalar.copy(c["xlT"][:, :, bass.ds((BLK * i + j) * P, P)],
                                   bank[4 + j % 4][:, 0:D].rearrange("p (h n) -> p h n", h=H)).then_inc(xTc_s, 1)

            turns(act, NB, block_turn)
            act.wait_ge(fmv_s, H)
            nc.scalar.activation(fsd[:], fmv[:, :, 1], ACT.Sqrt, bias=c["eps"][:]).then_inc(fsd_s, 1)
            act.wait_ge(w_in, 13 * 16)

        @block.tensor
        def _(pe):
            pe.wait_ge(consts, 2)
            pe.wait_ge(wn_s, 2)
            for ch in range(EC):
                if ch >= 2:
                    pe.wait_ge(edge_c, ch - 1)
                for k, v in enumerate((srcf, rel, iwn, own)):
                    last = nc.tensor.transpose(bank[ch % 2][:, k * P:(k + 1) * P], v[:, ch, :], c["ident"][:])
                last.then_inc(edge_T, 1)
            for ch in range(EC):
                last = nc.tensor.transpose(bank[2 + ch // 4][0:1, (ch % 4) * P:(ch % 4 + 1) * P], least[:, ch:ch + 1], c["ident"][:])
            last.then_inc(base_T, 1)
            pe.wait_ge(most_s, 1)
            pe.wait_ge(base_c, 2)
            nc.tensor.transpose(bank[2][0:1, 0:P], most[:], c["ident"][:]).then_inc(most_T, 1)

            def block_turn(i, first, last):
                for j in range(BLK):
                    pe.wait_ge(xn_s, BLK * i + j + 1)
                    reached(pe, xTc_s, BLK * i + j - 3)
                    for h in range(H):
                        mm = nc.tensor.transpose(bank[4 + j % 4][:, h * P:(h + 1) * P], XN[:, j, h * P:(h + 1) * P], c["ident"][:])
                    mm.then_inc(xT_s, 1)

            turns(pe, NB, block_turn)

        @block.vector
        def _(dve):
            nc.vector.memset(X[:, NT - 1, :], 0.0).then_inc(tail_z, 1)
            dve.wait_ge(e_in, 12 * 16)
            nc.vector.tensor_copy(srcf, rows[:, 0]).then_inc(idx_f, 1)
            nc.vector.tensor_copy(dstf, rows[:, 1]).then_inc(idx_f, 1)
            dve.wait_ge(idx_f, 2)
            nc.vector.tensor_reduce(least[:], dstf, AX.X, ALU.min).then_inc(lst, 1)
            dve.wait_ge(lst, 1)
            nc.vector.tensor_tensor(rel, dstf, least[:].unsqueeze(2).to_broadcast([P, EC, P]), ALU.subtract).then_inc(rel_s, 1)
            dve.wait_ge(rel_s, 1)
            nc.vector.tensor_scalar(near, rel, float(P), None, ALU.is_lt).then_inc(near_s, 1)
            nc.vector.tensor_reduce(most[:], rel, AX.XY, ALU.max).then_inc(most_s, 1)
            dve.wait_ge(near_s, 1)
            nc.vector.tensor_tensor(iwn, wrow[:, 0], near, ALU.mult).then_inc(wn_s, 1)
            nc.vector.tensor_tensor(own, wrow[:, 1], near, ALU.mult).then_inc(wn_s, 1)
            dve.wait_ge(wn_s, 2)
            nc.vector.tensor_tensor(iwf, wrow[:, 0], iwn, ALU.subtract).then_inc(wf_s, 1)
            nc.vector.tensor_tensor(owf, wrow[:, 1], own, ALU.subtract).then_inc(wf_s, 1)
            dve.wait_ge(most_T, 1)
            nc.vector.tensor_reduce(mostr[:], bank[2][0:1, 0:P], AX.X, ALU.max).then_inc(most_r, 1)
            dve.wait_ge(most_r, 1)
            nc.vector.tensor_scalar(c["far"][:], mostr[:], float(P), None, ALU.is_ge).then_inc(far_s, 1)

            def block_turn(i, first, last):
                if not first:
                    dve.wait_ge(xn_s, BLK * i)
                for j in range(BLK):
                    nc.vector.bn_stats(stats[:, j, :], tile_at(X, BLK * i + j)).then_inc(st_s, 1)
                dve.wait_ge(st_s, BLK * i + BLK)
                dve.sem_inc(held, 1)
                for j in range(BLK):
                    mm = nc.vector.bn_aggr(mv[:, j, :], stats[:, j, :])
                mm.then_inc(mv_s, 1)
                dve.wait_ge(sd_s, i + 1)
                nc.vector.reciprocal(rstd[:], sd[:]).then_inc(rs_s, 1)
                dve.wait_ge(rs_s, i + 1)
                for j in range(BLK):
                    if not first:
                        dve.wait_ge(xT_s, BLK * i + j - BLK + 1)
                    nc.vector.tensor_scalar(XN[:, j, :], tile_at(X, BLK * i + j),
                                            mv[:, j, 0:1], rstd[:, j:j + 1], ALU.subtract, ALU.mult).then_inc(xn_s, 1)

            for b in range(NB):
                dve.wait_ge(x_in[b], 16)
            dve.wait_ge(tail_in, 16)
            turns(dve, NB, block_turn)
            dve.wait_ge(xTc_s, NT)
            pieces = [(n, min(n + 512, N)) for n in range(0, N, 512)]
            for h in range(H):
                for k, (n0, n1) in enumerate(pieces):
                    nc.vector.bn_stats(fstat[:, h, k, :], c["xlT"][:, h, n0:n1]).then_inc(fst, 1)
            dve.wait_ge(fst, H * len(pieces))
            for h in range(H):
                nc.vector.bn_aggr(fmv[:, h, :], fstat[:, h, 0:len(pieces), :].rearrange("p k s -> p (k s)")).then_inc(fmv_s, 1)
            dve.wait_ge(fsd_s, 1)
            nc.vector.reciprocal(frs[:], fsd[:]).then_inc(frs_s, 1)
            dve.wait_ge(frs_s, 1)
            dve.wait_ge(w_in, 13 * 16)
            nc.vector.tensor_tensor(c["scale"][:], frs[:], c["gamma"][:], ALU.mult).then_inc(fsc, 1)
            dve.wait_ge(fsc, 1)
            nc.vector.tensor_tensor(fms[:], fmv[:, :, 0], c["scale"][:], ALU.mult).then_inc(fms_s, 1)
            dve.wait_ge(fms_s, 1)
            nc.vector.tensor_tensor(c["shift"][:], c["beta"][:], fms[:], ALU.subtract).then_inc(fsc, 1)


def transform_nodes(nc, c, bank, a, dram):
    with ExitStack() as ctx:
        def sb(name, shape, dt=F32):
            return ctx.enter_context(nc.sbuf_tensor(name, shape, dt))

        def sem(name):
            return ctx.enter_context(nc.semaphore(name))

        hT = sb("hT", [P, BLK, H, P])
        F = sb("F", [P, BLK, 2 * D])
        bio = sb("bio", [P, 2 * D])
        b_in = sem("b_in")
        h_s = sem("h_s")
        mm_s = sem("mm_s")
        f_s = sem("f_s")
        out_in = [sem(f"out_in{j}") for j in range(BLK)]
        out_out = [sem(f"out_out{j}") for j in range(BLK)]
        acc_z = sem("acc_z")
        z_out = sem("z_out")
        we_in = sem("we_in")
        block = ctx.enter_context(nc.Block())

        @block.gpsimd
        def _(pool):
            for n in range(3):
                pool.dma_start(c["we"][:, n], a[f"L0_ffn_expert_w{n + 1}"].rearrange("e (k p) n -> p e k n", p=P)).then_inc(we_in, 16)
            acc = c["accT"][:].rearrange("p h n -> p (h n)")
            nc.gpsimd.memset(acc, 0.0).then_inc(acc_z, 1)
            pool.wait_ge(acc_z, 1)
            for n in ("T0", "T1"):
                pool.dma_start(dram[n].rearrange("(p r) d -> p (r d)", p=P), acc).then_inc(z_out, 16)
            pool.dma_start(dram["x1"][SPARE:ROWS], acc[:, 0:D]).then_inc(z_out, 16)
            pool.dma_start(dram["Fin"][NP:ROWS], acc[:, 0:D]).then_inc(z_out, 16)
            pool.dma_start(dram["Fout"][NP:ROWS], acc[:, 0:D]).then_inc(z_out, 16)
            pool.wait_ge(z_out, 80)
            pool.wait_ge(we_in, 48)

        def node_turns(eng, step):
            def body(i, first, last):
                for j in range(BLK):
                    step(i, j, BLK * i + j, first)
            turns(eng, NB, body)

        @block.scalar
        def _(act):
            def step(i, j, t, first):
                reached(act, mm_s, t - BLK + 1)
                for h in range(H):
                    mm = nc.scalar.activation(hT[:, j, h, :], c["xlT"][:, h, bass.ds(t * P, P)], ACT.Identity,
                                              bias=c["shift"][:, h:h + 1], scale=c["scale"][:, h:h + 1])
                mm.then_inc(h_s, 1)
            node_turns(act, step)

        @block.tensor
        def _(pe):
            def step(i, j, t, first):
                pe.wait_ge(h_s, t + 1)
                reached(pe, f_s, t - BLK + 1)
                for h in range(H):
                    mm = nc.tensor.matmul(bank[j][:], hT[:, j, h, :], c["wio"][:, h, :], start=(h == 0), stop=(h == H - 1))
                mm.then_inc(mm_s, 1)
            node_turns(pe, step)

        @block.vector
        def _(dve):
            dve.wait_ge(b_in, 32)

            def step(i, j, t, first):
                dve.wait_ge(mm_s, t + 1)
                if not first:
                    dve.wait_ge(out_in[j], 16 * i)
                    dve.wait_ge(out_out[j], 16 * i)
                nc.vector.tensor_tensor(F[:, j, :], bank[j][:], bio[:], ALU.add).then_inc(f_s, 1)
            node_turns(dve, step)

        @block.sync
        def _(sp):
            for k, name in enumerate(("L0_gnn_b_in", "L0_gnn_b_out")):
                sp.dma_start(bio[:, k * D:(k + 1) * D], a[name].rearrange("(a d) -> a d", a=1).partition_broadcast(P)).then_inc(b_in, 16)

            def step(i, j, t, first):
                sp.wait_ge(f_s, t + 1)
                sp.dma_start(dram["Fin"][bass.ds(t * P, P), :], F[:, j, 0:D]).then_inc(out_in[j], 16)
                sp.dma_start(dram["Fout"][bass.ds(t * P, P), :], F[:, j, D:2 * D]).then_inc(out_out[j], 16)
            node_turns(sp, step)
            for j in range(BLK):
                sp.wait_ge(out_in[j], 16 * NB)
                sp.wait_ge(out_out[j], 16 * NB)


def sum_over_edges(nc, c, bank, a, dram):
    with ExitStack() as ctx:
        def sb(name, shape, dt=F32):
            return ctx.enter_context(nc.sbuf_tensor(name, shape, dt))

        def sem(name):
            return ctx.enter_context(nc.semaphore(name))

        stage = sb("stage", [P, 2, QUAD, 4])
        gsrc = sb("gsrc", [P, 2, QUAD], I32)
        sdst = sb("sdst", [P, 2, QUAD], I32)
        seen = sb("seen", [P, 2, QUAD])
        moved = sb("moved", [P, 2, QUAD])
        G = sb("G", [P, BODY, D])
        W = sb("W", [P, QUAD, D])
        place_w = sb("place_w", [P, 2, P])
        place = sb("place", [P, 2, P])
        same = sb("same", [P, 2, P])
        cnt_junk = sb("cnt_junk", [P, 2, P])
        Ps = sb("Ps", [P, 2, P])
        O = sb("O", [P, BODY, D])

        stage_s = sem("stage_s")
        bc_s = sem("bc_s")
        place_s = sem("place_s")
        same_s = sem("same_s")
        a_s = sem("a_s")
        add_s = sem("add_s")
        p_s = sem("p_s")
        ps_s = sem("ps_s")
        o_s = sem("o_s")
        os_s = sem("os_s")
        held = sem("held3")
        cl_s = sem("cl_s")
        sd_s = sem("sd_s")
        g_in = [sem(f"g_in{j}") for j in range(BODY)]
        w_in = [sem(f"w_in{j}") for j in range(QUAD)]
        t_out = [sem(f"t_out{j}") for j in range(2)]
        block = ctx.enter_context(nc.Block())

        def edge_turns(eng, quad_step, tile_step):
            def body(i, first, last):
                for q in range(2):
                    quad_step(i, q, 2 * i + q, first and q == 0, last and q == 1)
                    for u in range(QUAD):
                        tile_step(i, q, u, BODY * i + QUAD * q + u, first, last)
            turns(eng, TURNS, body, peel_last=True)

        @block.sync
        def _(sp):
            def tile_step(i, q, u, t, first, last):
                reached(sp, o_s, t - QUAD + 1)
                base = sp.value_load(c["base"][0:1, bass.ds(t, 1)], min_val=0, max_val=N - 1)
                sp.dma_start(W[:, u, :], dram["Fout"][bass.ds(base, P), :]).then_inc(w_in[u], 16)
            edge_turns(sp, lambda *x: None, tile_step)

        @block.gpsimd
        def _(pool):
            def gather(j):
                pool.indirect_dma_start(G[:, j, :], None, dram["Fin"],
                                        bass.IndirectOffsetOnAxis(ap=gsrc[:, j // QUAD, j % QUAD:j % QUAD + 1], axis=0)
                                        ).then_inc(g_in[j], 16)

            def scatter(j, t):
                pool.wait_ge(os_s, t + 1)
                reached(pool, t_out[j % 2], 8 * (t - j % 2))
                pool.sem_inc(held, 1)
                pool.indirect_dma_start(dram[f"T{j % 2}"],
                                        bass.IndirectOffsetOnAxis(ap=sdst[:, j // QUAD, j % QUAD:j % QUAD + 1], axis=0),
                                        O[:, j, :], None, compute_op=ALU.add).then_inc(t_out[j % 2], 16)

            def quad_step(i, q, Q, first, last):
                if not last:
                    pool.wait_ge(stage_s, Q + 2)
                if not first:
                    pool.wait_ge(sd_s, Q)

            def tile_step(i, q, u, t, first, last):
                if not (last and q == 1):
                    reached(pool, a_s, t - QUAD + 1)
                    pool.sem_inc(held, 1)
                    gather(QUAD * (1 - q) + u)
                if not (first and q == 0):
                    scatter(QUAD * (1 - q) + u, t - QUAD)

            pool.wait_ge(stage_s, 1)
            for u in range(QUAD):
                gather(u)
            edge_turns(pool, quad_step, tile_step)
            pool.wait_ge(sd_s, TILES // QUAD)
            for u in range(QUAD):
                scatter(QUAD + u, TILES - QUAD + u)
            for j in range(2):
                pool.wait_ge(t_out[j], 16 * (TILES // 2))

        @block.scalar
        def _(act):
            def stage_quad(Q, q):
                nc.scalar.copy(stage[:, q], c["col"][:, bass.ds(QUAD * Q, QUAD), :])
                nc.scalar.copy(gsrc[:, q], c["col"][:, bass.ds(QUAD * Q, QUAD), 0:1].rearrange("p t a -> p (t a)")).then_inc(stage_s, 1)

            def quad_step(i, q, Q, first, last):
                if last:
                    return
                if not first:
                    act.wait_ge(same_s, QUAD * Q)
                    act.wait_ge(bc_s, QUAD * Q)
                    act.wait_ge(sd_s, Q)
                    for u in range(QUAD):
                        reached(act, g_in[QUAD * (1 - q) + u], 8 * (Q + q))
                stage_quad(Q + 1, 1 - q)

            def rows_out(j, t):
                act.wait_ge(o_s, t + 1)
                reached(act, t_out[j % 2], 8 * (t - 6 - j % 2))
                nc.scalar.copy(O[:, j, :], bank[6 + j % 2][:, 0:D]).then_inc(os_s, 1)

            def tile_step(i, q, u, t, first, last):
                act.wait_ge(p_s, t + 1)
                reached(act, o_s, t - 1)
                nc.scalar.copy(Ps[:, u % 2, :], bank[4 + u % 2][:, 0:P]).then_inc(ps_s, 1)
                if not (first and q == 0 and u == 0):
                    rows_out((QUAD * q + u - 1) % BODY, t - 1)

            stage_quad(0, 0)
            edge_turns(act, quad_step, tile_step)
            rows_out(BODY - 1, TILES - 1)

        @block.tensor
        def _(pe):
            def spread(q, Q):
                pe.wait_ge(stage_s, Q + 1)
                reached(pe, same_s, QUAD * (Q - 1))
                for u in range(QUAD):
                    nc.tensor.transpose(bank[q][:, u * P:(u + 1) * P], stage[:, q, u, 0:1].to_broadcast([P, P]),
                                        c["ident"][:]).then_inc(bc_s, 1)

            def quad_step(i, q, Q, first, last):
                if not last:
                    spread(1 - q, Q + 1)

            def out_rows(j, t):
                pe.wait_ge(ps_s, t + 1)
                pe.wait_ge(w_in[j % QUAD], 4 * (t - j % QUAD) + 16)
                reached(pe, os_s, t - 1)
                nc.tensor.matmul(bank[6 + j % 2][:, 0:D], Ps[:, j % 2, :], W[:, j % QUAD, :], start=True, stop=True).then_inc(o_s, 1)

            def tile_step(i, q, u, t, first, last):
                j = QUAD * q + u
                pe.wait_ge(place_s, t + 1)
                pe.wait_ge(g_in[j], 2 * (t - j) + 16)
                reached(pe, add_s, t - 1)
                for h in range(H):
                    mm = nc.tensor.matmul(bank[2 + j % 2][:, h * P:(h + 1) * P], G[:, j, h * P:(h + 1) * P],
                                          place_w[:, j % 2, :], start=True, stop=True)
                mm.then_inc(a_s, 1)
                pe.wait_ge(same_s, t + 1)
                reached(pe, ps_s, t - 1)
                nc.tensor.matmul(bank[4 + j % 2][:, 0:P], place[:, j % 2, :], same[:, j % 2, :], start=True, stop=True).then_inc(p_s, 1)
                if not (first and j == 0):
                    out_rows((j - 1) % BODY, t - 1)

            spread(0, 0)
            edge_turns(pe, quad_step, tile_step)
            out_rows(BODY - 1, TILES - 1)

        @block.vector
        def _(dve):
            def quad_step(i, q, Q, first, last):
                dve.wait_ge(stage_s, Q + 1)

            def add_sums(j, t):
                dve.wait_ge(a_s, t + 1)
                reached(dve, add_s, t)
                base = dve.value_load(c["base"][0:1, bass.ds(t, 1)], min_val=0, max_val=N - 1)
                at = c["accT"][:, :, bass.ds(base, P)]
                nc.vector.tensor_tensor(at, bank[2 + j % 2][:, 0:D].rearrange("p (h n) -> p h n", h=H), at, ALU.add).then_inc(add_s, 1)

            def tile_step(i, q, u, t, first, last):
                j = QUAD * q + u
                s = stage[:, q, u]
                reached(dve, p_s, t - 1)
                nc.vector.tensor_scalar(place_w[:, j % 2, :], c["iota"][:], s[:, 1:2], s[:, 2:3], ALU.is_equal, ALU.mult)
                nc.vector.tensor_scalar(place[:, j % 2, :], c["iota"][:], s[:, 1:2], None, ALU.is_equal).then_inc(place_s, 1)
                if u == 0:
                    dve.wait_ge(bc_s, QUAD * (2 * i + q + 1))
                srcs = bank[q][:, u * P:(u + 1) * P]
                nc.vector.tensor_scalar(same[:, j % 2, :], srcs, s[:, 0:1], s[:, 3:4], ALU.is_equal, ALU.mult)
                nc.vector.scalar_tensor_tensor(out=cnt_junk[:, j % 2, :], in0=srcs, scalar=s[:, 0:1], in1=c["below"][:],
                                               op0=ALU.is_equal, op1=ALU.mult, accum_out=seen[:, q, u:u + 1]).then_inc(same_s, 1)
                if not (first and j == 0):
                    add_sums((j - 1) % BODY, t - 1)
                if u == QUAD - 1:
                    Q = 2 * i + q
                    dve.wait_ge(same_s, t + 1)
                    for k in range(2):
                        reached(dve, t_out[k], 16 * 2 * (Q - 1))
                    nc.vector.scalar_tensor_tensor(out=moved[:, q], in0=seen[:, q], scalar=1.0, in1=c["spare"][:],
                                                   op0=ALU.min, op1=ALU.mult).then_inc(cl_s, 1)
                    dve.wait_ge(cl_s, Q + 1)
                    nc.vector.tensor_tensor(sdst[:, q], moved[:, q], stage[:, q, :, 0:1].rearrange("p t a -> p (t a)"),
                                            ALU.max).then_inc(sd_s, 1)

            edge_turns(dve, quad_step, tile_step)
            add_sums(BODY - 1, TILES - 1)


def sum_far_edges(nc, c, bank, dram):
    with ExitStack() as ctx:
        def sb(name, shape, dt=F32):
            return ctx.enter_context(nc.sbuf_tensor(name, shape, dt))

        def sem(name):
            return ctx.enter_context(nc.semaphore(name))

        edge = sb("far_edge", [P, 4])
        gidx = sb("far_gidx", [P, 2], I32)
        sidx = sb("far_sidx", [P, 2], I32)
        G = sb("far_G", [P, 2, D])
        O = sb("far_O", [P, 2, D])
        same = sb("far_same", [P, 2, P])
        seen = sb("far_seen", [P, 2])
        junk = sb("far_junk", [P, P])
        moved = sb("far_moved", [P, 2])
        e_in = sem("far_e_in")
        gidx_s = sem("far_gidx_s")
        g_in = [sem(f"far_g_in{k}") for k in range(2)]
        bc_s = sem("far_bc_s")
        same_s = sem("far_same_s")
        mm_s = sem("far_mm_s")
        o_s = sem("far_o_s")
        moved_s = sem("far_moved_s")
        sidx_s = sem("far_sidx_s")
        t_out = [sem(f"far_t_out{k}") for k in range(2)]
        held = sem("far_held")
        z_s = sem("far_z_s")
        z_out = sem("far_z_out")
        f_in = sem("far_f_in")
        fT_s = sem("far_fT_s")
        fa_s = sem("far_fa_s")
        block = ctx.enter_context(nc.Block())

        def if_far(eng, body, fold, before=lambda: None):
            far = eng.value_load(c["far"][0:1, 0:1], min_val=0, max_val=1)
            with eng.If(far):
                before()
                body(0, True)
                with eng.Fori(1, ET) as t:
                    body(t, False)
                fold(0)
                with eng.Fori(1, NT) as t:
                    fold(t)
            with eng.Else():
                eng.nop()

        @block.sync
        def _(sp):
            def tile_step(t, first):
                reached(sp, t_out[0], 16 * t)
                reached(sp, t_out[1], 16 * t)
                sp.dma_start(edge[:].unsqueeze(2), dram["slow"][:, bass.ds(t * P, P)].rearrange("k (p a) -> p k a", a=1)).then_inc(e_in, 16)
            def fold(t):
                reached(sp, fT_s, t)
                if isinstance(t, int):
                    for k in range(2):
                        sp.wait_ge(t_out[k], 16 * ET)
                sp.dma_start(G[:, 0, :], dram["TA"][bass.ds(t * P, P), :]).then_inc(f_in, 16)
            if_far(sp, tile_step, fold)

        @block.vector
        def _(dve):
            def tile_step(t, first):
                dve.wait_ge(e_in, 16 * t + 16)
                nc.vector.tensor_copy(gidx[:], edge[:, 0:2]).then_inc(gidx_s, 1)
                dve.wait_ge(bc_s, 2 * t + 2)
                for k in range(2):
                    row = bank[k][:, 0:P]
                    nc.vector.tensor_scalar(same[:, k, :], row, edge[:, 1 - k:2 - k], edge[:, 2 + k:3 + k], ALU.is_equal, ALU.mult)
                    nc.vector.scalar_tensor_tensor(out=junk[:], in0=row, scalar=edge[:, 1 - k:2 - k], in1=c["below"][:],
                                                   op0=ALU.is_equal, op1=ALU.mult, accum_out=seen[:, k:k + 1]).then_inc(same_s, 1)
                    dve.wait_ge(same_s, 2 * t + 1 + k)
                nc.vector.scalar_tensor_tensor(out=moved[:], in0=seen[:], scalar=1.0, in1=c["spare"][:, 0:2],
                                               op0=ALU.min, op1=ALU.mult).then_inc(moved_s, 1)
                dve.wait_ge(moved_s, t + 1)
                for k in range(2):
                    nc.vector.tensor_tensor(sidx[:, k:k + 1], moved[:, k:k + 1], edge[:, 1 - k:2 - k], ALU.max).then_inc(sidx_s, 1)
            def fold(t):
                dve.wait_ge(fT_s, t + 1)
                at = c["accT"][:, :, bass.ds(t * P, P)]
                nc.vector.tensor_tensor(at, bank[4][:, 0:D].rearrange("p (h n) -> p h n", h=H), at, ALU.add).then_inc(fa_s, 1)
            if_far(dve, tile_step, fold)

        @block.gpsimd
        def _(pool):
            def tile_step(t, first):
                pool.wait_ge(gidx_s, t + 1)
                pool.sem_inc(held, 1)
                for k, table in enumerate(("Fin", "Fout")):
                    pool.indirect_dma_start(G[:, k, :], None, dram[table],
                                            bass.IndirectOffsetOnAxis(ap=gidx[:, k:k + 1], axis=0)).then_inc(g_in[k], 16)
                pool.wait_ge(sidx_s, 2 * t + 2)
                pool.wait_ge(o_s, 2 * t + 2)
                pool.sem_inc(held, 1)
                for k, table in enumerate(("TA", "T0")):
                    pool.indirect_dma_start(dram[table], bass.IndirectOffsetOnAxis(ap=sidx[:, k:k + 1], axis=0),
                                            O[:, k, :], None, compute_op=ALU.add).then_inc(t_out[k], 16)
                for k in range(2):
                    pool.wait_ge(t_out[k], 16 * t + 16)
            def clear():
                nc.gpsimd.memset(O[:], 0.0).then_inc(z_s, 1)
                pool.wait_ge(z_s, 1)
                for n in range(0, ROWS, 2 * P):
                    pool.dma_start(dram["TA"][n:n + 2 * P].rearrange("(p r) d -> p (r d)", p=P),
                                   O[:].rearrange("p r d -> p (r d)")).then_inc(z_out, 16)
                pool.wait_ge(z_out, 16 * ROWS // (2 * P))
                pool.sem_inc(z_s, 1)
            if_far(pool, tile_step, lambda t: pool.wait_ge(fa_s, t + 1), clear)

        @block.tensor
        def _(pe):
            def tile_step(t, first):
                pe.wait_ge(e_in, 16 * t + 16)
                for k in range(2):
                    nc.tensor.transpose(bank[k][:, 0:P], edge[:, 1 - k:2 - k].to_broadcast([P, P]), c["ident"][:]).then_inc(bc_s, 1)
                pe.wait_ge(same_s, 2 * t + 2)
                for k in range(2):
                    pe.wait_ge(g_in[k], 16 * t + 16)
                    nc.tensor.matmul(bank[2 + k][:, 0:D], same[:, k, :], G[:, k, :], start=True, stop=True).then_inc(mm_s, 1)
            def fold(t):
                pe.wait_ge(f_in, 16 * t + 16)
                reached(pe, fa_s, t)
                for h in range(H):
                    mm = nc.tensor.transpose(bank[4][:, h * P:(h + 1) * P], G[:, 0, h * P:(h + 1) * P], c["ident"][:])
                mm.then_inc(fT_s, 1)
            if_far(pe, tile_step, fold)

        @block.scalar
        def _(act):
            def tile_step(t, first):
                for k in range(2):
                    act.wait_ge(mm_s, 2 * t + 1 + k)
                    nc.scalar.copy(O[:, k, :], bank[2 + k][:, 0:D]).then_inc(o_s, 1)
            if_far(act, tile_step, lambda t: act.wait_ge(fa_s, t + 1), lambda: act.wait_ge(z_s, 2))


def start_of(g):
    return min(GN * g, N - GN) if isinstance(g, int) else GN * g


def group_turns(eng, turn):
    turn(0, 0)
    with eng.Fori(0, (GROUPS - 4) // 2) as i:
        turn(2 * i + 1, 1)
        turn(2 * i + 2, 0)
    for g in range(GROUPS - 3, GROUPS + 1):
        turn(g, g % 2)


def has(g, n):
    return not isinstance(g, int) or 0 <= g + n < GROUPS


def gate_nodes(nc, c, bank, a, dram):
    with ExitStack() as ctx:
        def sb(name, shape, dt=F32):
            return ctx.enter_context(nc.sbuf_tensor(name, shape, dt))

        def sem(name):
            return ctx.enter_context(nc.semaphore(name))

        T3 = [GP, ST, NE]
        T4 = [GP, ST, NE, NE]
        xg = sb("xg", [GP, 2, ST, D])
        tg = sb("tg", [GP, 2, ST, D])
        aT = sb("aT", [P, 2, H, GN])
        hT = sb("hTg", [P, 2, H, GN])
        gate = sb("gate", [P, H, GN])
        new = sb("new", [P, H, GN])
        yT = sb("yT", [P, H, GN])
        rhT = sb("rhT", [P, GN])
        pay = sb("pay", [GP, 2, ST, ROWX])
        stats = sb("lstats", [GP, ST, 6])
        mv = sb("lmv", [GP, ST, 2])
        sd = sb("lsd", [GP, ST])
        rstd = sb("lrstd", [GP, ST])
        lg = sb("lg", T3)
        lg2 = sb("lg2", T3)
        pexp = sb("pexp", T3)
        pr = sb("pr", T3)
        m1 = sb("m1", [GP, ST])
        s1 = sb("s1", [GP, ST])
        r1 = sb("r1", [GP, ST])
        m2 = sb("m2", [GP, ST])
        s2 = sb("s2", [GP, ST])
        r2 = sb("r2", [GP, ST])
        pd = sb("pd", T3)
        pex = sb("pex", T3)
        pse = sb("pse", T3)
        gt = sb("gt", T4)
        eq = sb("eq", T4)
        rank = sb("rank", T3)
        sel = sb("sel", T3, BF16)
        one = sb("one", [GP, 2, ST, NE])
        tmp = sb("tmp", [GP, 2, ST, NE])
        tmp2 = sb("tmp2", [GP, 2, ST, NE])
        slot = sb("slot", T3)
        slotf = sb("slotf", [GP, 2, ST])
        sloti = sb("sloti", [GP, 2, ST], I32)
        wsum = sb("wsum", [GP, 2, ST])
        tri = sb("tri", [GP, GP], BF16)
        ones = sb("ones", [GP, P], BF16)
        node = sb("node", [GP, ST])
        fresh = sb("fresh", [GP, ST])

        held = sem("held4")
        k_s = sem("k_s")
        k2_s = sem("k2_s")
        x_in = [sem(f"gx_in{q}") for q in range(2)]
        t_in = sem("gt_in")
        ts_s = sem("ts_s")
        tT_s = sem("tT_s")
        ao_s = sem("ao_s")
        h_s = sem("gh_s")
        g_s = sem("g_s")
        act_s = sem("act_s")
        v = sem("v")
        gnn_s = sem("gnn_s")
        gT_s = sem("gT_s")
        x1_s = sem("x1_s")
        x1_out = [sem(f"x1_out{q}") for q in range(2)]
        mv_s = sem("lmv_s")
        sd_s = sem("lsd_s")
        y_s = sem("y_s")
        y2_s = sem("y2_s")
        yT_s = sem("yT_s")
        yTc_s = sem("yTc_s")
        r_s = sem("r_s")
        rh_s = sem("rh_s")
        lg_s = sem("lg_s")
        l2_s = sem("l2_s")
        e1_s = sem("e1_s")
        pd_s = sem("pd_s")
        e2_s = sem("e2_s")
        sel_s = sem("sel_s")
        cum_s = sem("cum_s")
        pay_s = sem("pay_s")
        y_out = sem("y_out")
        fill_s = sem("fill_s")
        block = ctx.enter_context(nc.Block())

        def rows_of(t, s):
            return t[bass.ds(s, GN), :].rearrange("(j p) d -> p j d", p=GP)

        def three(col):
            return col.unsqueeze(2).to_broadcast(T3)

        @block.sync
        def _(sp):
            def load_tables(g):
                reached(sp, tT_s, H * g)
                for n in range(2):
                    sp.dma_start(tg[:, n], rows_of(dram[f"T{n}"], start_of(g))).then_inc(t_in, 16)

            def load_x(g, q):
                if not isinstance(g, int):
                    sp.wait_ge(x1_out[q], 8 * (g - q))
                    sp.sem_inc(held, 1)
                elif g >= 2:
                    sp.wait_ge(x1_out[q], 16 * (g // 2))
                reached(sp, y_s, ST * (g - 1))
                sp.dma_start(xg[:, q], rows_of(a["x"], start_of(g))).then_inc(x_in[q], 16)

            def stores(g, q):
                sp.wait_ge(x1_s, 2 * (g + 1))
                if isinstance(g, int) and g == GROUPS - 1:
                    sp.wait_ge(x1_out[1 - q], 16 * (GROUPS // 2))
                sp.dma_start(rows_of(dram["x1"], start_of(g)), xg[:, q]).then_inc(x1_out[q], 16)

            def turn(g, q):
                if has(g, 1):
                    load_tables(g + 1)
                if has(g, -1):
                    stores(g - 1, 1 - q)
                if has(g, 1):
                    load_x(g + 1, 1 - q)
            load_tables(0)
            load_x(0, 0)
            group_turns(sp, turn)
            for q in range(2):
                sp.wait_ge(x1_out[q], 16 * (GROUPS // 2))

        @block.gpsimd
        def _(pool):
            nc.gpsimd.memset(tri[:], 1.0).then_inc(k_s, 1)
            nc.gpsimd.memset(ones[:], 1.0).then_inc(k_s, 1)
            nc.gpsimd.memset(fresh[:], 1.0).then_inc(k_s, 1)
            nc.gpsimd.memset(c["count"][:], 0.0).then_inc(k_s, 1)
            nc.gpsimd.iota(node[:], pattern=[[GP, ST]], base=-GN, channel_multiplier=1, allow_small_or_imprecise_dtypes=True).then_inc(k_s, 1)
            nc.gpsimd.iota(c["region"][:], pattern=[[0, ST], [REG, NE]], base=0, channel_multiplier=0, allow_small_or_imprecise_dtypes=True).then_inc(k_s, 1)
            pool.wait_ge(k_s, 6)
            nc.gpsimd.affine_select(out=tri[:], in_=tri[:], compare_op=ALU.is_gt, fill=0.0, base=0,
                                    pattern=[[1, GP]], channel_multiplier=-1).then_inc(k2_s, 1)
            nc.gpsimd.affine_select(out=fresh[:], in_=fresh[:], compare_op=ALU.is_ge, fill=0.0, base=-(GROUPS * GN - N),
                                    pattern=[[GP, ST]], channel_multiplier=1).then_inc(k2_s, 1)

            def add_tables(g):
                pool.wait_ge(t_in, 32 * (g + 1))
                nc.gpsimd.tensor_tensor(tg[:, 0], tg[:, 0], tg[:, 1], ALU.add).then_inc(ts_s, 1)

            def scatters(g):
                pool.wait_ge(pay_s, g + 1)
                pool.sem_inc(held, 1)
                for k in range(2):
                    for j in range(ST):
                        pool.indirect_dma_start(dram["Y"], bass.IndirectOffsetOnAxis(ap=sloti[:, k, j:j + 1], axis=0),
                                                pay[:, k, j, :], None).then_inc(y_out, 16)

            def turn(g, q):
                if has(g, -1):
                    pool.wait_ge(y_s, ST * g)
                    pool.sem_inc(held, 1)
                    nc.gpsimd.tensor_copy(pay[:, 1, :, 0:D], pay[:, 0, :, 0:D]).then_inc(y2_s, 1)
                if has(g, 1):
                    add_tables(g + 1)
                if has(g, -1):
                    scatters(g - 1)
            add_tables(0)
            group_turns(pool, turn)
            pool.wait_ge(y_out, 16 * 2 * ST * GROUPS)

        @block.scalar
        def _(act):
            def head(g, q):
                reached(act, gnn_s, g - 1)
                for h in range(H):
                    nc.scalar.activation(hT[:, q, h, :], c["xlT"][:, h, bass.ds(start_of(g), GN)], ACT.Identity,
                                         bias=c["shift"][:, h:h + 1], scale=c["scale"][:, h:h + 1]).then_inc(h_s, 1)
                for h in range(H):
                    act.wait_ge(tT_s, H * g + 1 + h)
                    nc.scalar.copy(aT[:, q, h, :], bank[2 + h][:, 0:GN]).then_inc(ao_s, 1)

            def gates(g, m):
                act.wait_ge(g_s, 2 * H * g + m + 1)
                if m == 0:
                    reached(act, gnn_s, g)
                if m == H:
                    reached(act, gT_s, ST * g)
                nc.scalar.activation((gate if m < H else new)[:, m % H, :], bank[4 + m][:, 0:GN],
                                     ACT.Sigmoid if m < H else ACT.Tanh, bias=c["bx"][:, m:m + 1]).then_inc(act_s, 1)

            def turn(g, q):
                now, tail = has(g, 0), has(g, -1)
                if now:
                    gates(g, 0)
                if tail:
                    act.wait_ge(mv_s, g)
                    nc.scalar.activation(sd[:], mv[:, :, 1], ACT.Sqrt, bias=c["eps"][0:GP]).then_inc(sd_s, 1)
                if now:
                    gates(g, 1)
                if tail:
                    for h in range(H):
                        act.wait_ge(yT_s, H * (g - 1) + h + 1)
                        nc.scalar.copy(yT[:, h, :], bank[h][:, 0:GN]).then_inc(yTc_s, 1)
                if now:
                    gates(g, 2)
                if tail:
                    act.wait_ge(r_s, g)
                    nc.scalar.activation(rhT[:], bank[0][:, 0:GN], ACT.Relu, bias=c["br1"][:]).then_inc(rh_s, 1)
                if has(g, 1):
                    head(g + 1, 1 - q)
                if tail:
                    act.wait_ge(l2_s, g)
                    nc.scalar.activation(pexp[:], lg2[:], ACT.Exp).then_inc(e1_s, 1)
                    act.wait_ge(pd_s, g)
                    nc.scalar.activation(pex[:], pd[:], ACT.Exp).then_inc(e2_s, 1)
                if now:
                    gates(g, 3)
            head(0, 0)
            group_turns(act, turn)

        @block.tensor
        def _(pe):
            def tables(g):
                pe.wait_ge(ts_s, g + 1)
                for h in range(H):
                    for j in range(ST):
                        mm = nc.tensor.transpose(bank[2 + h][:, j * GP:(j + 1) * GP], tg[:, 0, j, h * P:(h + 1) * P],
                                                 c["ident"][0:GP, 0:GP])
                    mm.then_inc(tT_s, 1)

            def gates(g, q, m):
                o = bank[4 + m][:, 0:GN]
                if m == 0:
                    pe.wait_ge(h_s, H * (g + 1))
                    pe.wait_ge(ao_s, H * (g + 1))
                reached(pe, act_s, 2 * H * (g - 1) + m + 1)
                w, wh = c["wx"], c["wh"]
                for k in range(H):
                    nc.tensor.matmul(o, wh[:, k, m * P:(m + 1) * P], hT[:, q, k, :], start=(k == 0), stop=False)
                for k in range(H):
                    nc.tensor.matmul(o, w[:, k, m * P:(m + 1) * P], c["accT"][:, k, bass.ds(start_of(g), GN)], start=False, stop=False)
                for k in range(H):
                    mm = nc.tensor.matmul(o, w[:, H + k, m * P:(m + 1) * P], aT[:, q, k, :], start=False, stop=(k == H - 1))
                mm.then_inc(g_s, 1)

            def turn(g, q):
                now, tail = has(g, 0), has(g, -1)
                if now:
                    gates(g, q, 0)
                if tail:
                    pe.wait_ge(gnn_s, g)
                    reached(pe, yTc_s, H * (g - 1))
                    reached(pe, pay_s, g - 1)
                    for j in range(ST):
                        for h in range(H):
                            mm = nc.tensor.transpose(bank[j // 2][0:GP, (j % 2) * D + h * P:(j % 2) * D + (h + 1) * P],
                                                     new[:, h, j * GP:(j + 1) * GP], c["ident"][:])
                        mm.then_inc(gT_s, 1)
                if now:
                    gates(g, q, 1)
                if tail:
                    pe.wait_ge(x1_s, 2 * g)
                    pe.wait_ge(y_s, ST * g)
                    for h in range(H):
                        for j in range(ST):
                            mm = nc.tensor.transpose(bank[h][:, j * GP:(j + 1) * GP], pay[:, 0, j, h * P:(h + 1) * P], c["ident"][0:GP, 0:GP])
                        mm.then_inc(yT_s, 1)
                if now:
                    gates(g, q, 2)
                if tail:
                    pe.wait_ge(yTc_s, H * g)
                    for k in range(H):
                        mm = nc.tensor.matmul(bank[0][:, 0:GN], c["wr1"][:, k, :], yT[:, k, :], start=(k == 0), stop=(k == H - 1))
                    mm.then_inc(r_s, 1)
                if has(g, 1):
                    reached(pe, ao_s, H * g + H)
                    tables(g + 1)
                if tail:
                    pe.wait_ge(rh_s, g)
                    for j in range(ST):
                        mm = nc.tensor.matmul(bank[1][0:GP, j * NE:(j + 1) * NE], rhT[:, j * GP:(j + 1) * GP], c["wr2"][:], start=True, stop=True)
                    mm.then_inc(lg_s, 1)
                if now:
                    gates(g, q, 3)
                if tail:
                    pe.wait_ge(sel_s, g)
                    for j in range(ST):
                        for i in range(j + 1):
                            nc.tensor.matmul(bank[0][0:GP, j * NE:(j + 1) * NE], (tri if i == j else ones)[:, 0:GP], sel[:, i, :],
                                             start=(i == 0), stop=(i == j))
                    for i in range(ST):
                        mm = nc.tensor.matmul(bank[0][0:GP, ST * NE:(ST + 1) * NE], ones[:, 0:GP], sel[:, i, :], start=(i == 0), stop=(i == ST - 1))
                    mm.then_inc(cum_s, 1)
            pe.wait_ge(k2_s, 2)
            tables(0)
            group_turns(pe, turn)

        @block.vector
        def _(dve):
            OWN = 24
            region = c["region"][0:GP].rearrange("p (j e) -> p j e", e=NE)

            def tail(g, q):
                count = [0]

                def link(ins):
                    count[0] += 1
                    ins.then_inc(v, 1)
                    dve.wait_ge(v, OWN * g + count[0])

                last = isinstance(g, int) and g == GROUPS - 1
                dve.wait_ge(act_s, 2 * H * (g + 1))
                link(nc.vector.tensor_tensor(hT[:, q], hT[:, q], new[:], ALU.subtract))
                link(nc.vector.tensor_tensor(hT[:, q], hT[:, q], gate[:], ALU.mult))
                nc.vector.tensor_tensor(new[:], new[:], hT[:, q], ALU.add).then_inc(gnn_s, 1)
                if isinstance(g, int):
                    dve.wait_ge(x_in[q], 16 * (g // 2 + 1))
                else:
                    dve.wait_ge(x_in[q], 8 * (g - q) + 16)
                for j in range(0, ST, 2):
                    dve.wait_ge(gT_s, ST * g + j + 2)
                    x2 = xg[:, q, j:j + 2, :]
                    nc.vector.tensor_tensor(x2, x2, bank[j // 2][0:GP, :].rearrange("p (j d) -> p j d", j=2), ALU.add).then_inc(x1_s, 1)
                dve.wait_ge(x1_s, 2 * (g + 1))
                for j in range(ST):
                    mm = nc.vector.bn_stats(stats[:, j, :], xg[:, q, j, :])
                mm.then_inc(v, 1)
                count[0] += 1
                dve.wait_ge(v, OWN * g + count[0])
                dve.sem_inc(held, 1)
                for j in range(ST):
                    mm = nc.vector.bn_aggr(mv[:, j, :], stats[:, j, :])
                mm.then_inc(mv_s, 1)
                dve.wait_ge(sd_s, g + 1)
                link(nc.vector.reciprocal(rstd[:], sd[:]))
                reached(dve, y_out, 16 * 2 * ST * g)
                for j in range(ST):
                    nc.vector.tensor_scalar(pay[:, 0, j, 0:D], xg[:, q, j, :], mv[:, j, 0:1], rstd[:, j:j + 1], ALU.subtract, ALU.mult).then_inc(y_s, 1)
                dve.wait_ge(lg_s, g + 1)
                link(nc.vector.tensor_tensor(lg[:], bank[1][0:GP, 0:ST * NE].rearrange("p (j e) -> p j e", e=NE),
                                             c["br2"][0:GP, :].unsqueeze(1).to_broadcast(T3), ALU.add))
                link(nc.vector.tensor_reduce(m1[:], lg[:], AX.X, ALU.max))
                nc.vector.tensor_tensor(lg2[:], lg[:], three(m1[:]), ALU.subtract).then_inc(l2_s, 1)
                dve.wait_ge(e1_s, g + 1)
                link(nc.vector.tensor_reduce(s1[:], pexp[:], AX.X, ALU.add))
                link(nc.vector.reciprocal(r1[:], s1[:]))
                link(nc.vector.tensor_tensor(pr[:], pexp[:], three(r1[:]), ALU.mult))
                link(nc.vector.tensor_reduce(m2[:], pr[:], AX.X, ALU.max))
                nc.vector.tensor_tensor(pd[:], pr[:], three(m2[:]), ALU.subtract).then_inc(pd_s, 1)
                other = pr[:].unsqueeze(2).to_broadcast(T4)
                own = pr[:].unsqueeze(3).to_broadcast(T4)
                nc.vector.tensor_tensor(gt[:], other, own, ALU.is_gt)
                link(nc.vector.tensor_tensor(eq[:], other, own, ALU.is_equal))
                link(nc.vector.tensor_tensor(eq[:], eq[:], c["prior"][0:GP].unsqueeze(1).to_broadcast(T4), ALU.mult))
                link(nc.vector.tensor_tensor(gt[:], gt[:], eq[:], ALU.add))
                link(nc.vector.tensor_reduce(rank[:], gt[:], AX.X, ALU.add))
                nc.vector.tensor_scalar(sel[:], rank[:], 2.0, None, ALU.is_lt).then_inc(sel_s, 1)
                for k in range(2):
                    mm = nc.vector.tensor_scalar(one[:, k], rank[:], float(k), None, ALU.is_equal)
                link(mm)
                dve.wait_ge(e2_s, g + 1)
                link(nc.vector.tensor_tensor(tmp[:], one[:], pex[:].unsqueeze(1).to_broadcast([GP, 2, ST, NE]), ALU.mult))
                link(nc.vector.tensor_reduce(wsum[:], tmp[:], AX.X, ALU.add))
                link(nc.vector.tensor_tensor(s2[:], wsum[:, 0], wsum[:, 1], ALU.add))
                link(nc.vector.reciprocal(r2[:], s2[:]))
                if last:
                    link(nc.vector.tensor_tensor(r2[:], r2[:], fresh[:], ALU.mult))
                dve.wait_ge(cum_s, g + 1)
                link(nc.vector.tensor_tensor(slot[:], bank[0][0:GP, 0:ST * NE].rearrange("p (j e) -> p j e", e=NE), region, ALU.add))
                link(nc.vector.tensor_tensor(slot[:], slot[:], c["count"][0:GP, :].unsqueeze(1).to_broadcast(T3), ALU.add))
                nc.vector.tensor_tensor(c["count"][0:GP, :], c["count"][0:GP, :], bank[0][0:GP, ST * NE:(ST + 1) * NE], ALU.add)
                link(nc.vector.tensor_tensor(tmp2[:], one[:], slot[:].unsqueeze(1).to_broadcast([GP, 2, ST, NE]), ALU.mult))
                link(nc.vector.tensor_reduce(slotf[:], tmp2[:], AX.X, ALU.add))
                nc.vector.tensor_copy(sloti[:], slotf[:])
                dve.wait_ge(y2_s, g + 1)
                step = float(N - GN - GN * (GROUPS - 2)) if last else float(GN)
                if last:
                    aside = float(ROWS - (N - GN))
                    link(nc.vector.tensor_scalar(node[:], node[:], step + aside, None, ALU.add))
                    link(nc.vector.scalar_tensor_tensor(out=node[:], in0=fresh[:], scalar=-aside, in1=node[:], op0=ALU.mult, op1=ALU.add))
                else:
                    link(nc.vector.tensor_scalar(node[:], node[:], step, None, ALU.add))
                nc.vector.tensor_copy(pay[:, 0, :, D + 1], node[:])
                nc.vector.tensor_copy(pay[:, 1, :, D + 1], node[:])
                nc.vector.tensor_tensor(pay[:, 0, :, D], wsum[:, 0], r2[:], ALU.mult)
                nc.vector.tensor_tensor(pay[:, 1, :, D], wsum[:, 1], r2[:], ALU.mult).then_inc(pay_s, 1)
                assert last or count[0] == OWN, count

            dve.wait_ge(k2_s, 2)

            def turn(g, q):
                if has(g, -1):
                    tail(g - 1, 1 - q)
            group_turns(dve, turn)


def run_experts(nc, c, bank, a, dram, out):
    with ExitStack() as ctx:
        def sb(name, shape, dt=F32):
            return ctx.enter_context(nc.sbuf_tensor(name, shape, dt))

        def sem(name):
            return ctx.enter_context(nc.semaphore(name))

        S = STEPS
        tl = sb("tl", [P, NE])
        tli = sb("tli", [P, NE], I32)
        cnti = sb("cnti", [P, NE], I32)
        endm = sb("endm", [P, NE, NE])
        first = sb("first", [P, NE])
        end = sb("end", [P, NE])
        stepf = sb("stepf", [1, S])
        over = sb("over", [1, S, NE])
        jump = sb("jump", [1, S, NE])
        ex = sb("ex", [1, S])
        jm = sb("jm", [1, S])
        row = sb("row", [1, S])
        exi = sb("exi", [1, S], I32)
        rowi = sb("rowi", [1, S], I32)
        b3 = sb("b3", [P, NE, D])
        padt = sb("padt", [P, ROWX])
        yt = sb("yt", [P, 4, ROWX])
        pair = sb("pair", [P, 4, 2])
        yT = sb("yTe", [P, 2, H, P])
        z1 = sb("z1", [P, D])
        h1 = sb("h1", [P, H, P])
        z2 = sb("z2", [P, D])
        h2 = sb("h2", [P, H, P])
        z3 = sb("z3", [P, D])
        O = sb("Oe", [P, 4, D])
        oid = sb("oid", [P, 4], I32)

        p_s = sem("ep_s")
        v = sem("ev")
        tab_s = sem("tab_s")
        pad_out = sem("pad_out")
        b_in = sem("b_in")
        y_in = [sem(f"ey_in{n}") for n in range(4)]
        A_s = sem("A_s")
        Ac_s = sem("Ac_s")
        B_s = sem("B_s")
        Bc_s = sem("Bc_s")
        C_s = sem("C_s")
        Cc_s = sem("Cc_s")
        D_s = sem("D_s")
        Dc_s = sem("Dc_s")
        E_s = sem("E_s")
        Ec_s = sem("Ec_s")
        F_s = sem("F_s")
        Fz_s = sem("Fz_s")
        Fc_s = sem("Fc_s")
        held = sem("held5")
        o_out = sem("eo_out")
        out_s = sem("out_s")
        block = ctx.enter_context(nc.Block())

        def step_turns(eng, turn):
            head, loops = 6, (S - 3 - 6) // 4
            for s in range(head):
                turn(s, s % 4, lambda k: expert(eng, s - k))
            with eng.Fori(0, loops) as i:
                of = several(eng, 4 * i + head - 2)
                for n in range(4):
                    turn(4 * i + head + n, (head + n) % 4, lambda k: of[n + 2 - k])
            for s in range(head + 4 * loops, S + 2):
                turn(s, s % 4, lambda k: expert(eng, s - k))

        def several(eng, s):
            if eng.engine in (mybir.EngineType.Pool, mybir.EngineType.SP):
                return None
            return nc.values_load_multi_w_load_instructions(exi[0:1, bass.ds(s, 6)], engines=(eng.engine,),
                                                            min_val=0, max_val=NE - 1)[1]

        def live(s):
            return not isinstance(s, int) or 0 <= s < S

        def expert(eng, s):
            return eng.value_load(exi[0:1, bass.ds(s, 1)], min_val=0, max_val=NE - 1)

        @block.gpsimd
        def _(pool):
            nc.gpsimd.memset(padt[:], 0.0).then_inc(p_s, 1)
            nc.gpsimd.iota(stepf[:], pattern=[[1, S]], base=0, channel_multiplier=0, allow_small_or_imprecise_dtypes=True).then_inc(p_s, 1)
            pool.wait_ge(p_s, 2)
            nc.gpsimd.iota(padt[:, D + 1:D + 2], pattern=[[0, 1]], base=SPARE, channel_multiplier=1, allow_small_or_imprecise_dtypes=True).then_inc(p_s, 1)

            def turn(s, n, experts):
                if live(s - 2):
                    pool.wait_ge(Fc_s, s - 1)
                    reached(pool, o_out, 16 * (s - 2))
                    pool.sem_inc(held, 1)
                    m = (n + 2) % 4
                    pool.indirect_dma_start(dram["x1"], bass.IndirectOffsetOnAxis(ap=oid[:, m:m + 1], axis=0),
                                            O[:, m, :], None, compute_op=ALU.add).then_inc(o_out, 16)
            step_turns(pool, turn)

        @block.sync
        def _(sp):
            sp.dma_start(b3[:].rearrange("p e d -> p (e d)"), a["L0_ffn_expert_b3"].rearrange("(a e) d -> a (e d)", a=1).partition_broadcast(P)).then_inc(b_in, 16)
            sp.wait_ge(p_s, 3)
            for n in (SPARE, ROWS):
                sp.dma_start(dram["x1"][n:n + P, :], padt[:, 0:D]).then_inc(pad_out, 16)
            sp.dma_start(dram["Y"][NE * REG:NE * REG + P, :], padt[:]).then_inc(pad_out, 16)
            sp.wait_ge(tab_s, 1)
            for e in range(NE):
                used = sp.value_load(cnti[0:1, e:e + 1], min_val=0, max_val=GROUPS * GN)
                sp.dma_start(dram["Y"][bass.ds(used + e * REG, P), :], padt[:]).then_inc(pad_out, 16)
            sp.wait_ge(pad_out, 16 * (NE + 3))

            def load(s, m):
                reached(sp, Ac_s, s - 3)
                r = sp.value_load(rowi[0:1, bass.ds(s, 1)], min_val=0, max_val=NE * REG)
                sp.dma_start(yt[:, m, :], dram["Y"][bass.ds(r, P), :]).then_inc(y_in[m], 16)
            for s in range(3):
                load(s, s)

            def turn(s, n, experts):
                if live(s + 3):
                    load(s + 3, (n + 3) % 4)
            step_turns(sp, turn)
            sp.wait_ge(o_out, 16 * S)
            sp.dma_start(out.rearrange("n d -> (n d)").rearrange("(p f) -> p f", p=P),
                         dram["x1"][0:N, :].rearrange("n d -> (n d)").rearrange("(p f) -> p f", p=P)).then_inc(out_s, 16)
            sp.wait_ge(out_s, 16)

        @block.tensor
        def _(pe):
            def transposes(b, src, s, sem_out):
                for h in range(H):
                    mm = nc.tensor.transpose(bank[b][:, h * P:(h + 1) * P], src[:, h * P:(h + 1) * P], c["ident"][:])
                mm.then_inc(sem_out, 1)

            def layer(b, n, src, e, sem_out):
                for k in range(H):
                    w = c["we"][:, n].rearrange("p e h d -> p e (h d)")[:, bass.ds(e, 1), k * D:(k + 1) * D].rearrange("p a d -> p (a d)")
                    mm = nc.tensor.matmul(bank[b][:, 0:D], src[:, k, :], w, start=(k == 0), stop=(k == H - 1))
                mm.then_inc(sem_out, 1)

            def stage_a(s, m):
                if isinstance(s, int):
                    pe.wait_ge(y_in[m], 16 * (s // 4 + 1))
                else:
                    pe.wait_ge(y_in[m], 4 * (s - m) + 16)
                reached(pe, Ac_s, s)
                transposes(0, yt[:, m, :], s, A_s)

            def turn(s, n, experts):
                if live(s - 1):
                    pe.wait_ge(Bc_s, s)
                    reached(pe, Cc_s, s - 1)
                    transposes(2, z1[:], s - 1, C_s)
                if live(s - 2):
                    pe.wait_ge(Dc_s, s - 1)
                    reached(pe, Ec_s, s - 2)
                    transposes(4, z2[:], s - 2, E_s)
                if live(s + 1):
                    stage_a(s + 1, (n + 1) % 4)
                if live(s):
                    e = experts(0)
                    pe.wait_ge(Ac_s, s + 1)
                    reached(pe, Bc_s, s)
                    layer(1, 0, yT[:, n % 2], e, B_s)
                if live(s - 1):
                    e = experts(1)
                    pe.wait_ge(Cc_s, s)
                    reached(pe, Dc_s, s - 1)
                    layer(3, 1, h1, e, D_s)
                if live(s - 2):
                    e = experts(2)
                    pe.wait_ge(Ec_s, s - 1)
                    reached(pe, Fz_s, s - 2)
                    layer(5, 2, h2, e, F_s)
            pe.wait_ge(tab_s, 1)
            stage_a(0, 0)
            step_turns(pe, turn)

        @block.scalar
        def _(act):
            def relu(b, to, bias, e):
                for h in range(H):
                    mm = nc.scalar.activation(to[:, h, :], bank[b][:, h * P:(h + 1) * P], ACT.Relu,
                                              bias=c[bias][:, bass.ds(e, 1), h:h + 1].rearrange("p a b -> p (a b)"))
                return mm

            def stage_a(s, m):
                act.wait_ge(A_s, s + 1)
                reached(act, B_s, s - 1)
                reached(act, Fc_s, s - 3)
                nc.scalar.copy(pair[:, m, :], yt[:, m, D:ROWX])
                nc.scalar.copy(yT[:, m % 2], bank[0][:, 0:D].rearrange("p (h n) -> p h n", h=H)).then_inc(Ac_s, 1)

            def turn(s, n, experts):
                if live(s - 1):
                    e = experts(1)
                    act.wait_ge(C_s, s)
                    reached(act, D_s, s - 1)
                    relu(2, h1, "be1", e).then_inc(Cc_s, 1)
                if live(s - 2):
                    e = experts(2)
                    act.wait_ge(E_s, s - 1)
                    reached(act, F_s, s - 2)
                    relu(4, h2, "be2", e).then_inc(Ec_s, 1)
                if live(s + 1):
                    stage_a(s + 1, (n + 1) % 4)
            act.wait_ge(tab_s, 1)
            stage_a(0, 0)
            step_turns(act, turn)

        @block.vector
        def _(dve):
            count = [0]

            def link(ins):
                count[0] += 1
                ins.then_inc(v, 1)
                dve.wait_ge(v, count[0])

            dve.wait_ge(b_in, 16)
            dve.wait_ge(p_s, 3)
            c1 = c["count"][0:1, :]
            link(nc.vector.tensor_scalar(tl[0:1], c1, 1.0 / P, 127.0 / P - 0.5 + 0.5 / P, ALU.mult, ALU.add))
            link(nc.vector.tensor_copy(tli[0:1], tl[0:1]))
            link(nc.vector.tensor_copy(tl[0:1], tli[0:1]))
            nc.vector.tensor_copy(cnti[0:1], c1)
            link(nc.vector.tensor_tensor(endm[0:1], c["prior"][0:1], tl[0:1].unsqueeze(1).to_broadcast([1, NE, NE]), ALU.mult))
            link(nc.vector.tensor_reduce(first[0:1], endm[0:1], AX.X, ALU.add))
            link(nc.vector.tensor_tensor(end[0:1], first[0:1], tl[0:1], ALU.add))
            steps = stepf[:].unsqueeze(2).to_broadcast([1, S, NE])
            link(nc.vector.tensor_tensor(over[:], steps, end[0:1].unsqueeze(1).to_broadcast([1, S, NE]), ALU.is_ge))
            link(nc.vector.tensor_reduce(ex[:], over[:], AX.X, ALU.add))
            link(nc.vector.tensor_tensor(jump[:], over[:], tl[0:1].unsqueeze(1).to_broadcast([1, S, NE]), ALU.mult))
            link(nc.vector.tensor_reduce(jm[:], jump[:], AX.X, ALU.add))
            link(nc.vector.tensor_tensor(row[:], stepf[:], jm[:], ALU.subtract))
            link(nc.vector.tensor_scalar(row[:], row[:], float(P), None, ALU.mult))
            link(nc.vector.scalar_tensor_tensor(out=row[:], in0=ex[:], scalar=float(REG), in1=row[:], op0=ALU.mult, op1=ALU.add))
            link(nc.vector.tensor_scalar(rowi[:], row[:], float(NE * REG), None, ALU.min))
            link(nc.vector.tensor_scalar(exi[:], ex[:], float(NE - 1), None, ALU.min))
            dve.sem_inc(tab_s, 1)

            def turn(s, n, experts):
                if live(s):
                    dve.wait_ge(B_s, s + 1)
                    reached(dve, C_s, s)
                    nc.vector.tensor_copy(z1[:], bank[1][:, 0:D]).then_inc(Bc_s, 1)
                if live(s - 1):
                    dve.wait_ge(D_s, s)
                    reached(dve, E_s, s - 1)
                    nc.vector.tensor_copy(z2[:], bank[3][:, 0:D]).then_inc(Dc_s, 1)
                if live(s - 2):
                    e = experts(2)
                    dve.wait_ge(F_s, s - 1)
                    reached(dve, Fc_s, s - 2)
                    nc.vector.tensor_tensor(z3[:], bank[5][:, 0:D], b3[:, bass.ds(e, 1), :].rearrange("p a d -> p (a d)"), ALU.add).then_inc(Fz_s, 1)
                    m = (n + 2) % 4
                    dve.wait_ge(Fz_s, s - 1)
                    reached(dve, o_out, 16 * (s - 5))
                    nc.vector.tensor_scalar(O[:, m, :], z3[:], pair[:, m, 0:1], None, ALU.mult)
                    nc.vector.tensor_copy(oid[:, m:m + 1], pair[:, m, 1:2]).then_inc(Fc_s, 1)
            step_turns(dve, turn)


def graph_layer(nc, a, out):
    dram = {n: nc.dram_tensor(n, [ROWS, D], F32).ap() for n in ("Fin", "Fout", "T0", "T1", "TA")}
    dram["x1"] = nc.dram_tensor("x1", [ROWS + P, D], F32).ap()
    dram["Y"] = nc.dram_tensor("Y", [NE * REG + P, ROWX], F32).ap()
    dram["slow"] = nc.dram_tensor("slow", [4, EC * P * P], F32).ap()
    with ExitStack() as ctx:
        ctx.enter_context(nc.allow_non_contiguous_dma(reason="bias columns, and single edges on the rare path"))
        bank = [ctx.enter_context(nc.psum_tensor(f"bank{n}", [P, 512], F32)) for n in range(8)]
        c = persistent(nc, ctx)
        with ExitStack() as edges:
            c.update(for_edges(nc, edges))
            with nc.cleanup_on_exit():
                normalise_nodes(nc, c, bank, a, dram)
            transform_nodes(nc, c, bank, a, dram)
            sum_over_edges(nc, c, bank, a, dram)
            sum_far_edges(nc, c, bank, dram)
        gate_nodes(nc, c, bank, a, dram)
        run_experts(nc, c, bank, a, dram, out)


_INS = ['x', 'src', 'dst', 'edge_weight', 'edge_weight_n2', 'L0_gnn_gamma', 'L0_gnn_beta', 'L0_gnn_W_in', 'L0_gnn_b_in',
        'L0_gnn_W_out', 'L0_gnn_b_out', 'L0_gnn_W_x2i', 'L0_gnn_b_x2i', 'L0_gnn_W_h2h', 'L0_ffn_router_w1',
        'L0_ffn_router_b1', 'L0_ffn_router_w2', 'L0_ffn_router_b2', 'L0_ffn_expert_w1', 'L0_ffn_expert_b1',
        'L0_ffn_expert_w2', 'L0_ffn_expert_b2', 'L0_ffn_expert_w3', 'L0_ffn_expert_b3']


def kernel(**inputs):
    import numpy as _np
    import concourse.bacc as _bacc
    from concourse import mybir as _mybir
    from concourse.bass_utils import run_bass_kernel_spmd as _run

    nc = _bacc.Bacc("TRN2", target_bir_lowering=False, num_devices=1)
    arrays, args = {}, {}
    for name in _INS:
        arr = _np.ascontiguousarray(inputs[name])
        arrays[f"in_{name}_dram"] = arr
        args[name] = nc.dram_tensor(f"in_{name}_dram", arr.shape, _mybir.dt.from_np(arr.dtype), kind="ExternalInput").ap()
    out = nc.dram_tensor("out_0_dram", (N, D), F32, kind="ExternalOutput").ap()
    graph_layer(nc, args, out)
    r = _run(nc, [arrays], core_ids=[0])
    return r.results[0]["out_0_dram"]
```

```python
from contextlib import ExitStack

import concourse.bass as bass
from concourse import mybir

P = 128
N = 6250
E = 100000
D = 256
H = D // P
EPS = 1e-5
NT = -(-N // P)
NP = NT * P
TAIL = N - (NT - 1) * P
BLK = 7
NB = NT // BLK
ET = -(-E // P)
ETAIL = E - (ET - 1) * P
EC = -(-ET // P)
QUAD = 4
BODY = 2 * QUAD
TILES = -(-ET // BODY) * BODY
TURNS = TILES // BODY
ROWS = 6400
SPARE = ROWS - P
ACCW = ROWS
GN = 448
ST = 4
GP = GN // ST
GROUPS = -(-N // GN)
NE = 6
ROWX = D + NE + 1
REG = 6400
STEPS = 2 * GROUPS * GN // P + NE
RH = 128

F32 = mybir.dt.float32
I32 = mybir.dt.int32
BF16 = mybir.dt.bfloat16
ALU = mybir.AluOpType
ACT = mybir.ActivationFunctionType
AX = mybir.AxisListType


def reached(eng, sem, value):
    if not isinstance(value, int) or value > 0:
        eng.wait_ge(sem, value)


def turns(eng, n, body, peel_last=False, peel=1):
    for i in range(peel):
        body(i, i == 0, False)
    with eng.Fori(peel, n - peel_last) as i:
        body(i, False, False)
    if peel_last:
        body(n - 1, False, True)


def tile_at(x, i):
    return x[:, i, :] if isinstance(i, int) else x[:, bass.ds(i, 1), :].rearrange("p a d -> p (a d)")


def persistent(nc, ctx):
    def sb(name, shape, dt=F32):
        return ctx.enter_context(nc.sbuf_tensor(name, shape, dt))

    return {
        "ident": sb("ident", [P, P]),
        "eps": sb("eps", [P, 1]),
        "wx": sb("wx", [P, 2 * H, 2 * D]),
        "wh": sb("wh", [P, H, 2 * D]),
        "wr1": sb("wr1", [P, H, RH]),
        "wr2": sb("wr2", [P, NE]),
        "bx": sb("bx", [P, 2 * H]),
        "br1": sb("br1", [P, 1]),
        "gamma": sb("gamma", [P, H]),
        "beta": sb("beta", [P, H]),
        "be1": sb("be1", [P, NE, H]),
        "be2": sb("be2", [P, NE, H]),
        "count": sb("count", [P, NE]),
        "region": sb("region", [P, ST * NE]),
        "br2": sb("br2", [P, NE]),
        "exi": sb("exi", [1, STEPS], I32),
        "rowi": sb("rowi", [1, STEPS], I32),
        "scale": sb("scale", [P, H]),
        "shift": sb("shift", [P, H]),
        "xlT": sb("xlT", [P, H, NP]),
        "accT": sb("accT", [P, H, ACCW]),
        "we": sb("we", [P, 3, NE, H, D]),
        "far": sb("far", [1, 1], I32),
        "prior": sb("prior", [P, NE, NE]),
    }


def for_edges(nc, ctx):
    def sb(name, shape, dt=F32):
        return ctx.enter_context(nc.sbuf_tensor(name, shape, dt))

    return {
        "zero": sb("zero", [P, D]),
        "below": sb("below", [P, P]),
        "iota": sb("iota", [P, P]),
        "spare": sb("spare", [P, QUAD]),
        "wio": sb("wio", [P, H, 2 * D]),
        "col": sb("col", [P, EC * P, 4]),
        "base": sb("base", [1, EC * P], I32),
    }


def normalise_nodes(nc, c, bank, a, dram, z_out):
    with ExitStack() as ctx:
        def sb(name, shape, dt=F32):
            return ctx.enter_context(nc.sbuf_tensor(name, shape, dt))

        def sem(name):
            return nc.alloc_semaphore("n_" + name)

        X = c["accT"][:].rearrange("p h n -> p (h n)")[:, 0:NT * D].rearrange("p (t d) -> p t d", d=D)
        XN = sb("XN", [P, BLK, D])
        rows = sb("rows", [P, 2, EC, P], I32)
        wrow = sb("wrow", [P, 2, EC, P])
        stats = sb("stats", [P, BLK, 6])
        mv = sb("mv", [P, BLK, 2])
        sd = sb("sd", [P, BLK])
        rstd = sb("rstd", [P, BLK])
        nmr = sb("nmr", [P, BLK])
        fstat = sb("fstat", [P, H, 2 * NB, 6])
        fmv = sb("fmv", [P, H, 2])
        fsd = sb("fsd", [P, H])
        frs = sb("frs", [P, H])
        fms = sb("fms", [P, H])
        spot = c["we"][:].rearrange("p l e h d -> p (l e h d)")
        EW = EC * P

        def view(n):
            return spot[:, n * EW:(n + 1) * EW].rearrange("p (c j) -> p c j", c=EC)

        srcf, dstf, rel, near, iwn, own, iwf, owf = (view(n) for n in range(8))
        least = sb("least", [P, EC])
        most = sb("most", [P, 1])
        mostr = sb("mostr", [1, 1])

        x_in = [sem(f"x_in{b}") for b in range(2)]
        tail_in = sem("tail_in")
        tail_z = sem("tail_z")
        e_in = sem("e_in")
        w_in = sem("w_in")
        filled = sem("filled")
        consts = sem("consts")
        idx_f = sem("idx_f")
        lst = sem("lst")
        rel_s = sem("rel_s")
        near_s = sem("near_s")
        wn_s = sem("wn_s")
        wf_s = sem("wf_s")
        most_s = sem("most_s")
        edge_T = sem("edge_T")
        edge_c = sem("edge_c")
        base_T = sem("base_T")
        base_c = sem("base_c")
        most_T = sem("most_T")
        most_r = sem("most_r")
        far_s = sem("far_s")
        st_s = sem("st_s")
        held = sem("held1")
        mv_s = sem("mv_s")
        sd_s = sem("sd_s")
        rs_s = sem("rs_s")
        xn_s = sem("xn_s")
        xT_s = sem("xT_s")
        xTc_s = sem("xTc_s")
        fst = sem("fst")
        fmv_s = sem("fmv_s")
        fsd_s = sem("fsd_s")
        frs_s = sem("frs_s")
        fsc = sem("fsc")
        fms_s = sem("fms_s")
        slow_out = sem("slow_out")
        z_s = sem("z_s")

        block = ctx.enter_context(nc.Block())

        def block_turns(eng, turn, edges):
            turn(0, 0)
            edges()
            with eng.Fori(0, (NB - 1) // 2) as i:
                turn(2 * i + 1, 1)
                turn(2 * i + 2, 0)

        full = (ET - 1) // P * P
        rest = ET - 1 - full

        @block.sync
        def _(sp):
            sp.wait_ge(tail_z, 1)
            sp.dma_start(X[0:TAIL, NT - 1, :], a["x"][(NT - 1) * P:N]).then_inc(tail_in, 16)
            for b in range(NB):
                t0, t1 = b * BLK, min((b + 1) * BLK, NT - 1)
                if b >= 2:
                    sp.wait_ge(x_in[b % 2], 16 * (b // 2))
                sp.dma_start(X[:, t0:t1, :], a["x"][t0 * P:t1 * P].rearrange("(t p) d -> p t d", p=P)).then_inc(x_in[b % 2], 16)
            for name, src in (
                ("gamma", a["L0_gnn_gamma"].rearrange("(k p) -> p k", p=P)),
                ("beta", a["L0_gnn_beta"].rearrange("(k p) -> p k", p=P)),
                ("wx", a["L0_gnn_W_x2i"].rearrange("(k p) n -> p k n", p=P)),
                ("wh", a["L0_gnn_W_h2h"].rearrange("(k p) n -> p k n", p=P)),
                ("wr1", a["L0_ffn_router_w1"].rearrange("(k p) n -> p k n", p=P)),
                ("wr2", a["L0_ffn_router_w2"]),
                ("bx", a["L0_gnn_b_x2i"].rearrange("(k p) -> p k", p=P)),
                ("br1", a["L0_ffn_router_b1"].rearrange("(p a) -> p a", a=1)),
                ("br2", a["L0_ffn_router_b2"].rearrange("(a e) -> a e", a=1).partition_broadcast(P)),
            ):
                sp.dma_start(c[name][:], src).then_inc(w_in, 16)
            sp.dma_start(c["be1"][:], a["L0_ffn_expert_b1"].rearrange("e (k p) -> p e k", p=P)).then_inc(w_in, 16)
            sp.dma_start(c["be2"][:], a["L0_ffn_expert_b2"].rearrange("e (k p) -> p e k", p=P)).then_inc(w_in, 16)
            for k, name in enumerate(("L0_gnn_W_in", "L0_gnn_W_out")):
                sp.dma_start(c["wio"][:, :, k * D:(k + 1) * D], a[name].rearrange("(k p) n -> p k n", p=P)).then_inc(w_in, 16)
            sp.wait_ge(wf_s, 2)
            for k, v in enumerate((srcf, dstf, iwf, owf)):
                sp.dma_start(dram["slow"][k].rearrange("(c p j) -> p c j", p=P, j=P), v).then_inc(slow_out, 16)
            sp.wait_ge(slow_out, 64)

        @block.gpsimd
        def _(pool):
            nc.gpsimd.memset(rows[:, 0, EC - 1, :], 0).then_inc(filled, 1)
            nc.gpsimd.memset(rows[:, 1, EC - 1, :], N - 1).then_inc(filled, 1)
            nc.gpsimd.memset(wrow[:, :, EC - 1, :], 0.0).then_inc(filled, 1)
            nc.gpsimd.memset(c["ident"][:], 0.0).then_inc(filled, 1)
            nc.gpsimd.memset(c["zero"][:], 0.0).then_inc(z_s, 1)
            nc.gpsimd.memset(c["below"][:], 1.0).then_inc(consts, 1)
            pool.wait_ge(filled, 4)
            nc.gpsimd.affine_select(out=c["ident"][:], in_=c["ident"][:], compare_op=ALU.not_equal, fill=1.0, base=0,
                                    pattern=[[-1, P]], channel_multiplier=1).then_inc(consts, 1)
            pool.wait_ge(consts, 2)
            nc.gpsimd.affine_select(out=c["below"][:], in_=c["below"][:], compare_op=ALU.is_gt, fill=0.0, base=0,
                                    pattern=[[-1, P]], channel_multiplier=1).then_inc(consts, 1)
            nc.gpsimd.iota(c["iota"][:], pattern=[[1, P]], base=0, channel_multiplier=0,
                           allow_small_or_imprecise_dtypes=True).then_inc(consts, 1)
            nc.gpsimd.iota(c["spare"][:], pattern=[[0, QUAD]], base=SPARE, channel_multiplier=1,
                           allow_small_or_imprecise_dtypes=True).then_inc(consts, 1)
            nc.gpsimd.memset(c["eps"][:], EPS).then_inc(consts, 1)
            nc.gpsimd.memset(c["prior"][:], 1.0).then_inc(consts, 1)
            pool.wait_ge(consts, 7)
            nc.gpsimd.affine_select(out=c["prior"][:], in_=c["prior"][:], compare_op=ALU.is_gt, fill=0.0, base=0,
                                    pattern=[[1, NE], [-1, NE]], channel_multiplier=0).then_inc(consts, 1)
            pool.wait_ge(z_s, 1)
            pool.wait_ge(x_in[0], 16 * (NB // 2 + 1))
            for n in ("T0", "T1"):
                pool.dma_start(dram[n].rearrange("(p r) d -> p r d", p=P),
                               c["zero"][:].unsqueeze(1).to_broadcast([P, ROWS // P, D])).then_inc(z_out, 16)
            for n in ("Fin", "Fout"):
                pool.dma_start(dram[n][NP:ROWS], c["zero"][:]).then_inc(z_out, 16)

        @block.scalar
        def _(act):
            act.wait_ge(filled, 4)
            for n, e in enumerate((a["src"], a["dst"], a["edge_weight"], a["edge_weight_n2"])):
                to = rows[:, n] if n < 2 else wrow[:, n - 2]
                act.dma_start(to[:, 0:EC - 1, :], e[0:full * P].rearrange("(c p j) -> p c j", p=P, j=P)).then_inc(e_in, 16)
                act.dma_start(to[0:rest, EC - 1, :],
                              e[full * P:(full + rest) * P].rearrange("(p j) -> p j", j=P)).then_inc(e_in, 16)
                act.dma_start(to[rest:rest + 1, EC - 1, 0:ETAIL],
                              e[(full + rest) * P:E].rearrange("(p j) -> p j", p=1)).then_inc(e_in, 16)
            act.wait_ge(consts, 6)

            def transposed(t, j):
                act.wait_ge(xT_s, t + 1)
                nc.scalar.copy(c["xlT"][:, :, bass.ds(t * P, P)],
                               bank[4 + j % 4][:, 0:D].rearrange("p (h n) -> p h n", h=H)).then_inc(xTc_s, 1)

            def block_turn(i, q):
                act.wait_ge(mv_s, i + 1)
                reached(act, rs_s, i)
                nc.scalar.activation(sd[:], mv[:, :, 1], ACT.Sqrt, bias=c["eps"][:]).then_inc(sd_s, 1)
                act.wait_ge(rs_s, 2 * i + 2)
                for j in range(BLK):
                    t = BLK * i + j
                    reached(act, xT_s, t - BLK + 1)
                    nc.scalar.activation(XN[:, j, :], tile_at(X, t), ACT.Identity, bias=nmr[:, j:j + 1],
                                         scale=rstd[:, j:j + 1]).then_inc(xn_s, 1)
                    if j >= 2:
                        transposed(t - 2, j - 2)
                for j in range(BLK - 2, BLK):
                    transposed(BLK * i + j, j)

            def edges():
                for ch in range(EC):
                    act.wait_ge(edge_T, ch + 1)
                    nc.scalar.copy(c["col"][:, ch * P:(ch + 1) * P, :].rearrange("p t k -> p k t"),
                                   bank[ch % 2][:].rearrange("p (k t) -> p k t", k=4)).then_inc(edge_c, 1)
                act.wait_ge(base_T, 1)
                nc.scalar.copy(c["base"][:, 0:4 * P], bank[2][0:1, :]).then_inc(base_c, 1)
                nc.scalar.copy(c["base"][:, 4 * P:EC * P], bank[3][0:1, 0:(EC - 4) * P]).then_inc(base_c, 1)

            block_turns(act, block_turn, edges)

            act.wait_ge(fmv_s, H)
            nc.scalar.activation(fsd[:], fmv[:, :, 1], ACT.Sqrt, bias=c["eps"][:]).then_inc(fsd_s, 1)

        @block.tensor
        def _(pe):
            pe.wait_ge(consts, 2)

            def edges():
                pe.wait_ge(wn_s, 2)
                for ch in range(EC):
                    if ch >= 2:
                        pe.wait_ge(edge_c, ch - 1)
                    for k, v in enumerate((srcf, rel, iwn, own)):
                        last = nc.tensor.transpose(bank[ch % 2][:, k * P:(k + 1) * P], v[:, ch, :], c["ident"][:])
                    last.then_inc(edge_T, 1)
                for ch in range(EC):
                    last = nc.tensor.transpose(bank[2 + ch // 4][0:1, (ch % 4) * P:(ch % 4 + 1) * P], least[:, ch:ch + 1], c["ident"][:])
                last.then_inc(base_T, 1)
                pe.wait_ge(most_s, 1)
                pe.wait_ge(base_c, 2)
                nc.tensor.transpose(bank[2][0:1, 0:P], most[:], c["ident"][:]).then_inc(most_T, 1)

            def block_turn(i, q):
                for j in range(BLK):
                    pe.wait_ge(xn_s, BLK * i + j + 1)
                    reached(pe, xTc_s, BLK * i + j - 3)
                    for h in range(H):
                        mm = nc.tensor.transpose(bank[4 + j % 4][:, h * P:(h + 1) * P], XN[:, j, h * P:(h + 1) * P], c["ident"][:])
                    mm.then_inc(xT_s, 1)

            block_turns(pe, block_turn, edges)

        @block.vector
        def _(dve):
            nc.vector.memset(X[:, NT - 1, :], 0.0).then_inc(tail_z, 1)

            def edges():
                dve.wait_ge(e_in, 12 * 16)
                nc.vector.tensor_copy(srcf, rows[:, 0]).then_inc(idx_f, 1)
                nc.vector.tensor_copy(dstf, rows[:, 1]).then_inc(idx_f, 1)
                dve.wait_ge(idx_f, 2)
                nc.vector.tensor_reduce(least[:], dstf, AX.X, ALU.min).then_inc(lst, 1)
                dve.wait_ge(lst, 1)
                nc.vector.tensor_tensor(rel, dstf, least[:].unsqueeze(2).to_broadcast([P, EC, P]), ALU.subtract).then_inc(rel_s, 1)
                dve.wait_ge(rel_s, 1)
                nc.vector.tensor_scalar(near, rel, float(P), None, ALU.is_lt).then_inc(near_s, 1)
                nc.vector.tensor_reduce(most[:], rel, AX.XY, ALU.max).then_inc(most_s, 1)
                dve.wait_ge(near_s, 1)
                nc.vector.tensor_tensor(iwn, wrow[:, 0], near, ALU.mult).then_inc(wn_s, 1)
                nc.vector.tensor_tensor(own, wrow[:, 1], near, ALU.mult).then_inc(wn_s, 1)
                dve.wait_ge(wn_s, 2)
                nc.vector.tensor_tensor(iwf, wrow[:, 0], iwn, ALU.subtract).then_inc(wf_s, 1)
                nc.vector.tensor_tensor(owf, wrow[:, 1], own, ALU.subtract).then_inc(wf_s, 1)

            def feature_stats(i):
                dve.wait_ge(xTc_s, BLK * i + BLK)
                half = BLK * P // 2
                for h in range(H):
                    for k in range(2):
                        width = half if not isinstance(i, int) or i < NB - 1 or k == 0 else N - (2 * NB - 1) * half
                        nc.vector.bn_stats(fstat[:, h, bass.ds(2 * i + k, 1), :].rearrange("p a s -> p (a s)"),
                                           c["xlT"][:, h, bass.ds((2 * i + k) * half, width)]).then_inc(fst, 1)

            def block_turn(i, q):
                if isinstance(i, int):
                    dve.wait_ge(x_in[q], 16 * (i // 2 + 1))
                    dve.wait_ge(tail_in, 16)
                else:
                    dve.wait_ge(x_in[q], 8 * (i - q) + 16)
                for j in range(BLK):
                    nc.vector.bn_stats(stats[:, j, :], tile_at(X, BLK * i + j)).then_inc(st_s, 1)
                dve.wait_ge(st_s, BLK * i + BLK)
                dve.sem_inc(held, 1)
                for j in range(BLK):
                    mm = nc.vector.bn_aggr(mv[:, j, :], stats[:, j, :])
                mm.then_inc(mv_s, 1)
                reached(dve, xn_s, BLK * i)
                dve.wait_ge(sd_s, i + 1)
                nc.vector.reciprocal(rstd[:], sd[:]).then_inc(rs_s, 1)
                dve.wait_ge(rs_s, 2 * i + 1)
                nc.vector.scalar_tensor_tensor(out=nmr[:], in0=mv[:, :, 0], scalar=-1.0, in1=rstd[:],
                                               op0=ALU.mult, op1=ALU.mult).then_inc(rs_s, 1)
                if not isinstance(i, int):
                    feature_stats(i - 1)

            block_turns(dve, block_turn, edges)
            feature_stats(NB - 1)
            dve.wait_ge(fst, 2 * H * NB)
            for h in range(H):
                nc.vector.bn_aggr(fmv[:, h, :], fstat[:, h].rearrange("p k s -> p (k s)")).then_inc(fmv_s, 1)
            dve.wait_ge(most_T, 1)
            nc.vector.tensor_reduce(mostr[:], bank[2][0:1, 0:P], AX.X, ALU.max).then_inc(most_r, 1)
            dve.wait_ge(most_r, 1)
            nc.vector.tensor_scalar(c["far"][:], mostr[:], float(P), None, ALU.is_ge).then_inc(far_s, 1)
            dve.wait_ge(fsd_s, 1)
            nc.vector.reciprocal(frs[:], fsd[:]).then_inc(frs_s, 1)
            dve.wait_ge(frs_s, 1)
            dve.wait_ge(w_in, 13 * 16)
            nc.vector.tensor_tensor(c["scale"][:], frs[:], c["gamma"][:], ALU.mult).then_inc(fsc, 1)
            dve.wait_ge(fsc, 1)
            nc.vector.tensor_tensor(fms[:], fmv[:, :, 0], c["scale"][:], ALU.mult).then_inc(fms_s, 1)
            dve.wait_ge(fms_s, 1)
            nc.vector.tensor_tensor(c["shift"][:], c["beta"][:], fms[:], ALU.subtract).then_inc(fsc, 1)


def transform_nodes(nc, c, bank, a, dram, z_out):
    with ExitStack() as ctx:
        def sb(name, shape, dt=F32):
            return ctx.enter_context(nc.sbuf_tensor(name, shape, dt))

        def sem(name):
            return ctx.enter_context(nc.semaphore(name))

        hT = sb("hT", [P, BLK, H, P])
        F = sb("F", [P, BLK, 2 * D])
        bio = sb("bio", [P, 2 * D])
        b_in = sem("b_in")
        h_s = sem("h_s")
        mm_s = sem("mm_s")
        f_s = sem("f_s")
        out_in = [sem(f"out_in{j}") for j in range(BLK)]
        out_out = [sem(f"out_out{j}") for j in range(BLK)]
        acc_z = sem("acc_z")
        block = ctx.enter_context(nc.Block())

        @block.gpsimd
        def _(pool):
            nc.gpsimd.memset(c["accT"][:].rearrange("p h n -> p (h n)"), 0.0).then_inc(acc_z, 1)
            pool.wait_ge(acc_z, 1)
            pool.wait_ge(z_out, 16 * 4)

        def node_turns(eng, step):
            def body(i, first, last):
                for j in range(BLK):
                    step(i, j, BLK * i + j, first)
            turns(eng, NB, body)

        @block.scalar
        def _(act):
            def step(i, j, t, first):
                reached(act, mm_s, t - BLK + 1)
                for h in range(H):
                    mm = nc.scalar.activation(hT[:, j, h, :], c["xlT"][:, h, bass.ds(t * P, P)], ACT.Identity,
                                              bias=c["shift"][:, h:h + 1], scale=c["scale"][:, h:h + 1])
                mm.then_inc(h_s, 1)
            node_turns(act, step)

        @block.tensor
        def _(pe):
            def step(i, j, t, first):
                pe.wait_ge(h_s, t + 1)
                reached(pe, f_s, t - BLK + 1)
                for h in range(H):
                    mm = nc.tensor.matmul(bank[j][:], hT[:, j, h, :], c["wio"][:, h, :], start=(h == 0), stop=(h == H - 1))
                mm.then_inc(mm_s, 1)
            node_turns(pe, step)

        @block.vector
        def _(dve):
            dve.wait_ge(b_in, 32)

            def step(i, j, t, first):
                dve.wait_ge(mm_s, t + 1)
                if not first:
                    dve.wait_ge(out_in[j], 16 * i)
                    dve.wait_ge(out_out[j], 16 * i)
                nc.vector.tensor_tensor(F[:, j, :], bank[j][:], bio[:], ALU.add).then_inc(f_s, 1)
            node_turns(dve, step)

        @block.sync
        def _(sp):
            for k, name in enumerate(("L0_gnn_b_in", "L0_gnn_b_out")):
                sp.dma_start(bio[:, k * D:(k + 1) * D], a[name].rearrange("(a d) -> a d", a=1).partition_broadcast(P)).then_inc(b_in, 16)

            def step(i, j, t, first):
                sp.wait_ge(f_s, t + 1)
                sp.dma_start(dram["Fin"][bass.ds(t * P, P), :], F[:, j, 0:D]).then_inc(out_in[j], 16)
                sp.dma_start(dram["Fout"][bass.ds(t * P, P), :], F[:, j, D:2 * D]).then_inc(out_out[j], 16)
            node_turns(sp, step)
            for j in range(BLK):
                sp.wait_ge(out_in[j], 16 * NB)
                sp.wait_ge(out_out[j], 16 * NB)


def sum_over_edges(nc, c, bank, a, dram):
    with ExitStack() as ctx:
        def sb(name, shape, dt=F32):
            return ctx.enter_context(nc.sbuf_tensor(name, shape, dt))

        def sem(name):
            return ctx.enter_context(nc.semaphore(name))

        stage = sb("stage", [P, 2, QUAD, 4])
        gsrc = sb("gsrc", [P, 2, QUAD], I32)
        sdst = sb("sdst", [P, 2, QUAD], I32)
        seen = sb("seen", [P, 2, QUAD])
        moved = sb("moved", [P, 2, QUAD])
        G = sb("G", [P, BODY, D])
        W = sb("W", [P, QUAD, D])
        place_w = sb("place_w", [P, 2, P])
        place = sb("place", [P, 2, P])
        same = sb("same", [P, 2, P])
        cnt_junk = sb("cnt_junk", [P, 2, P])
        Ps = sb("Ps", [P, 2, P])
        O = sb("O", [P, BODY, D])
        hx = sb("hx", [P, H, P])
        hh = sb("hh", [P, 2, 2, P])

        stage_s = sem("stage_s")
        bc_s = sem("bc_s")
        place_s = sem("place_s")
        same_s = sem("same_s")
        a_s = sem("a_s")
        add_s = sem("add_s")
        p_s = sem("p_s")
        ps_s = sem("ps_s")
        o_s = sem("o_s")
        os_s = sem("os_s")
        held = sem("held3")
        hx_s = sem("hx_s")
        hm_s = sem("hm_s")
        hc_s = sem("hc_s")
        hh_out = [sem(f"hh_out{j}") for j in range(2)]
        cl_s = sem("cl_s")
        we_in = sem("we_in")
        sd_s = sem("sd_s")
        g_in = [sem(f"g_in{j}") for j in range(BODY)]
        w_in = [sem(f"w_in{j}") for j in range(QUAD)]
        t_out = [sem(f"t_out{j}") for j in range(2)]
        block = ctx.enter_context(nc.Block())

        def edge_turns(eng, quad_step, tile_step, peel=1):
            def body(i, first, last):
                for q in range(2):
                    quad_step(i, q, 2 * i + q, first and q == 0, last and q == 1)
                    for u in range(QUAD):
                        tile_step(i, q, u, BODY * i + QUAD * q + u, first, last)
            turns(eng, TURNS, body, peel_last=True, peel=peel)

        def edge_and_node_turns(eng, quad_step, tile_step, peel=1):
            def body(i, first, last, nodes):
                for q in range(2):
                    quad_step(i, q, 2 * i + q, first and q == 0, last and q == 1, nodes)
                    for u in range(QUAD):
                        tile_step(i, q, u, BODY * i + QUAD * q + u, first, last, nodes)
            for i in range(peel):
                body(i, i == 0, False, True)
            with eng.Fori(peel, NT) as i:
                body(i, False, False, True)
            with eng.Fori(NT, TURNS - 1) as i:
                body(i, False, False, False)
            body(TURNS - 1, False, True, False)

        @block.sync
        def _(sp):
            def tile_step(i, q, u, t, first, last):
                reached(sp, o_s, t - QUAD + 1)
                base = sp.value_load(c["base"][0:1, bass.ds(t, 1)], min_val=0, max_val=N - 1)
                sp.dma_start(W[:, u, :], dram["Fout"][bass.ds(base, P), :]).then_inc(w_in[u], 16)
            def turn(i, first, last, nodes=True):
                for j in range(BODY):
                    tile_step(i, j // QUAD, j % QUAD, BODY * i + j, first, last)
                if nodes:
                    for j in range(2):
                        sp.wait_ge(hc_s, 2 * i + 1 + j)
                        sp.sem_inc(held, 1)
                        sp.dma_start(dram["hh"][2 * j:2 * j + 2, :, bass.ds(i * P, P)].rearrange("m p n -> p m n"),
                                     hh[:, j]).then_inc(hh_out[j], 16)

            turn(0, True, False)
            for n in range(3):
                start = 1 + NE * n
                with sp.Fori(start, start + NE) as i:
                    turn(i, False, False)
                    sp.dma_start(c["we"][:, n, bass.ds(i - start, 1)].rearrange("p a k d -> p (a k) d"),
                                 a[f"L0_ffn_expert_w{n + 1}"][bass.ds(i - start, 1)].rearrange("a (k p) d -> p (a k) d", p=P)
                                 ).then_inc(we_in, 16)
            with sp.Fori(1 + 3 * NE, NT) as i:
                turn(i, False, False)
            with sp.Fori(NT, TURNS - 1) as i:
                turn(i, False, False, nodes=False)
            turn(TURNS - 1, False, True, nodes=False)
            for j in range(2):
                sp.wait_ge(hh_out[j], 16 * NT)
            sp.wait_ge(we_in, 16 * 3 * NE)

        @block.gpsimd
        def _(pool):
            def gather(j):
                pool.indirect_dma_start(G[:, j, :], None, dram["Fin"],
                                        bass.IndirectOffsetOnAxis(ap=gsrc[:, j // QUAD, j % QUAD:j % QUAD + 1], axis=0)
                                        ).then_inc(g_in[j], 16)

            def scatter(j, t):
                pool.wait_ge(os_s, t + 1)
                reached(pool, t_out[j % 2], 8 * (t - j % 2))
                pool.sem_inc(held, 1)
                pool.indirect_dma_start(dram[f"T{j % 2}"],
                                        bass.IndirectOffsetOnAxis(ap=sdst[:, j // QUAD, j % QUAD:j % QUAD + 1], axis=0),
                                        O[:, j, :], None, compute_op=ALU.add).then_inc(t_out[j % 2], 16)

            def quad_step(i, q, Q, first, last):
                if not last:
                    pool.wait_ge(stage_s, Q + 2)
                if not first:
                    pool.wait_ge(sd_s, Q)

            def tile_step(i, q, u, t, first, last):
                if not (last and q == 1):
                    reached(pool, a_s, t - QUAD + 1)
                    pool.sem_inc(held, 1)
                    gather(QUAD * (1 - q) + u)
                if not (first and q == 0):
                    scatter(QUAD * (1 - q) + u, t - QUAD)

            pool.wait_ge(stage_s, 1)
            for u in range(QUAD):
                gather(u)
            edge_turns(pool, quad_step, tile_step)
            pool.wait_ge(sd_s, TILES // QUAD)
            for u in range(QUAD):
                scatter(QUAD + u, TILES - QUAD + u)
            for j in range(2):
                pool.wait_ge(t_out[j], 16 * (TILES // 2))

        @block.scalar
        def _(act):
            def stage_quad(Q, q):
                nc.scalar.copy(stage[:, q], c["col"][:, bass.ds(QUAD * Q, QUAD), :])
                nc.scalar.copy(gsrc[:, q], c["col"][:, bass.ds(QUAD * Q, QUAD), 0:1].rearrange("p t a -> p (t a)")).then_inc(stage_s, 1)

            def quad_step(i, q, Q, first, last, nodes):
                if nodes and q == 0:
                    reached(act, hm_s, 2 * i)
                    for h in range(H):
                        mm = nc.scalar.activation(hx[:, h, :], c["xlT"][:, h, bass.ds(i * P, P)], ACT.Identity,
                                                  bias=c["shift"][:, h:h + 1], scale=c["scale"][:, h:h + 1])
                    mm.then_inc(hx_s, 1)
                if last:
                    return
                if not first:
                    act.wait_ge(same_s, QUAD * Q)
                    act.wait_ge(bc_s, QUAD * Q)
                    act.wait_ge(sd_s, Q)
                    for u in range(QUAD):
                        reached(act, g_in[QUAD * (1 - q) + u], 8 * (Q + q))
                stage_quad(Q + 1, 1 - q)

            def rows_out(j, t, i=None, nodes=False):
                act.wait_ge(o_s, t + 1)
                if nodes and j < 2:
                    reached(act, hh_out[j], 16 * i)
                    nc.scalar.copy(hh[:, j], bank[6 + j][:, D:2 * D].rearrange("p (m n) -> p m n", m=2)).then_inc(hc_s, 1)
                reached(act, t_out[j % 2], 8 * (t - 6 - j % 2))
                nc.scalar.copy(O[:, j, :], bank[6 + j % 2][:, 0:D]).then_inc(os_s, 1)

            def tile_step(i, q, u, t, first, last, nodes):
                act.wait_ge(p_s, t + 1)
                reached(act, o_s, t - 1)
                nc.scalar.copy(Ps[:, u % 2, :], bank[4 + u % 2][:, 0:P]).then_inc(ps_s, 1)
                if not (first and q == 0 and u == 0):
                    rows_out((QUAD * q + u - 1) % BODY, t - 1, i, nodes)

            stage_quad(0, 0)
            edge_and_node_turns(act, quad_step, tile_step, peel=2)
            rows_out(BODY - 1, TILES - 1)

        @block.tensor
        def _(pe):
            def spread(q, Q):
                pe.wait_ge(stage_s, Q + 1)
                reached(pe, same_s, QUAD * (Q - 1))
                for u in range(QUAD):
                    nc.tensor.transpose(bank[q][:, u * P:(u + 1) * P], stage[:, q, u, 0:1].to_broadcast([P, P]),
                                        c["ident"][:]).then_inc(bc_s, 1)

            def quad_step(i, q, Q, first, last, nodes):
                if not last:
                    spread(1 - q, Q + 1)

            def out_rows(j, t, i=None, nodes=False):
                pe.wait_ge(ps_s, t + 1)
                pe.wait_ge(w_in[j % QUAD], 4 * (t - j % QUAD) + 16)
                reached(pe, os_s, t - 1)
                if nodes and j < 2:
                    pe.wait_ge(hx_s, i + 1)
                    for m in range(2):
                        for k in range(H):
                            mm = nc.tensor.matmul(bank[6 + j][:, D + m * P:D + (m + 1) * P],
                                                  c["wh"][:, k, (2 * j + m) * P:(2 * j + m + 1) * P], hx[:, k, :],
                                                  start=(k == 0), stop=(k == H - 1))
                    mm.then_inc(hm_s, 1)
                nc.tensor.matmul(bank[6 + j % 2][:, 0:D], Ps[:, j % 2, :], W[:, j % QUAD, :], start=True, stop=True).then_inc(o_s, 1)

            def tile_step(i, q, u, t, first, last, nodes):
                j = QUAD * q + u
                pe.wait_ge(place_s, t + 1)
                pe.wait_ge(g_in[j], 2 * (t - j) + 16)
                reached(pe, add_s, t - 1)
                for h in range(H):
                    mm = nc.tensor.matmul(bank[2 + j % 2][:, h * P:(h + 1) * P], G[:, j, h * P:(h + 1) * P],
                                          place_w[:, j % 2, :], start=True, stop=True)
                mm.then_inc(a_s, 1)
                pe.wait_ge(same_s, t + 1)
                reached(pe, ps_s, t - 1)
                nc.tensor.matmul(bank[4 + j % 2][:, 0:P], place[:, j % 2, :], same[:, j % 2, :], start=True, stop=True).then_inc(p_s, 1)
                if not (first and j == 0):
                    out_rows((j - 1) % BODY, t - 1, i, nodes)

            spread(0, 0)
            edge_and_node_turns(pe, quad_step, tile_step)
            out_rows(BODY - 1, TILES - 1)

        @block.vector
        def _(dve):
            def quad_step(i, q, Q, first, last):
                dve.wait_ge(stage_s, Q + 1)

            def add_sums(j, t):
                dve.wait_ge(a_s, t + 1)
                reached(dve, add_s, t)
                base = dve.value_load(c["base"][0:1, bass.ds(t, 1)], min_val=0, max_val=N - 1)
                at = c["accT"][:, :, bass.ds(base, P)]
                nc.vector.tensor_tensor(at, bank[2 + j % 2][:, 0:D].rearrange("p (h n) -> p h n", h=H), at, ALU.add).then_inc(add_s, 1)

            def tile_step(i, q, u, t, first, last):
                j = QUAD * q + u
                s = stage[:, q, u]
                reached(dve, p_s, t - 1)
                nc.vector.tensor_scalar(place_w[:, j % 2, :], c["iota"][:], s[:, 1:2], s[:, 2:3], ALU.is_equal, ALU.mult)
                nc.vector.tensor_scalar(place[:, j % 2, :], c["iota"][:], s[:, 1:2], None, ALU.is_equal).then_inc(place_s, 1)
                if u == 0:
                    dve.wait_ge(bc_s, QUAD * (2 * i + q + 1))
                srcs = bank[q][:, u * P:(u + 1) * P]
                nc.vector.tensor_scalar(same[:, j % 2, :], srcs, s[:, 0:1], s[:, 3:4], ALU.is_equal, ALU.mult)
                nc.vector.scalar_tensor_tensor(out=cnt_junk[:, j % 2, :], in0=srcs, scalar=s[:, 0:1], in1=c["below"][:],
                                               op0=ALU.is_equal, op1=ALU.mult, accum_out=seen[:, q, u:u + 1]).then_inc(same_s, 1)
                if not (first and j == 0):
                    add_sums((j - 1) % BODY, t - 1)
                if u == QUAD - 1:
                    Q = 2 * i + q
                    dve.wait_ge(same_s, t + 1)
                    for k in range(2):
                        reached(dve, t_out[k], 16 * 2 * (Q - 1))
                    nc.vector.scalar_tensor_tensor(out=moved[:, q], in0=seen[:, q], scalar=1.0, in1=c["spare"][:],
                                                   op0=ALU.min, op1=ALU.mult).then_inc(cl_s, 1)
                    dve.wait_ge(cl_s, Q + 1)
                    nc.vector.tensor_tensor(sdst[:, q], moved[:, q], stage[:, q, :, 0:1].rearrange("p t a -> p (t a)"),
                                            ALU.max).then_inc(sd_s, 1)

            edge_turns(dve, quad_step, tile_step)
            add_sums(BODY - 1, TILES - 1)


def sum_far_edges(nc, c, bank, dram):
    with ExitStack() as ctx:
        def sb(name, shape, dt=F32):
            return ctx.enter_context(nc.sbuf_tensor(name, shape, dt))

        def sem(name):
            return ctx.enter_context(nc.semaphore(name))

        edge = sb("far_edge", [P, 4])
        gidx = sb("far_gidx", [P, 2], I32)
        sidx = sb("far_sidx", [P, 2], I32)
        G = sb("far_G", [P, 2, D])
        O = sb("far_O", [P, 2, D])
        same = sb("far_same", [P, 2, P])
        seen = sb("far_seen", [P, 2])
        junk = sb("far_junk", [P, P])
        moved = sb("far_moved", [P, 2])
        e_in = sem("far_e_in")
        gidx_s = sem("far_gidx_s")
        g_in = [sem(f"far_g_in{k}") for k in range(2)]
        bc_s = sem("far_bc_s")
        same_s = sem("far_same_s")
        mm_s = sem("far_mm_s")
        o_s = sem("far_o_s")
        moved_s = sem("far_moved_s")
        sidx_s = sem("far_sidx_s")
        t_out = [sem(f"far_t_out{k}") for k in range(2)]
        held = sem("far_held")
        z_s = sem("far_z_s")
        z_out = sem("far_z_out")
        f_in = sem("far_f_in")
        fT_s = sem("far_fT_s")
        fa_s = sem("far_fa_s")
        block = ctx.enter_context(nc.Block())

        def if_far(eng, body, fold, before=lambda: None):
            far = eng.value_load(c["far"][0:1, 0:1], min_val=0, max_val=1)
            with eng.If(far):
                before()
                body(0, True)
                with eng.Fori(1, ET) as t:
                    body(t, False)
                fold(0)
                with eng.Fori(1, NT) as t:
                    fold(t)
            with eng.Else():
                eng.nop()

        @block.sync
        def _(sp):
            def tile_step(t, first):
                reached(sp, t_out[0], 16 * t)
                reached(sp, t_out[1], 16 * t)
                sp.dma_start(edge[:].unsqueeze(2), dram["slow"][:, bass.ds(t * P, P)].rearrange("k (p a) -> p k a", a=1)).then_inc(e_in, 16)
            def fold(t):
                reached(sp, fT_s, t)
                if isinstance(t, int):
                    for k in range(2):
                        sp.wait_ge(t_out[k], 16 * ET)
                sp.dma_start(G[:, 0, :], dram["TA"][bass.ds(t * P, P), :]).then_inc(f_in, 16)
            if_far(sp, tile_step, fold)

        @block.vector
        def _(dve):
            def tile_step(t, first):
                dve.wait_ge(e_in, 16 * t + 16)
                nc.vector.tensor_copy(gidx[:], edge[:, 0:2]).then_inc(gidx_s, 1)
                dve.wait_ge(bc_s, 2 * t + 2)
                for k in range(2):
                    row = bank[k][:, 0:P]
                    nc.vector.tensor_scalar(same[:, k, :], row, edge[:, 1 - k:2 - k], edge[:, 2 + k:3 + k], ALU.is_equal, ALU.mult)
                    nc.vector.scalar_tensor_tensor(out=junk[:], in0=row, scalar=edge[:, 1 - k:2 - k], in1=c["below"][:],
                                                   op0=ALU.is_equal, op1=ALU.mult, accum_out=seen[:, k:k + 1]).then_inc(same_s, 1)
                    dve.wait_ge(same_s, 2 * t + 1 + k)
                nc.vector.scalar_tensor_tensor(out=moved[:], in0=seen[:], scalar=1.0, in1=c["spare"][:, 0:2],
                                               op0=ALU.min, op1=ALU.mult).then_inc(moved_s, 1)
                dve.wait_ge(moved_s, t + 1)
                for k in range(2):
                    nc.vector.tensor_tensor(sidx[:, k:k + 1], moved[:, k:k + 1], edge[:, 1 - k:2 - k], ALU.max).then_inc(sidx_s, 1)
            def fold(t):
                dve.wait_ge(fT_s, t + 1)
                at = c["accT"][:, :, bass.ds(t * P, P)]
                nc.vector.tensor_tensor(at, bank[4][:, 0:D].rearrange("p (h n) -> p h n", h=H), at, ALU.add).then_inc(fa_s, 1)
            if_far(dve, tile_step, fold)

        @block.gpsimd
        def _(pool):
            def tile_step(t, first):
                pool.wait_ge(gidx_s, t + 1)
                pool.sem_inc(held, 1)
                for k, table in enumerate(("Fin", "Fout")):
                    pool.indirect_dma_start(G[:, k, :], None, dram[table],
                                            bass.IndirectOffsetOnAxis(ap=gidx[:, k:k + 1], axis=0)).then_inc(g_in[k], 16)
                pool.wait_ge(sidx_s, 2 * t + 2)
                pool.wait_ge(o_s, 2 * t + 2)
                pool.sem_inc(held, 1)
                for k, table in enumerate(("TA", "T0")):
                    pool.indirect_dma_start(dram[table], bass.IndirectOffsetOnAxis(ap=sidx[:, k:k + 1], axis=0),
                                            O[:, k, :], None, compute_op=ALU.add).then_inc(t_out[k], 16)
                for k in range(2):
                    pool.wait_ge(t_out[k], 16 * t + 16)
            def clear():
                nc.gpsimd.memset(O[:], 0.0).then_inc(z_s, 1)
                pool.wait_ge(z_s, 1)
                for n in range(0, ROWS, 2 * P):
                    pool.dma_start(dram["TA"][n:n + 2 * P].rearrange("(p r) d -> p (r d)", p=P),
                                   O[:].rearrange("p r d -> p (r d)")).then_inc(z_out, 16)
                pool.wait_ge(z_out, 16 * ROWS // (2 * P))
                pool.sem_inc(z_s, 1)
            if_far(pool, tile_step, lambda t: pool.wait_ge(fa_s, t + 1), clear)

        @block.tensor
        def _(pe):
            def tile_step(t, first):
                pe.wait_ge(e_in, 16 * t + 16)
                for k in range(2):
                    nc.tensor.transpose(bank[k][:, 0:P], edge[:, 1 - k:2 - k].to_broadcast([P, P]), c["ident"][:]).then_inc(bc_s, 1)
                pe.wait_ge(same_s, 2 * t + 2)
                for k in range(2):
                    pe.wait_ge(g_in[k], 16 * t + 16)
                    nc.tensor.matmul(bank[2 + k][:, 0:D], same[:, k, :], G[:, k, :], start=True, stop=True).then_inc(mm_s, 1)
            def fold(t):
                pe.wait_ge(f_in, 16 * t + 16)
                reached(pe, fa_s, t)
                for h in range(H):
                    mm = nc.tensor.transpose(bank[4][:, h * P:(h + 1) * P], G[:, 0, h * P:(h + 1) * P], c["ident"][:])
                mm.then_inc(fT_s, 1)
            if_far(pe, tile_step, fold)

        @block.scalar
        def _(act):
            def tile_step(t, first):
                for k in range(2):
                    act.wait_ge(mm_s, 2 * t + 1 + k)
                    nc.scalar.copy(O[:, k, :], bank[2 + k][:, 0:D]).then_inc(o_s, 1)
            if_far(act, tile_step, lambda t: act.wait_ge(fa_s, t + 1), lambda: act.wait_ge(z_s, 2))


def start_of(g):
    return min(GN * g, N - GN) if isinstance(g, int) else GN * g


def group_turns(eng, turn):
    for g in range(3):
        turn(g, g % 2)
    with eng.Fori(0, (GROUPS - 6) // 2) as i:
        turn(2 * i + 3, 1)
        turn(2 * i + 4, 0)
    for g in range(GROUPS - 3, GROUPS + 1):
        turn(g, g % 2)


def has(g, n):
    return not isinstance(g, int) or 0 <= g + n < GROUPS


def gate_nodes(nc, c, bank, a, dram):
    with ExitStack() as ctx:
        def sb(name, shape, dt=F32):
            return ctx.enter_context(nc.sbuf_tensor(name, shape, dt))

        def sem(name):
            return ctx.enter_context(nc.semaphore(name))

        T3 = [GP, ST, NE]
        T4 = [GP, ST, NE, NE]
        xg = sb("xg", [GP, 2, ST, D])
        tg = sb("tg", [GP, 2, ST, D])
        aT = sb("aT", [P, 2, H, GN])
        hh = sb("hhg", [P, 2 * H, GN])
        gate = sb("gate", [P, H, GN])
        new = sb("new", [P, H, GN])
        diff = sb("diff", [P, GN])
        yT = sb("yT", [P, H, GN])
        rhT = sb("rhT", [P, GN])
        pay = sb("pay", [GP, 2, ST, ROWX])
        stats = sb("lstats", [GP, ST, 6])
        mv = sb("lmv", [GP, ST, 2])
        sd = sb("lsd", [GP, ST])
        rstd = sb("lrstd", [GP, ST])
        lg = sb("lg", T3)
        lg2 = sb("lg2", T3)
        pexp = sb("pexp", T3)
        pr = sb("pr", T3)
        m1 = sb("m1", [GP, ST])
        s1 = sb("s1", [GP, ST])
        r1 = sb("r1", [GP, ST])
        m2 = sb("m2", [GP, ST])
        s2 = sb("s2", [GP, ST])
        r2 = sb("r2", [GP, ST])
        pd = sb("pd", T3)
        pex = sb("pex", T3)
        gt = sb("gt", T4)
        eq = sb("eq", T4)
        rank = sb("rank", T3)
        sel = sb("sel", T3, BF16)
        one = sb("one", [GP, 2, ST, NE])
        wt = sb("wt", T3)
        tmp2 = sb("tmp2", [GP, 2, ST, NE])
        slot = sb("slot", T3)
        slotf = sb("slotf", [GP, 2, ST])
        sloti = sb("sloti", [GP, 2, ST], I32)
        tri = sb("tri", [GP, GP], BF16)
        ones = sb("ones", [GP, P], BF16)
        node = sb("node", [GP, ST])
        fresh = sb("fresh", [GP, ST])

        S = STEPS
        spot = aT[0:1].rearrange("p q h n -> p (q h n)")
        over = spot[:, 0:S * NE].rearrange("p (s e) -> p s e", e=NE)
        jump = spot[:, S * NE:2 * S * NE].rearrange("p (s e) -> p s e", e=NE)
        stepf, ex, jm, row = (spot[:, (2 * NE + n) * S:(2 * NE + n + 1) * S] for n in range(4))
        tl = sb("tl", [1, NE])
        tli = sb("tli", [1, NE], I32)
        cnti = sb("cnti", [1, NE], I32)
        endm = sb("endm", [1, NE, NE])
        first = sb("first", [1, NE])
        end = sb("end", [1, NE])
        padt = sb("padt", [P, ROWX])

        held = sem("held4")
        p_s = sem("ep_s")
        ev = sem("ev")
        cnt_s = sem("cnt_s")
        step_s = sem("step_s")
        pad_out = sem("pad_out")
        k_s = sem("k_s")
        k2_s = sem("k2_s")
        x_in = [sem(f"gx_in{q}") for q in range(2)]
        t_in = sem("gt_in")
        ts_s = sem("ts_s")
        tT_s = sem("tT_s")
        ao_s = sem("ao_s")
        hh_in = [sem(f"hh_in{m}") for m in range(2 * H)]
        z_s = sem("z_s")
        g_s = sem("g_s")
        act_s = sem("act_s")
        v = sem("v")
        gnn_s = sem("gnn_s")
        gT_s = sem("gT_s")
        x1_s = sem("x1_s")
        x1_out = [sem(f"x1_out{q}") for q in range(2)]
        mv_s = sem("lmv_s")
        sd_s = sem("lsd_s")
        y_s = sem("y_s")
        yT_s = sem("yT_s")
        yTc_s = sem("yTc_s")
        r_s = sem("r_s")
        rh_s = sem("rh_s")
        lg_s = sem("lg_s")
        l2_s = sem("l2_s")
        e1_s = sem("e1_s")
        pd_s = sem("pd_s")
        e2_s = sem("e2_s")
        sel_s = sem("sel_s")
        cum_s = sem("cum_s")
        cr_s = sem("cr_s")
        pay_s = sem("pay_s")
        y_out = [sem(f"y_out{q}") for q in range(2)]
        block = ctx.enter_context(nc.Block())

        def rows_of(t, s):
            return t[bass.ds(s, GN), :].rearrange("(j p) d -> p j d", p=GP)

        def three(col):
            return col.unsqueeze(2).to_broadcast(T3)

        @block.sync
        def _(sp):
            def load_tables(g):
                reached(sp, tT_s, H * g)
                for n in range(2):
                    sp.dma_start(tg[:, n], rows_of(dram[f"T{n}"], start_of(g))).then_inc(t_in, 16)

            def load_hh(g, m):
                reached(sp, z_s, 2 * H * (g - 1) + m + 1)
                sp.sem_inc(held, 1)
                sp.dma_start(hh[:, m, :], dram["hh"][m][:, bass.ds(start_of(g), GN)]).then_inc(hh_in[m], 16)

            def load_x(g, q):
                if not isinstance(g, int):
                    sp.wait_ge(x1_out[q], 8 * (g - q))
                    sp.sem_inc(held, 1)
                elif g >= 2:
                    sp.wait_ge(x1_out[q], 16 * (g // 2))
                reached(sp, y_s, ST * (g - 1))
                sp.dma_start(xg[:, q], rows_of(a["x"], start_of(g))).then_inc(x_in[q], 16)

            def stores(g, q):
                sp.wait_ge(x1_s, 2 * (g + 1))
                if isinstance(g, int) and g == GROUPS - 1:
                    sp.wait_ge(x1_out[1 - q], 16 * (GROUPS // 2))
                sp.dma_start(rows_of(dram["x1"], start_of(g)), xg[:, q]).then_inc(x1_out[q], 16)

            def turn(g, q):
                if has(g, 1):
                    load_tables(g + 1)
                    load_hh(g + 1, 0)
                if has(g, -1):
                    stores(g - 1, 1 - q)
                if has(g, 1):
                    load_x(g + 1, 1 - q)
                    for m in range(1, 2 * H):
                        load_hh(g + 1, m)
            load_tables(0)
            for m in range(2 * H):
                load_hh(0, m)
            load_x(0, 0)
            sp.wait_ge(p_s, 2)
            for n in (SPARE, ROWS):
                sp.dma_start(dram["x1"][n:n + P, :], padt[:, 0:D]).then_inc(pad_out, 16)
            sp.dma_start(dram["Y"][NE * REG:NE * REG + P, :], padt[:]).then_inc(pad_out, 16)
            group_turns(sp, turn)
            sp.wait_ge(cnt_s, 1)
            for e in range(NE):
                used = sp.value_load(cnti[0:1, e:e + 1], min_val=0, max_val=GROUPS * GN)
                sp.dma_start(dram["Y"][bass.ds(used + e * REG, P), :], padt[:]).then_inc(pad_out, 16)
            sp.wait_ge(pad_out, 16 * (NE + 3))
            for q in range(2):
                sp.wait_ge(x1_out[q], 16 * (GROUPS // 2))

        @block.gpsimd
        def _(pool):
            nc.gpsimd.memset(tri[:], 1.0).then_inc(k_s, 1)
            nc.gpsimd.memset(ones[:], 1.0).then_inc(k_s, 1)
            nc.gpsimd.memset(fresh[:], 1.0).then_inc(k_s, 1)
            nc.gpsimd.memset(c["count"][:], 0.0).then_inc(k_s, 1)
            nc.gpsimd.iota(node[:], pattern=[[GP, ST]], base=-GN, channel_multiplier=1, allow_small_or_imprecise_dtypes=True).then_inc(k_s, 1)
            nc.gpsimd.iota(c["region"][:], pattern=[[0, ST], [REG, NE]], base=0, channel_multiplier=0, allow_small_or_imprecise_dtypes=True).then_inc(k_s, 1)
            nc.gpsimd.memset(padt[:], 0.0).then_inc(p_s, 1)
            pool.wait_ge(p_s, 1)
            nc.gpsimd.iota(padt[:, D + NE:ROWX], pattern=[[0, 1]], base=SPARE, channel_multiplier=1, allow_small_or_imprecise_dtypes=True).then_inc(p_s, 1)
            pool.wait_ge(k_s, 6)
            nc.gpsimd.affine_select(out=tri[:], in_=tri[:], compare_op=ALU.is_gt, fill=0.0, base=0,
                                    pattern=[[1, GP]], channel_multiplier=-1).then_inc(k2_s, 1)
            nc.gpsimd.affine_select(out=fresh[:], in_=fresh[:], compare_op=ALU.is_ge, fill=0.0, base=-(GROUPS * GN - N),
                                    pattern=[[GP, ST]], channel_multiplier=1).then_inc(k2_s, 1)

            def add_tables(g):
                pool.wait_ge(t_in, 32 * (g + 1))
                nc.gpsimd.tensor_tensor(tg[:, 0], tg[:, 0], tg[:, 1], ALU.add).then_inc(ts_s, 1)

            def scatters(g, q):
                pool.wait_ge(pay_s, g + 1)
                pool.sem_inc(held, 1)
                for k in range(2):
                    for j in range(ST):
                        pool.indirect_dma_start(dram["Y"], bass.IndirectOffsetOnAxis(ap=sloti[:, k, j:j + 1], axis=0),
                                                pay[:, q, j, :], None).then_inc(y_out[q], 16)

            def turn(g, q):
                if has(g, 1):
                    add_tables(g + 1)
                if isinstance(g, int) and g == GROUPS:
                    pool.wait_ge(g_s, 2 * H * GROUPS)
                    nc.gpsimd.iota(stepf, pattern=[[1, S]], base=0, channel_multiplier=0, allow_small_or_imprecise_dtypes=True).then_inc(step_s, 1)
                if has(g, -1):
                    scatters(g - 1, 1 - q)
            add_tables(0)
            group_turns(pool, turn)
            for q in range(2):
                pool.wait_ge(y_out[q], 16 * ST * GROUPS)

        @block.scalar
        def _(act):
            def head(g, q):
                for h in range(H):
                    act.wait_ge(tT_s, H * g + 1 + h)
                    nc.scalar.copy(aT[:, q, h, :], bank[2 + h][:, 0:GN]).then_inc(ao_s, 1)

            def gates(g, m):
                act.wait_ge(z_s, 2 * H * g + m + 1)
                z = (gate if m < H else new)[:, m % H, :]
                nc.scalar.activation(z, z, ACT.Sigmoid if m < H else ACT.Tanh, bias=c["bx"][:, m:m + 1]).then_inc(act_s, 1)

            def turn(g, q):
                now, tail = has(g, 0), has(g, -1)
                if tail:
                    act.wait_ge(mv_s, g)
                    nc.scalar.activation(sd[:], mv[:, :, 1], ACT.Sqrt, bias=c["eps"][0:GP]).then_inc(sd_s, 1)
                if now:
                    gates(g, 0)
                    gates(g, 1)
                if tail:
                    for h in range(H):
                        act.wait_ge(yT_s, H * (g - 1) + h + 1)
                        nc.scalar.copy(yT[:, h, :], bank[h][:, 0:GN]).then_inc(yTc_s, 1)
                if now:
                    gates(g, 2)
                if tail:
                    act.wait_ge(r_s, g)
                    nc.scalar.activation(rhT[:], bank[0][:, 0:GN], ACT.Relu, bias=c["br1"][:]).then_inc(rh_s, 1)
                if tail:
                    act.wait_ge(l2_s, g)
                    nc.scalar.activation(pexp[:], lg2[:], ACT.Exp).then_inc(e1_s, 1)
                    act.wait_ge(pd_s, g)
                    nc.scalar.activation(pex[:], pd[:], ACT.Exp).then_inc(e2_s, 1)
                if has(g, 1):
                    head(g + 1, 1 - q)
                if now:
                    gates(g, 3)
            head(0, 0)
            group_turns(act, turn)

        @block.tensor
        def _(pe):
            def tables(g):
                pe.wait_ge(ts_s, g + 1)
                for h in range(H):
                    for j in range(ST):
                        mm = nc.tensor.transpose(bank[2 + h][:, j * GP:(j + 1) * GP], tg[:, 0, j, h * P:(h + 1) * P],
                                                 c["ident"][0:GP, 0:GP])
                    mm.then_inc(tT_s, 1)

            def gates(g, q, m, parts=(0, 1)):
                o = bank[4 + m][:, 0:GN]
                if m == 0:
                    pe.wait_ge(ao_s, H * (g + 1))
                if parts[0] == 0:
                    reached(pe, z_s, 2 * H * (g - 1) + m + 1)
                for part in parts:
                    for k in range(H):
                        x = (c["accT"][:, k, bass.ds(start_of(g), GN)], aT[:, q, k, :])[part]
                        mm = nc.tensor.matmul(o, c["wx"][:, H * part + k, m * P:(m + 1) * P], x,
                                              start=(part == 0 and k == 0), stop=(part == 1 and k == H - 1))
                if parts[-1] == 1:
                    mm.then_inc(g_s, 1)

            def turn(g, q):
                now, tail = has(g, 0), has(g, -1)
                if now:
                    gates(g, q, 0)
                if tail:
                    pe.wait_ge(gnn_s, 3 * H * g)
                    reached(pe, yTc_s, H * (g - 1))
                    reached(pe, cr_s, g - 1)
                    for j in range(ST):
                        for h in range(H):
                            mm = nc.tensor.transpose(bank[j // 2][0:GP, (j % 2) * D + h * P:(j % 2) * D + (h + 1) * P],
                                                     new[:, h, j * GP:(j + 1) * GP], c["ident"][:])
                        mm.then_inc(gT_s, 1)
                if now:
                    gates(g, q, 1)
                    gates(g, q, 2, (0,))
                if tail:
                    pe.wait_ge(x1_s, 2 * g)
                    pe.wait_ge(y_s, ST * g)
                    for h in range(H):
                        for j in range(ST):
                            mm = nc.tensor.transpose(bank[h][:, j * GP:(j + 1) * GP], pay[:, 1 - q, j, h * P:(h + 1) * P], c["ident"][0:GP, 0:GP])
                        mm.then_inc(yT_s, 1)
                if now:
                    gates(g, q, 2, (1,))
                if tail:
                    pe.wait_ge(yTc_s, H * g)
                    for k in range(H):
                        mm = nc.tensor.matmul(bank[0][:, 0:GN], c["wr1"][:, k, :], yT[:, k, :], start=(k == 0), stop=(k == H - 1))
                    mm.then_inc(r_s, 1)
                if tail:
                    pe.wait_ge(rh_s, g)
                    for j in range(ST):
                        mm = nc.tensor.matmul(bank[1][0:GP, j * NE:(j + 1) * NE], rhT[:, j * GP:(j + 1) * GP], c["wr2"][:], start=True, stop=True)
                    mm.then_inc(lg_s, 1)
                if has(g, 1):
                    reached(pe, ao_s, H * g + H)
                    tables(g + 1)
                if now:
                    gates(g, q, 3)
                if tail:
                    pe.wait_ge(sel_s, g)
                    for j in range(ST):
                        for i in range(j + 1):
                            nc.tensor.matmul(bank[0][0:GP, j * NE:(j + 1) * NE], (tri if i == j else ones)[:, 0:GP], sel[:, i, :],
                                             start=(i == 0), stop=(i == j))
                    for i in range(ST):
                        mm = nc.tensor.matmul(bank[0][0:GP, ST * NE:(ST + 1) * NE], ones[:, 0:GP], sel[:, i, :], start=(i == 0), stop=(i == ST - 1))
                    mm.then_inc(cum_s, 1)
            pe.wait_ge(k2_s, 2)
            tables(0)
            group_turns(pe, turn)

        @block.vector
        def _(dve):
            OWN = 21
            region = c["region"][0:GP].rearrange("p (j e) -> p j e", e=NE)

            def rows_out(g, q):
                if not isinstance(g, int):
                    dve.wait_ge(y_out[q], 8 * ST * 2 * (g - q))
                elif g >= 2:
                    dve.wait_ge(y_out[q], 16 * 2 * ST * (g // 2))

            def add_hh(g, m):
                dve.wait_ge(hh_in[m], 16 * (g + 1))
                dve.wait_ge(g_s, 2 * H * g + m + 1)
                nc.vector.tensor_tensor((gate if m < H else new)[:, m % H, :], bank[4 + m][:, 0:GN], hh[:, m, :], ALU.add).then_inc(z_s, 1)

            def new_state(g, q, h):
                done = 3 * (H * g + h)
                dve.wait_ge(act_s, 2 * H * g + H + h + 1)
                reached(dve, gnn_s, done)
                xl = c["xlT"][:, h, bass.ds(start_of(g), GN)]
                nc.vector.scalar_tensor_tensor(out=diff[:], in0=xl, scalar=c["scale"][:, h:h + 1], in1=new[:, h],
                                               op0=ALU.mult, op1=ALU.subtract).then_inc(gnn_s, 1)
                dve.wait_ge(gnn_s, done + 1)
                nc.vector.scalar_tensor_tensor(out=diff[:], in0=diff[:], scalar=c["shift"][:, h:h + 1], in1=gate[:, h],
                                               op0=ALU.add, op1=ALU.mult).then_inc(gnn_s, 1)
                dve.wait_ge(gnn_s, done + 2)
                nc.vector.tensor_tensor(new[:, h], new[:, h], diff[:], ALU.add).then_inc(gnn_s, 1)

            def tail(g, q):
                count = [0]

                def link(ins):
                    count[0] += 1
                    ins.then_inc(v, 1)
                    dve.wait_ge(v, OWN * g + count[0])

                last = isinstance(g, int) and g == GROUPS - 1
                if isinstance(g, int):
                    dve.wait_ge(x_in[q], 16 * (g // 2 + 1))
                else:
                    dve.wait_ge(x_in[q], 8 * (g - q) + 16)
                for j in range(0, ST, 2):
                    dve.wait_ge(gT_s, ST * g + j + 2)
                    x2 = xg[:, q, j:j + 2, :]
                    nc.vector.tensor_tensor(x2, x2, bank[j // 2][0:GP, :].rearrange("p (j d) -> p j d", j=2), ALU.add).then_inc(x1_s, 1)
                dve.wait_ge(x1_s, 2 * (g + 1))
                for j in range(ST):
                    mm = nc.vector.bn_stats(stats[:, j, :], xg[:, q, j, :])
                mm.then_inc(v, 1)
                count[0] += 1
                dve.wait_ge(v, OWN * g + count[0])
                dve.sem_inc(held, 1)
                for j in range(ST):
                    mm = nc.vector.bn_aggr(mv[:, j, :], stats[:, j, :])
                mm.then_inc(mv_s, 1)
                if not last:
                    for m in range(2):
                        add_hh(g + 1, m)
                dve.wait_ge(sd_s, g + 1)
                link(nc.vector.reciprocal(rstd[:], sd[:]))
                rows_out(g, q)
                for j in range(ST):
                    nc.vector.tensor_scalar(pay[:, q, j, 0:D], xg[:, q, j, :], mv[:, j, 0:1], rstd[:, j:j + 1], ALU.subtract, ALU.mult).then_inc(y_s, 1)
                if not last:
                    add_hh(g + 1, 2)
                    new_state(g + 1, 1 - q, 0)
                dve.wait_ge(lg_s, g + 1)
                link(nc.vector.tensor_tensor(lg[:], bank[1][0:GP, 0:ST * NE].rearrange("p (j e) -> p j e", e=NE),
                                             c["br2"][0:GP, :].unsqueeze(1).to_broadcast(T3), ALU.add))
                link(nc.vector.tensor_reduce(m1[:], lg[:], AX.X, ALU.max))
                nc.vector.tensor_tensor(lg2[:], lg[:], three(m1[:]), ALU.subtract).then_inc(l2_s, 1)
                dve.wait_ge(e1_s, g + 1)
                link(nc.vector.tensor_reduce(s1[:], pexp[:], AX.X, ALU.add))
                link(nc.vector.reciprocal(r1[:], s1[:]))
                link(nc.vector.tensor_tensor(pr[:], pexp[:], three(r1[:]), ALU.mult))
                link(nc.vector.tensor_reduce(m2[:], pr[:], AX.X, ALU.max))
                nc.vector.tensor_tensor(pd[:], pr[:], three(m2[:]), ALU.subtract).then_inc(pd_s, 1)
                other = pr[:].unsqueeze(2).to_broadcast(T4)
                own = pr[:].unsqueeze(3).to_broadcast(T4)
                nc.vector.tensor_tensor(gt[:], other, own, ALU.is_gt)
                link(nc.vector.tensor_tensor(eq[:], other, own, ALU.is_equal))
                link(nc.vector.tensor_tensor(eq[:], eq[:], c["prior"][0:GP].unsqueeze(1).to_broadcast(T4), ALU.mult))
                link(nc.vector.tensor_tensor(gt[:], gt[:], eq[:], ALU.add))
                link(nc.vector.tensor_reduce(rank[:], gt[:], AX.X, ALU.add))
                nc.vector.tensor_scalar(sel[:], rank[:], 2.0, None, ALU.is_lt).then_inc(sel_s, 1)
                if not last:
                    add_hh(g + 1, 3)
                for k in range(2):
                    mm = nc.vector.tensor_scalar(one[:, k], rank[:], float(k), None, ALU.is_equal)
                link(mm)
                dve.wait_ge(e2_s, g + 1)
                link(nc.vector.scalar_tensor_tensor(out=wt[:], in0=rank[:], scalar=2.0, in1=pex[:], op0=ALU.is_lt, op1=ALU.mult))
                link(nc.vector.tensor_reduce(s2[:], wt[:], AX.X, ALU.add))
                link(nc.vector.reciprocal(r2[:], s2[:]))
                if last:
                    link(nc.vector.tensor_tensor(r2[:], r2[:], fresh[:], ALU.mult))
                dve.wait_ge(cum_s, g + 1)
                link(nc.vector.tensor_tensor(slot[:], bank[0][0:GP, 0:ST * NE].rearrange("p (j e) -> p j e", e=NE), region, ALU.add))
                link(nc.vector.tensor_tensor(slot[:], slot[:], c["count"][0:GP, :].unsqueeze(1).to_broadcast(T3), ALU.add))
                nc.vector.tensor_tensor(c["count"][0:GP, :], c["count"][0:GP, :], bank[0][0:GP, ST * NE:(ST + 1) * NE], ALU.add).then_inc(cr_s, 1)
                if not last:
                    new_state(g + 1, 1 - q, 1)
                link(nc.vector.tensor_tensor(tmp2[:], one[:], slot[:].unsqueeze(1).to_broadcast([GP, 2, ST, NE]), ALU.mult))
                link(nc.vector.tensor_reduce(slotf[:], tmp2[:], AX.X, ALU.add))
                if not (isinstance(g, int) and g == 0):
                    rows_out(g + 1, 1 - q)
                nc.vector.tensor_copy(sloti[:], slotf[:])
                step = float(N - GN - GN * (GROUPS - 2)) if last else float(GN)
                if last:
                    aside = float(ROWS - (N - GN))
                    link(nc.vector.tensor_scalar(node[:], node[:], step + aside, None, ALU.add))
                    link(nc.vector.scalar_tensor_tensor(out=node[:], in0=fresh[:], scalar=-aside, in1=node[:], op0=ALU.mult, op1=ALU.add))
                else:
                    link(nc.vector.tensor_scalar(node[:], node[:], step, None, ALU.add))
                nc.vector.tensor_copy(pay[:, q, :, D + NE], node[:])
                nc.vector.tensor_tensor(pay[:, q, :, D:D + NE], wt[:], three(r2[:]), ALU.mult).then_inc(pay_s, 1)
                assert last or count[0] == OWN, count

            dve.wait_ge(k2_s, 2)
            for m in range(2 * H):
                add_hh(0, m)
            for h in range(H):
                new_state(0, 0, h)

            def turn(g, q):
                if has(g, -1):
                    tail(g - 1, 1 - q)
            group_turns(dve, turn)

            done = [0]

            def step(ins):
                done[0] += 1
                ins.then_inc(ev, 1)
                dve.wait_ge(ev, done[0])

            dve.wait_ge(step_s, 1)
            c1 = c["count"][0:1, :]
            step(nc.vector.tensor_scalar(tl[:], c1, 1.0 / P, 127.0 / P - 0.5 + 0.5 / P, ALU.mult, ALU.add))
            step(nc.vector.tensor_copy(tli[:], tl[:]))
            step(nc.vector.tensor_copy(tl[:], tli[:]))
            nc.vector.tensor_copy(cnti[:], c1).then_inc(cnt_s, 1)
            step(nc.vector.tensor_tensor(endm[:], c["prior"][0:1], tl[:].unsqueeze(1).to_broadcast([1, NE, NE]), ALU.mult))
            step(nc.vector.tensor_reduce(first[:], endm[:], AX.X, ALU.add))
            step(nc.vector.tensor_tensor(end[:], first[:], tl[:], ALU.add))
            steps = stepf.unsqueeze(2).to_broadcast([1, S, NE])
            step(nc.vector.tensor_tensor(over, steps, end[:].unsqueeze(1).to_broadcast([1, S, NE]), ALU.is_ge))
            step(nc.vector.tensor_reduce(ex, over, AX.X, ALU.add))
            step(nc.vector.tensor_tensor(jump, over, tl[:].unsqueeze(1).to_broadcast([1, S, NE]), ALU.mult))
            step(nc.vector.tensor_reduce(jm, jump, AX.X, ALU.add))
            step(nc.vector.tensor_tensor(row, stepf, jm, ALU.subtract))
            step(nc.vector.tensor_scalar(row, row, float(P), None, ALU.mult))
            step(nc.vector.scalar_tensor_tensor(out=row, in0=ex, scalar=float(REG), in1=row, op0=ALU.mult, op1=ALU.add))
            step(nc.vector.tensor_scalar(c["rowi"][:], row, float(NE * REG), None, ALU.min))
            step(nc.vector.tensor_scalar(c["exi"][:], ex, float(NE - 1), None, ALU.min))


def run_experts(nc, c, bank, a, dram, out):
    with ExitStack() as ctx:
        def sb(name, shape, dt=F32):
            return ctx.enter_context(nc.sbuf_tensor(name, shape, dt))

        def sem(name):
            return ctx.enter_context(nc.semaphore(name))

        S = STEPS
        exi = c["exi"]
        b3 = sb("b3", [P, NE, D])
        yt = sb("yt", [P, 4, ROWX])
        mark = sb("mark", [P, 4, NE + 1])
        yT = sb("yTe", [P, 2, H, P])
        z1 = sb("z1", [P, D])
        h1 = sb("h1", [P, H, P])
        z2 = sb("z2", [P, D])
        h2 = sb("h2", [P, H, P])
        z3 = sb("z3", [P, D])
        O = sb("Oe", [P, 4, D])
        oid = sb("oid", [P, 4], I32)

        b_in = sem("b_in")
        y_in = [sem(f"ey_in{n}") for n in range(4)]
        A_s = sem("A_s")
        Ac_s = sem("Ac_s")
        B_s = sem("B_s")
        Bc_s = sem("Bc_s")
        C_s = sem("C_s")
        Cc_s = sem("Cc_s")
        D_s = sem("D_s")
        Dc_s = sem("Dc_s")
        E_s = sem("E_s")
        Ec_s = sem("Ec_s")
        F_s = sem("F_s")
        Fz_s = sem("Fz_s")
        Fc_s = sem("Fc_s")
        held = sem("held5")
        o_out = sem("eo_out")
        out_s = sem("out_s")
        block = ctx.enter_context(nc.Block())

        def step_turns(eng, turn):
            head, loops = 6, (S - 3 - 6) // 4
            for s in range(head):
                turn(s, s % 4, lambda k: expert(eng, s - k))
            with eng.Fori(0, loops) as i:
                of = several(eng, 4 * i + head - 2)
                for n in range(4):
                    turn(4 * i + head + n, (head + n) % 4, lambda k: of[n + 2 - k])
            for s in range(head + 4 * loops, S + 2):
                turn(s, s % 4, lambda k: expert(eng, s - k))

        def several(eng, s):
            if eng.engine in (mybir.EngineType.Pool, mybir.EngineType.SP):
                return None
            return nc.values_load_multi_w_load_instructions(exi[0:1, bass.ds(s, 6)], engines=(eng.engine,),
                                                            min_val=0, max_val=NE - 1)[1]

        def live(s):
            return not isinstance(s, int) or 0 <= s < S

        def expert(eng, s):
            return eng.value_load(exi[0:1, bass.ds(s, 1)], min_val=0, max_val=NE - 1)

        @block.gpsimd
        def _(pool):
            def turn(s, n, experts):
                if live(s - 2):
                    pool.wait_ge(Fc_s, s - 1)
                    reached(pool, o_out, 16 * (s - 2))
                    pool.sem_inc(held, 1)
                    m = (n + 2) % 4
                    pool.indirect_dma_start(dram["x1"], bass.IndirectOffsetOnAxis(ap=oid[:, m:m + 1], axis=0),
                                            O[:, m, :], None, compute_op=ALU.add).then_inc(o_out, 16)
            step_turns(pool, turn)

        @block.sync
        def _(sp):
            sp.dma_start(b3[:].rearrange("p e d -> p (e d)"), a["L0_ffn_expert_b3"].rearrange("(a e) d -> a (e d)", a=1).partition_broadcast(P)).then_inc(b_in, 16)

            def load(s, m):
                reached(sp, Ac_s, s - 3)
                r = sp.value_load(c["rowi"][0:1, bass.ds(s, 1)], min_val=0, max_val=NE * REG)
                sp.dma_start(yt[:, m, :], dram["Y"][bass.ds(r, P), :]).then_inc(y_in[m], 16)
            for s in range(3):
                load(s, s)

            def turn(s, n, experts):
                if live(s + 3):
                    load(s + 3, (n + 3) % 4)
            step_turns(sp, turn)
            sp.wait_ge(o_out, 16 * S)
            sp.dma_start(out.rearrange("n d -> (n d)").rearrange("(p f) -> p f", p=P),
                         dram["x1"][0:N, :].rearrange("n d -> (n d)").rearrange("(p f) -> p f", p=P)).then_inc(out_s, 16)
            sp.wait_ge(out_s, 16)

        @block.tensor
        def _(pe):
            def transposes(b, src, s, sem_out):
                for h in range(H):
                    mm = nc.tensor.transpose(bank[b][:, h * P:(h + 1) * P], src[:, h * P:(h + 1) * P], c["ident"][:])
                mm.then_inc(sem_out, 1)

            def layer(b, n, src, e, sem_out):
                for k in range(H):
                    w = c["we"][:, n].rearrange("p e h d -> p e (h d)")[:, bass.ds(e, 1), k * D:(k + 1) * D].rearrange("p a d -> p (a d)")
                    mm = nc.tensor.matmul(bank[b][:, 0:D], src[:, k, :], w, start=(k == 0), stop=(k == H - 1))
                mm.then_inc(sem_out, 1)

            def stage_a(s, m):
                if isinstance(s, int):
                    pe.wait_ge(y_in[m], 16 * (s // 4 + 1))
                else:
                    pe.wait_ge(y_in[m], 4 * (s - m) + 16)
                reached(pe, Ac_s, s)
                transposes(0, yt[:, m, :], s, A_s)

            def turn(s, n, experts):
                if live(s - 1):
                    pe.wait_ge(Bc_s, s)
                    reached(pe, Cc_s, s - 1)
                    transposes(2, z1[:], s - 1, C_s)
                if live(s - 2):
                    pe.wait_ge(Dc_s, s - 1)
                    reached(pe, Ec_s, s - 2)
                    transposes(4, z2[:], s - 2, E_s)
                if live(s + 1):
                    stage_a(s + 1, (n + 1) % 4)
                if live(s):
                    e = experts(0)
                    pe.wait_ge(Ac_s, s + 1)
                    reached(pe, Bc_s, s)
                    layer(1, 0, yT[:, n % 2], e, B_s)
                if live(s - 1):
                    e = experts(1)
                    pe.wait_ge(Cc_s, s)
                    reached(pe, Dc_s, s - 1)
                    layer(3, 1, h1, e, D_s)
                if live(s - 2):
                    e = experts(2)
                    pe.wait_ge(Ec_s, s - 1)
                    reached(pe, Fz_s, s - 2)
                    layer(5, 2, h2, e, F_s)
            stage_a(0, 0)
            step_turns(pe, turn)

        @block.scalar
        def _(act):
            def relu(b, to, bias, e):
                for h in range(H):
                    mm = nc.scalar.activation(to[:, h, :], bank[b][:, h * P:(h + 1) * P], ACT.Relu,
                                              bias=c[bias][:, bass.ds(e, 1), h:h + 1].rearrange("p a b -> p (a b)"))
                return mm

            def stage_a(s, m):
                act.wait_ge(A_s, s + 1)
                reached(act, B_s, s - 1)
                reached(act, Fc_s, s - 3)
                nc.scalar.copy(mark[:, m, :], yt[:, m, D:ROWX])
                nc.scalar.copy(yT[:, m % 2], bank[0][:, 0:D].rearrange("p (h n) -> p h n", h=H)).then_inc(Ac_s, 1)

            def turn(s, n, experts):
                if live(s - 1):
                    e = experts(1)
                    act.wait_ge(C_s, s)
                    reached(act, D_s, s - 1)
                    relu(2, h1, "be1", e).then_inc(Cc_s, 1)
                if live(s - 2):
                    e = experts(2)
                    act.wait_ge(E_s, s - 1)
                    reached(act, F_s, s - 2)
                    relu(4, h2, "be2", e).then_inc(Ec_s, 1)
                if live(s + 1):
                    stage_a(s + 1, (n + 1) % 4)
            stage_a(0, 0)
            step_turns(act, turn)

        @block.vector
        def _(dve):
            dve.wait_ge(b_in, 16)

            def turn(s, n, experts):
                if live(s):
                    dve.wait_ge(B_s, s + 1)
                    reached(dve, C_s, s)
                    nc.vector.tensor_copy(z1[:], bank[1][:, 0:D]).then_inc(Bc_s, 1)
                if live(s - 1):
                    dve.wait_ge(D_s, s)
                    reached(dve, E_s, s - 1)
                    nc.vector.tensor_copy(z2[:], bank[3][:, 0:D]).then_inc(Dc_s, 1)
                if live(s - 2):
                    e = experts(2)
                    dve.wait_ge(F_s, s - 1)
                    reached(dve, Fc_s, s - 2)
                    nc.vector.tensor_tensor(z3[:], bank[5][:, 0:D], b3[:, bass.ds(e, 1), :].rearrange("p a d -> p (a d)"), ALU.add).then_inc(Fz_s, 1)
                    m = (n + 2) % 4
                    dve.wait_ge(Fz_s, s - 1)
                    reached(dve, o_out, 16 * (s - 5))
                    nc.vector.tensor_scalar(O[:, m, :], z3[:], mark[:, m, bass.ds(e, 1)], None, ALU.mult)
                    nc.vector.tensor_copy(oid[:, m:m + 1], mark[:, m, NE:NE + 1]).then_inc(Fc_s, 1)
            step_turns(dve, turn)


def graph_layer(nc, a, out):
    dram = {n: nc.dram_tensor(n, [ROWS, D], F32).ap() for n in ("Fin", "Fout", "T0", "T1", "TA")}
    dram["x1"] = nc.dram_tensor("x1", [ROWS + P, D], F32).ap()
    dram["hh"] = nc.dram_tensor("HH", [2 * H, P, NP], F32).ap()
    dram["Y"] = nc.dram_tensor("Y", [NE * REG + P, ROWX], F32).ap()
    dram["slow"] = nc.dram_tensor("slow", [4, EC * P * P], F32).ap()
    with ExitStack() as ctx:
        ctx.enter_context(nc.allow_non_contiguous_dma(reason="bias columns, and single edges on the rare path"))
        bank = [ctx.enter_context(nc.psum_tensor(f"bank{n}", [P, 512], F32)) for n in range(8)]
        c = persistent(nc, ctx)
        with ExitStack() as edges:
            c.update(for_edges(nc, edges))
            z_out = ctx.enter_context(nc.semaphore("z_out"))
            with nc.cleanup_on_exit():
                normalise_nodes(nc, c, bank, a, dram, z_out)
            transform_nodes(nc, c, bank, a, dram, z_out)
            sum_over_edges(nc, c, bank, a, dram)
            sum_far_edges(nc, c, bank, dram)
        gate_nodes(nc, c, bank, a, dram)
        run_experts(nc, c, bank, a, dram, out)


_INS = ['x', 'src', 'dst', 'edge_weight', 'edge_weight_n2', 'L0_gnn_gamma', 'L0_gnn_beta', 'L0_gnn_W_in', 'L0_gnn_b_in',
        'L0_gnn_W_out', 'L0_gnn_b_out', 'L0_gnn_W_x2i', 'L0_gnn_b_x2i', 'L0_gnn_W_h2h', 'L0_ffn_router_w1',
        'L0_ffn_router_b1', 'L0_ffn_router_w2', 'L0_ffn_router_b2', 'L0_ffn_expert_w1', 'L0_ffn_expert_b1',
        'L0_ffn_expert_w2', 'L0_ffn_expert_b2', 'L0_ffn_expert_w3', 'L0_ffn_expert_b3']


def kernel(**inputs):
    import numpy as _np
    import concourse.bacc as _bacc
    from concourse import mybir as _mybir
    from concourse.bass_utils import run_bass_kernel_spmd as _run

    nc = _bacc.Bacc("TRN2", target_bir_lowering=False, num_devices=1)
    arrays, args = {}, {}
    for name in _INS:
        arr = _np.ascontiguousarray(inputs[name])
        arrays[f"in_{name}_dram"] = arr
        args[name] = nc.dram_tensor(f"in_{name}_dram", arr.shape, _mybir.dt.from_np(arr.dtype), kind="ExternalInput").ap()
    out = nc.dram_tensor("out_0_dram", (N, D), F32, kind="ExternalOutput").ap()
    graph_layer(nc, args, out)
    r = _run(nc, [arrays], core_ids=[0])
    return r.results[0]["out_0_dram"]
```
